# Optimizing a Trainium2 kernel written in Bass

```python
import numpy as np
import jax
import jax.numpy as jnp

def _softmax(x, axis=-1):
    return jax.nn.softmax(x, axis=axis)

def _gelu(x):
    return jax.nn.gelu(x, approximate=True)

def _silu(x):
    return jax.nn.silu(x)

def _sigmoid(x):
    return jax.nn.sigmoid(x)

def _layernorm(x, axis=-1, eps=1e-05):
    m = jnp.mean(x, axis=axis, keepdims=True)
    v = jnp.var(x, axis=axis, keepdims=True)
    return (x - m) / jnp.sqrt(v + eps)

def _scatter_add(tgt, idx, src, axis=0):
    return tgt.at[idx].add(src)

def _segment_sum(src, seg, n):
    return jax.ops.segment_sum(src, seg, n)
kernel_name = 'mk_hybrid_d2_jaxref_r8_d50eab'

def setup_inputs(seed: int=0):
    np.random.seed(seed)
    _w = jnp.asarray

    def _L0_attn_a_setup():
        import jax, jax.numpy as jnp
        import numpy as np
        DT_MIN, DT_MAX, STAB_EPS, RMS_EPS = (0.0001, 10.0, 1e-08, 1e-06)

        def soft_clamp(x, mn=DT_MIN, mx=DT_MAX):
            center = (mx + mn) / 2.0
            half = (mx - mn) / 2.0
            return center + half * jnp.tanh((x - center) / half)
        key = jax.random.key(seed)
        ks = jax.random.split(key, 8)
        B, L, D, N = (1, 512, 128, 16)
        s = D ** (-0.5)
        x = jax.random.normal(ks[0], (B, L, D), jnp.float32)
        A_log = jnp.broadcast_to(jnp.log(jnp.arange(1, N + 1, dtype=jnp.float32)), (D, N))
        W_delta = jax.random.normal(ks[1], (D, D), jnp.float32) * s
        b_delta = jax.random.normal(ks[2], (D,), jnp.float32) * 0.1
        W_B = jax.random.normal(ks[3], (D, N), jnp.float32) * s
        W_C = jax.random.normal(ks[4], (D, N), jnp.float32) * s
        D_skip = jax.random.normal(ks[5], (D,), jnp.float32) * 0.1 + 1.0
        norm_weight = jnp.ones((D,), jnp.float32)
        return {'x': x, 'A_log': A_log, 'W_delta': W_delta, 'b_delta': b_delta, 'W_B': W_B, 'W_C': W_C, 'D_skip': D_skip, 'norm_weight': norm_weight}
    _L0_attn_a_in = _L0_attn_a_setup()

    def _L0_attn_b_setup():
        import jax, jax.numpy as jnp
        import numpy as np
        H, HD, D = (16, 64, 128)
        SCALE = HD ** (-0.5)
        TEMP = 1.0
        EPS = 1e-05
        key = jax.random.key(seed)
        ks = jax.random.split(key, 10)
        B, N = (2, 256)
        lim = 1.0 / np.sqrt(D)

        def lin(k, out_d, in_d):
            k1, k2 = jax.random.split(k)
            W = jax.random.uniform(k1, (out_d, in_d), jnp.float32, -lim, lim)
            b = jax.random.uniform(k2, (out_d,), jnp.float32, -lim, lim)
            return (W, b)
        Wq, bq = lin(ks[0], H * HD, D)
        Wk, bk = lin(ks[1], H * HD, D)
        Wv, bv = lin(ks[2], H * HD, D)
        Wo, bo = lin(ks[3], D, H * HD)
        return {'x': jax.random.normal(ks[4], (B, N, D), jnp.float32), 'adaptive_scale': jnp.ones((H,), jnp.float32), 'Wq': Wq, 'bq': bq, 'Wk': Wk, 'bk': bk, 'Wv': Wv, 'bv': bv, 'Wo': Wo, 'bo': bo, 'gamma': jnp.ones((D,), jnp.float32), 'beta': jnp.zeros((D,), jnp.float32)}
    _L0_attn_b_in = _L0_attn_b_setup()

    def _L0_ffn_setup():
        import jax, jax.numpy as jnp
        import numpy as np
        E, K = (8, 2)
        DM, DE = (128, 352)
        B, S = (1, 256)
        EPS = 1e-06

        def _rmsnorm(x, w):
            var = jnp.mean(jnp.square(x), axis=-1, keepdims=True)
            return x * jax.lax.rsqrt(var + EPS) * w
        key = jax.random.key(seed)
        kx, kg, k1, k2, k3 = jax.random.split(key, 5)

        def kaiming_uniform(k, shape, fan_in):
            bound = 1.0 / np.sqrt(fan_in)
            return jax.random.uniform(k, shape, jnp.float32, -bound, bound)
        return {'x': jax.random.normal(kx, (B, S, DM), jnp.float32), 'gate_w': kaiming_uniform(kg, (E, DM), DM), 'rms_w': jnp.ones((DM,), jnp.float32), 'W1': kaiming_uniform(k1, (E, DE, DM), DE * DM), 'W2': kaiming_uniform(k2, (E, DE, DM), DE * DM), 'W3': kaiming_uniform(k3, (E, DM, DE), DM * DE)}
    _L0_ffn_in = _L0_ffn_setup()

    def _L1_attn_a_setup():
        import jax, jax.numpy as jnp
        import numpy as np
        import math
        B, S, D = (2, 512, 128)
        key = jax.random.key(seed)
        ks = jax.random.split(key, 8)
        s = 1.0 / math.sqrt(D)
        return {'x': jax.random.normal(ks[0], (B, S, D), dtype=jnp.float32), 'Wq': jax.random.normal(ks[1], (D, D), dtype=jnp.float32) * s, 'bq': jax.random.normal(ks[2], (D,), dtype=jnp.float32) * s, 'Wk': jax.random.normal(ks[3], (D, D), dtype=jnp.float32) * s, 'bk': jax.random.normal(ks[4], (D,), dtype=jnp.float32) * s, 'Wv': jax.random.normal(ks[5], (D, D), dtype=jnp.float32) * s, 'bv': jax.random.normal(ks[6], (D,), dtype=jnp.float32) * s, 'phase_bias': jnp.zeros((D,), dtype=jnp.float32)}
    _L1_attn_a_in = _L1_attn_a_setup()

    def _L1_attn_b_setup():
        import jax, jax.numpy as jnp
        import numpy as np
        B, S, D_IN, D_OUT, H = (2, 256, 128, 128, 16)
        HD = D_OUT // H
        key = jax.random.key(seed)
        ks = jax.random.split(key, 6)
        x = jax.random.normal(ks[0], (B, S, D_IN), jnp.float32)
        Wq = jax.random.normal(ks[1], (D_IN, D_OUT), jnp.float32) * 0.02
        Wk = jax.random.normal(ks[2], (D_IN, D_OUT), jnp.float32) * 0.02
        Wv = jax.random.normal(ks[3], (D_IN, D_OUT), jnp.float32) * 0.02
        Wo = jax.random.normal(ks[4], (D_OUT, D_OUT), jnp.float32) * 0.02
        bo = jax.random.normal(ks[5], (D_OUT,), jnp.float32) * 0.02
        return {'x': x, 'Wq': Wq, 'Wk': Wk, 'Wv': Wv, 'Wo': Wo, 'bo': bo}
    _L1_attn_b_in = _L1_attn_b_setup()

    def _L1_ffn_setup():
        import jax, jax.numpy as jnp
        import numpy as np
        B, S, H, F, E, K = (4, 256, 128, 512, 8, 2)
        key = jax.random.key(seed)
        ks = jax.random.split(key, 4)
        sc = lambda d: 1.0 / np.sqrt(d)
        return {'x': jax.random.normal(ks[0], (B, S, H), jnp.float32), 'gate_w': jax.random.normal(ks[1], (H, E), jnp.float32) * sc(H), 'gate_b': jnp.zeros((E,), jnp.float32), 'w1': jax.random.normal(ks[2], (E, H, F), jnp.float32) * sc(H), 'b1': jnp.zeros((E, F), jnp.float32), 'w2': jax.random.normal(ks[3], (E, F, H), jnp.float32) * sc(F), 'b2': jnp.zeros((E, H), jnp.float32)}
    _L1_ffn_in = _L1_ffn_setup()
    _d = {'L0_attn_a_x': _L0_attn_a_in['x'], 'L0_attn_a_A_log': _L0_attn_a_in['A_log'], 'L0_attn_a_W_delta': _L0_attn_a_in['W_delta'], 'L0_attn_a_b_delta': _L0_attn_a_in['b_delta'], 'L0_attn_a_W_B': _L0_attn_a_in['W_B'], 'L0_attn_a_W_C': _L0_attn_a_in['W_C'], 'L0_attn_a_D_skip': _L0_attn_a_in['D_skip'], 'L0_attn_a_norm_weight': _L0_attn_a_in['norm_weight'], 'L0_attn_b_adaptive_scale': _L0_attn_b_in['adaptive_scale'], 'L0_attn_b_Wq': _L0_attn_b_in['Wq'], 'L0_attn_b_bq': _L0_attn_b_in['bq'], 'L0_attn_b_Wk': _L0_attn_b_in['Wk'], 'L0_attn_b_bk': _L0_attn_b_in['bk'], 'L0_attn_b_Wv': _L0_attn_b_in['Wv'], 'L0_attn_b_bv': _L0_attn_b_in['bv'], 'L0_attn_b_Wo': _L0_attn_b_in['Wo'], 'L0_attn_b_bo': _L0_attn_b_in['bo'], 'L0_attn_b_gamma': _L0_attn_b_in['gamma'], 'L0_attn_b_beta': _L0_attn_b_in['beta'], 'L0_ffn_gate_w': _L0_ffn_in['gate_w'], 'L0_ffn_rms_w': _L0_ffn_in['rms_w'], 'L0_ffn_W1': _L0_ffn_in['W1'], 'L0_ffn_W2': _L0_ffn_in['W2'], 'L0_ffn_W3': _L0_ffn_in['W3'], 'L1_attn_a_Wq': _L1_attn_a_in['Wq'], 'L1_attn_a_bq': _L1_attn_a_in['bq'], 'L1_attn_a_Wk': _L1_attn_a_in['Wk'], 'L1_attn_a_bk': _L1_attn_a_in['bk'], 'L1_attn_a_Wv': _L1_attn_a_in['Wv'], 'L1_attn_a_bv': _L1_attn_a_in['bv'], 'L1_attn_a_phase_bias': _L1_attn_a_in['phase_bias'], 'L1_attn_b_Wq': _L1_attn_b_in['Wq'], 'L1_attn_b_Wk': _L1_attn_b_in['Wk'], 'L1_attn_b_Wv': _L1_attn_b_in['Wv'], 'L1_attn_b_Wo': _L1_attn_b_in['Wo'], 'L1_attn_b_bo': _L1_attn_b_in['bo'], 'L1_ffn_gate_w': _L1_ffn_in['gate_w'], 'L1_ffn_gate_b': _L1_ffn_in['gate_b'], 'L1_ffn_w1': _L1_ffn_in['w1'], 'L1_ffn_b1': _L1_ffn_in['b1'], 'L1_ffn_w2': _L1_ffn_in['w2'], 'L1_ffn_b2': _L1_ffn_in['b2']}
    _x0 = _d['L0_attn_a_x']
    _d['L0_attn_a_x'] = jax.random.normal(jax.random.fold_in(jax.random.key(seed), 1), (4, 512, 128), dtype=_x0.dtype)
    del _x0
    return _d

def reference(L0_attn_a_x, L0_attn_a_A_log, L0_attn_a_W_delta, L0_attn_a_b_delta, L0_attn_a_W_B, L0_attn_a_W_C, L0_attn_a_D_skip, L0_attn_a_norm_weight, L0_attn_b_adaptive_scale, L0_attn_b_Wq, L0_attn_b_bq, L0_attn_b_Wk, L0_attn_b_bk, L0_attn_b_Wv, L0_attn_b_bv, L0_attn_b_Wo, L0_attn_b_bo, L0_attn_b_gamma, L0_attn_b_beta, L0_ffn_gate_w, L0_ffn_rms_w, L0_ffn_W1, L0_ffn_W2, L0_ffn_W3, L1_attn_a_Wq, L1_attn_a_bq, L1_attn_a_Wk, L1_attn_a_bk, L1_attn_a_Wv, L1_attn_a_bv, L1_attn_a_phase_bias, L1_attn_b_Wq, L1_attn_b_Wk, L1_attn_b_Wv, L1_attn_b_Wo, L1_attn_b_bo, L1_ffn_gate_w, L1_ffn_gate_b, L1_ffn_w1, L1_ffn_b1, L1_ffn_w2, L1_ffn_b2):

    def _L0_attn_a_ref(x, A_log, W_delta, b_delta, W_B, W_C, D_skip, norm_weight):
        import jax, jax.numpy as jnp
        import numpy as np
        DT_MIN, DT_MAX, STAB_EPS, RMS_EPS = (0.0001, 10.0, 1e-08, 1e-06)

        def soft_clamp(x, mn=DT_MIN, mx=DT_MAX):
            center = (mx + mn) / 2.0
            half = (mx - mn) / 2.0
            return center + half * jnp.tanh((x - center) / half)
        rms = jnp.sqrt(jnp.mean(x * x, axis=-1, keepdims=True) + RMS_EPS)
        xn = norm_weight * x / rms
        delta = soft_clamp(jax.nn.softplus(xn @ W_delta + b_delta))
        Bp = xn @ W_B
        C = xn @ W_C
        A = -jnp.exp(A_log)
        half_dA = 0.5 * delta[..., None] * A
        denom_inv = 1.0 / jnp.maximum(1.0 - half_dA, STAB_EPS)
        A_bar = (1.0 + half_dA) * denom_inv
        B_bar = jnp.sqrt(delta)[..., None] * Bp[:, :, None, :] * denom_inv
        Bx = B_bar * xn[..., None]

        def step(h, inp):
            a_t, bx_t, c_t = inp
            h = a_t * h + bx_t
            y_t = jnp.einsum('bdn,bn->bd', h, c_t)
            return (h, y_t)
        h0 = jnp.zeros((x.shape[0], A.shape[0], A.shape[1]), x.dtype)
        seq = (jnp.moveaxis(A_bar, 1, 0), jnp.moveaxis(Bx, 1, 0), jnp.moveaxis(C, 1, 0))
        _, ys = jax.lax.scan(step, h0, seq)
        y = jnp.moveaxis(ys, 0, 1) + D_skip * xn
        return y

    def _L0_attn_b_ref(x, adaptive_scale, Wq, bq, Wk, bk, Wv, bv, Wo, bo, gamma, beta):
        import jax, jax.numpy as jnp
        import numpy as np
        H, HD, D = (16, 64, 128)
        SCALE = HD ** (-0.5)
        TEMP = 1.0
        EPS = 1e-05
        B, N, _ = x.shape
        Q = (x @ Wq.T + bq).reshape(B, N, H, HD)
        K = (x @ Wk.T + bk).reshape(B, N, H, HD)
        V = (x @ Wv.T + bv).reshape(B, N, H, HD)
        scores = jnp.einsum('bnhd,bmhd->bhnm', Q, K)
        scores = scores * (SCALE * adaptive_scale)[None, :, None, None] / TEMP
        w = jax.nn.softmax(scores, axis=-1)
        attn = jnp.einsum('bhnm,bmhd->bnhd', w, V).reshape(B, N, H * HD)
        y = x + (attn @ Wo.T + bo)
        mu = jnp.mean(y, axis=-1, keepdims=True)
        var = jnp.var(y, axis=-1, keepdims=True)
        return (y - mu) / jnp.sqrt(var + EPS) * gamma + beta

    def _L0_ffn_ref(x, gate_w, rms_w, W1, W2, W3):
        import jax, jax.numpy as jnp
        import numpy as np
        E, K = (8, 2)
        DM, DE = (128, 352)
        B, S = (1, 256)
        EPS = 1e-06

        def _rmsnorm(x, w):
            var = jnp.mean(jnp.square(x), axis=-1, keepdims=True)
            return x * jax.lax.rsqrt(var + EPS) * w
        y = _rmsnorm(x, rms_w)
        logits = jnp.einsum('bsd,ed->bse', y, gate_w)
        vals, idx = jax.lax.top_k(logits, K)
        w = jax.nn.softmax(vals, axis=-1)
        w_full = jnp.einsum('bsk,bske->bse', w, jax.nn.one_hot(idx, E, dtype=x.dtype))
        up = jnp.einsum('bsd,end->bsen', y, W1)
        gate = jnp.einsum('bsd,end->bsen', y, W2)
        h = jax.nn.silu(up) * gate
        out = jnp.einsum('bsen,emn->bsem', h, W3)
        comb = jnp.einsum('bsem,bse->bsm', out, w_full)
        return x + comb

    def _L1_attn_a_ref(x, Wq, bq, Wk, bk, Wv, bv, phase_bias):
        import jax, jax.numpy as jnp
        import numpy as np
        import math
        B, S, D = (2, 512, 128)
        d = x.shape[-1]
        wavelengths = jnp.arange(1, d + 1, dtype=jnp.float32) * (2.0 * math.pi / d)
        inv_wl = 1.0 / (wavelengths + 1e-08)
        Q = jnp.einsum('bsd,ed->bse', x, Wq) + bq
        K = jnp.einsum('bsd,ed->bse', x, Wk) + bk
        V = jnp.einsum('bsd,ed->bse', x, Wv) + bv
        theta_q = Q * inv_wl + phase_bias
        theta_k = K * inv_wl + phase_bias
        sim = jnp.einsum('bsd,btd->bst', jnp.cos(theta_q), jnp.cos(theta_k)) + jnp.einsum('bsd,btd->bst', jnp.sin(theta_q), jnp.sin(theta_k))
        weights = jax.nn.softmax(sim / math.sqrt(d), axis=-1)
        return jnp.einsum('bst,btd->bsd', weights, V)

    def _L1_attn_b_ref(x, Wq, Wk, Wv, Wo, bo):
        import jax, jax.numpy as jnp
        import numpy as np
        B, S, D_IN, D_OUT, H = (2, 256, 128, 128, 16)
        HD = D_OUT // H
        b, s, _ = x.shape

        def to_heads(t):
            return t.reshape(b, s, H, HD).transpose(0, 2, 1, 3)
        Q = to_heads(x @ Wq)
        K = to_heads(x @ Wk)
        V = to_heads(x @ Wv)
        scale = 1.0 / jnp.sqrt(jnp.asarray(HD, x.dtype))
        scores = jnp.einsum('bhqd,bhkd->bhqk', Q, K) * scale
        causal_mask = jnp.triu(jnp.ones((s, s), dtype=bool), k=1)
        scores = jnp.where(causal_mask, jnp.asarray(-1000000.0, scores.dtype), scores)
        weights = jax.nn.softmax(scores, axis=-1)
        attn = jnp.einsum('bhqk,bhkd->bhqd', weights, V)
        attn = attn.reshape(b, s, D_OUT)
        return attn @ Wo + bo

    def _L1_ffn_ref(x, gate_w, gate_b, w1, b1, w2, b2):
        import jax, jax.numpy as jnp
        import numpy as np
        B, S, H, F, E, K = (4, 256, 128, 512, 8, 2)
        Bb, Ss, Hh = x.shape
        xf = x.reshape(-1, Hh)
        gate = jax.nn.softmax(xf @ gate_w + gate_b)
        topv, topi = jax.lax.top_k(gate, K)
        topv = topv / topv.sum(-1, keepdims=True)
        combine = (jax.nn.one_hot(topi, gate.shape[-1], dtype=xf.dtype) * topv[..., None]).sum(1)

        def body(acc, p):
            w1e, b1e, w2e, b2e, ce = p
            h = jax.nn.relu(xf @ w1e + b1e)
            y = h @ w2e + b2e
            return (acc + y * ce[:, None], None)
        acc0 = jnp.zeros_like(xf)
        out, _ = jax.lax.scan(body, acc0, (w1, b1, w2, b2, combine.T))
        return out.reshape(Bb, Ss, Hh)
    x = L0_attn_a_x
    x = x + _L0_attn_a_ref(_layernorm(x, axis=-1), L0_attn_a_A_log, L0_attn_a_W_delta, L0_attn_a_b_delta, L0_attn_a_W_B, L0_attn_a_W_C, L0_attn_a_D_skip, L0_attn_a_norm_weight)
    x = x + _L0_ffn_ref(_layernorm(x, axis=-1), L0_ffn_gate_w, L0_ffn_rms_w, L0_ffn_W1, L0_ffn_W2, L0_ffn_W3)
    x = x + _L0_attn_b_ref(_layernorm(x, axis=-1), L0_attn_b_adaptive_scale, L0_attn_b_Wq, L0_attn_b_bq, L0_attn_b_Wk, L0_attn_b_bk, L0_attn_b_Wv, L0_attn_b_bv, L0_attn_b_Wo, L0_attn_b_bo, L0_attn_b_gamma, L0_attn_b_beta)
    x = x + _L0_ffn_ref(_layernorm(x, axis=-1), L0_ffn_gate_w, L0_ffn_rms_w, L0_ffn_W1, L0_ffn_W2, L0_ffn_W3)
    x = x + _L1_attn_a_ref(_layernorm(x, axis=-1), L1_attn_a_Wq, L1_attn_a_bq, L1_attn_a_Wk, L1_attn_a_bk, L1_attn_a_Wv, L1_attn_a_bv, L1_attn_a_phase_bias)
    x = x + _L1_ffn_ref(_layernorm(x, axis=-1), L1_ffn_gate_w, L1_ffn_gate_b, L1_ffn_w1, L1_ffn_b1, L1_ffn_w2, L1_ffn_b2)
    x = x + _L1_attn_b_ref(_layernorm(x, axis=-1), L1_attn_b_Wq, L1_attn_b_Wk, L1_attn_b_Wv, L1_attn_b_Wo, L1_attn_b_bo)
    x = x + _L1_ffn_ref(_layernorm(x, axis=-1), L1_ffn_gate_w, L1_ffn_gate_b, L1_ffn_w1, L1_ffn_b1, L1_ffn_w2, L1_ffn_b2)
    return x

_drawn_inputs = setup_inputs


def setup_inputs(seed=0):
    import zlib

    import numpy as np

    out = dict(_drawn_inputs(seed))
    spreads = {'L0_attn_a_norm_weight': (1.0, 0.2),
     'L0_attn_b_adaptive_scale': (1.0, 0.6),
     'L0_attn_b_gamma': (1.0, 0.2),
     'L0_attn_b_beta': (0.0, 0.27),
     'L0_ffn_rms_w': (1.0, 0.6),
     'L1_attn_a_phase_bias': (0.0, 2.0),
     'L1_ffn_gate_b': (0.0, 0.1),
     'L1_ffn_b1': (0.0, 0.382),
     'L1_ffn_b2': (0.0, 0.271)}
    factors = {'L0_attn_a_b_delta': 4.988,
     'L0_attn_b_Wq': 4.071,
     'L0_attn_b_bq': 8.0,
     'L0_attn_b_Wk': 4.762,
     'L0_attn_b_bk': 64.0,
     'L0_attn_b_Wv': 3.425,
     'L0_attn_b_bo': 3.159,
     'L0_ffn_gate_w': 8.0,
     'L0_ffn_W1': 8.0,
     'L0_ffn_W2': 8.0,
     'L0_ffn_W3': 8.0,
     'L1_attn_a_Wq': 6.963,
     'L1_attn_a_bq': 22.14,
     'L1_attn_a_Wk': 8.0,
     'L1_attn_a_bk': 21.553,
     'L1_attn_a_Wv': 3.187,
     'L1_attn_b_Wq': 8.0,
     'L1_attn_b_Wk': 8.0,
     'L1_attn_b_Wv': 8.0,
     'L1_attn_b_Wo': 8.0,
     'L1_attn_b_bo': 8.0}
    for name, (base, spread) in spreads.items():
        noise = np.random.default_rng([zlib.crc32(name.encode()), seed]).standard_normal(out[name].shape)
        drawn = base * np.exp(spread * noise) if base else spread * noise
        out[name] = jnp.asarray(drawn.astype(out[name].dtype))
    for name, factor in factors.items():
        out[name] = (out[name] * factor).astype(out[name].dtype)
    return out
```

```python
import math

import numpy as np

import concourse.bass as bass
from concourse import mybir

F32 = mybir.dt.float32
BF16 = mybir.dt.bfloat16
F16 = mybir.dt.float16
ACT = mybir.ActivationFunctionType
ALU = mybir.AluOpType
AX = mybir.AxisListType

D = 128
S = 512
NB = 4
T = S // 128
NT = NB * T
E = 8
NS = 16
DE = 352
DEC = 3
FE = 512
FC = FE // 128
H0, HD0 = 16, 64
PAIRS = H0 // 2
H1, HD1 = 16, 8
GROUPS = H1 // 4
CAUSAL_END = 3 * D + 2 * GROUPS * 128 + D + 16 * D
EXP_LN = "natural_log_exp_and_others"
LN_EPS, RMS_EPS = 1e-5, 1e-6
BOTH_SCALE, BOTH_EPS = 1.0 + RMS_EPS, LN_EPS * RMS_EPS
DT_MIN, DT_MAX = 1e-4, 10.0
CENTER, HALF = (DT_MAX + DT_MIN) / 2.0, (DT_MAX - DT_MIN) / 2.0
MAGIC = 1.5 * 2.0 ** 23
TWO_PI_HI = 6.28125
TWO_PI_LO = 2.0 * math.pi - TWO_PI_HI
PI_F = float(np.nextafter(np.float32(math.pi), np.float32(0)))

W_SCALE, Y_SCALE, H_SCALE = 2.0 ** 10, 2.0 ** 6, 2.0 ** 6
UP_BACK, DOWN_BACK = 1.0 / (W_SCALE * Y_SCALE), 1.0 / (W_SCALE * H_SCALE)
F0_COLS = 2 * E * DE + E * DEC * D
F1_COLS = E * FE + E * FC * D

COLS = {}
for _name, _n in (("A_log", NS), ("b_delta", 1), ("D_skip", 1), ("norm_w", 1), ("rms_w", 1),
                  ("adaptive", PAIRS), ("bq", PAIRS), ("bk", PAIRS), ("bv", PAIRS), ("bo", 1), ("gamma", 1),
                  ("beta", 1), ("pq", 1), ("pk", 1), ("pv", 1), ("phase", 1), ("inv_wl", 1),
                  ("co", 1), ("one_row", 1), ("low_q", 1), ("low_k", 1), ("b1", E * FC)):
    COLS[_name] = (sum(n for _, n in COLS.values()), _n)
NCOLS = sum(n for _, n in COLS.values())


def hybrid(nc, x_t, cols_d, ident_d, mask_d, wm_d, f0_up_d, f0_gate_d, f0_down_d, f0_router_d,
           qkv_d, wo_d, phase_w_d, causal_w_d, f1_up_d, f1_down_d, f1_router_d, f1_rb_d,
           f1_b2_d, out, phases=range(8)):
    from contextlib import ExitStack
    ctx = ExitStack()
    with ctx:
        def sb(name, shape, dt=F32):
            return ctx.enter_context(nc.sbuf_tensor(name, shape, dt))

        def sem(name):
            return ctx.enter_context(nc.semaphore(name))

        x = sb("x", [D, NB, S])
        sq = sb("sq", [D, NB, S])
        xn = sb("xn", [D, NB, S])
        y = sb("y", [D, NB, S])
        rstd, rstd2 = xn, y
        cols = sb("cols", [D, NCOLS])
        ident = sb("ident_sb", [128, 128])
        masks = sb("masks", [128, 3, 128])
        mean_w = sb("mean_w", [128, 128])
        center_w = sb("center_w", [128, 128])
        ones = sb("ones", [128, 128])
        kc = sb("kc", [128, 8])
        wm = sb("wm", [D, D + 2 * NS])
        f0_router = sb("f0_router", [D, E])
        f1_router = sb("f1_router", [D, E])
        f1_rb = sb("f1_rb", [128, E])
        f1_b2 = sb("f1_b2", [E, D])
        hot = sb("hot", [128, 6, NT, E])
        w_rt = sb("w_rt", [128, NT, E])
        rev = sb("rev", [128, NT, E])
        ident_h = sb("ident_h", [128, 128], F16)
        b2_s = sb("b2_s", [E, D])
        raw = sb("raw", [128, F0_COLS])
        w_h = sb("w_h", [128, F0_COLS], F16)
        w_l = sb("w_l", [128, F0_COLS], F16)
        small_w = sb("small_w", [128, CAUSAL_END])
        WK = sb("WK", [128, 19200])
        y_h = sq[:, :, :].bitcast(F16)[:, :, 0:S]
        y_l = sq[:, :, :].bitcast(F16)[:, :, S:2 * S]
        P = ctx.enter_context(nc.psum_tensor("P", [128, 8, S], F32))

        def col(name, i=0, lo=0, hi=128):
            return cols[lo:hi, COLS[name][0] + i:COLS[name][0] + i + 1]

        K_LN, K_BOTH, K_ONE, K_TANH, K_HALFPI = range(5)

        def const(k, lo=0, hi=128):
            return kc[lo:hi, k:k + 1]

        x_loaded = sem("x_loaded")
        w_loaded = [sem(f"w_loaded{p}") for p in range(8)]
        consts_set = sem("consts_set")
        x_done = sem("x_done")
        stored = sem("stored")
        dve_own = sem("dve_own")
        act_own = sem("act_own")
        pool_own = sem("pool_own")
        xc_ready = sem("xc_ready")
        sq_ready = sem("sq_ready")
        var_ready = sem("var_ready")
        ln_ready = sem("ln_ready")
        rstd_ready = sem("rstd_ready")
        rstd2_ready = sem("rstd2_ready")
        xn_ready = sem("xn_ready")
        y_ready = sem("y_ready")
        resid_ready = sem("resid_ready")

        class Own:

            def __init__(self, eng, s):
                self.eng, self.sem, self.n, self.base = eng, s, 0, 0

            def link(self, ins):
                self.n += 1
                ins.then_inc(self.sem, 1)
                self.eng.wait_ge(self.sem, self.base + self.n)

            def loop(self, i, per):
                self.saved, self.per = self.n, per
                self.base, self.n = self.n + i * per, 0

            def end(self, times):
                assert self.n == self.per, (self.n, self.per)
                self.base, self.n = 0, self.saved + times * self.per

        def norm_pe(pe, k, src):
            for c in range(NB):
                nc.tensor.matmul(P[:, c, :], center_w[:, :], src[:, c, :], start=True, stop=True)\
                  .then_inc(xc_ready, 1)
            for c in range(NB):
                pe.wait_ge(sq_ready, NB * k + c + 1)
                nc.tensor.matmul(P[:, 4 + c, :], mean_w[:, :], sq[:, c, :], start=True, stop=True)\
                  .then_inc(var_ready, 1)

        def norm_act(act, k, single, both, k2):
            for c in range(NB):
                act.wait_ge(xc_ready, NB * k + c + 1)
                nc.scalar.activation(sq[:, c, :], P[:, c, :], ACT.Square).then_inc(sq_ready, 1)
            kinds = [kind for want, kind in ((single, (rstd, rstd_ready, 1.0, K_LN)),
                                             (both, (rstd2, rstd2_ready, BOTH_SCALE, K_BOTH))) if want]
            jobs = [(c,) + kind for c in range(NB) for kind in kinds]
            for n, (c, dst, done, scale, eps) in enumerate(jobs + [jobs[-1]]):
                if n < len(jobs):
                    act.wait_ge(var_ready, NB * k + c + 1)
                    nc.scalar.activation(dst[:, c, :], P[:, 4 + c, :], ACT.Ln, scale=scale,
                                         bias=const(eps)).then_inc(ln_ready, 1)
                if n >= 1:
                    act.wait_ge(ln_ready, NB * k2 + n)
                    c, dst, done = jobs[n - 1][:3]
                    nc.scalar.activation(dst[:, c, :], dst[:, c, :], ACT.Exp, scale=-0.5).then_inc(done, 1)

        NORMS = []
        for p in phases:
            NORMS.append((p, p != 0, p in (0, 1, 3)))
            if p == 2:
                NORMS.append(("post", True, False))
        norm_of = {}
        singles = boths = lns = 0
        for k, (p, s1, b2) in enumerate(NORMS):
            norm_of[p] = (k, singles, boths, lns)
            singles += s1
            boths += b2
            lns += s1 + b2
        xns = {}
        nx = ny = nr = 0
        for p in phases:
            xns[p] = (nx, ny, nr)
            nx += p not in (0,)
            ny += p in (0, 1, 3)
            nr += p in (1, 3)
        at = {p: NB * i + 1 for i, p in enumerate(phases)}

        def start(eng, p):
            eng.wait_ge(x_done, at[p])
            if p == phases[0]:
                eng.wait_ge(x_loaded, 16 * 4)
                eng.wait_ge(consts_set, 2)

        m_z_ready = sem("m_z_ready")
        m_sp_ready = sem("m_sp_ready")
        m_soft_ready = sem("m_soft_ready")
        m_tanh_ready = sem("m_tanh_ready")
        m_delta_ready = sem("m_delta_ready")
        m_root_ready = sem("m_root_ready")
        m_bc_ready = sem("m_bc_ready")
        m_u_ready = sem("m_u_ready")
        m_r_ready = sem("m_r_ready")
        m_a_ready = sem("m_a_ready")
        m_bx_ready = sem("m_bx_ready")
        m_h_ready = sem("m_h_ready")
        m_g_ready = sem("m_g_ready")
        m_y_ready = sem("m_y_ready")

        C_BANKS = (2, 3, 5, 6)
        delta = WK[:, 0:2048].rearrange("p (c s) -> p c s", c=NB)
        wsq = WK[:, 2048:4096].rearrange("p (c s) -> p c s", c=NB)
        m_z = WK[:, 4096:6144].rearrange("p (c s) -> p c s", c=NB)
        m_t = WK[:, 6144:8192].rearrange("p (c s) -> p c s", c=NB)
        m_half = WK[:, 8192:8208]
        mb = 8208
        m_r = WK[:, mb:mb + 2048].rearrange("p (c s) -> p c s", c=4)
        m_a = WK[:, mb + 2048:mb + 4096].rearrange("p (c s) -> p c s", c=4)
        m_u = WK[:, mb + 4096:mb + 5120].rearrange("p (c s) -> p c s", c=2)
        m_bx = WK[:, mb + 5120:mb + 6144].rearrange("p (c s) -> p c s", c=2)
        m_h = WK[:, mb + 6144:mb + 7168].rearrange("p (c s) -> p c s", c=2)
        m_g = WK[:, mb + 7168:mb + 9216].rearrange("p (c s) -> p c s", c=4)
        m_l = WK[:, mb + 9216:mb + 10240].rearrange("p (c s) -> p c s", c=2)

        def scan_pe(pe):
            start(pe, 0)
            norm_pe(pe, norm_of[0][0], x)
            for c in range(NB):
                pe.wait_ge(y_ready, c + 1)
                nc.tensor.matmul(P[:, c, :], wm[:, 0:D], y[:, c, :], start=True, stop=True)\
                  .then_inc(m_z_ready, 1)
            pe.wait_ge(m_u_ready, 1)
            with pe.Fori(0, NB) as b:
                for n in range(NS + 3):
                    if n < NS:
                        if n >= 2:
                            pe.wait_ge(m_u_ready, b * NS + n)
                        nc.tensor.matmul(P[:, n % 2, :], wm[:, D + n:D + n + 1].broadcast_to([D, 128]),
                                         y[:, bass.ds(b, 1), :], start=True, stop=True)
                        if n >= 4:
                            pe.wait_ge(m_g_ready, b * NS + n - 3)
                        nc.tensor.matmul(P[:, C_BANKS[n % 4], :],
                                         wm[:, D + NS + n:D + NS + n + 1].broadcast_to([D, 128]),
                                         y[:, bass.ds(b, 1), :], start=True, stop=True)\
                          .then_inc(m_bc_ready, 1)
                    if n >= 3:
                        pe.wait_ge(m_g_ready, b * NS + n - 2)
                        if n == 3:
                            pe.wait_ge(x_done, b + 1)
                        nc.tensor.matmul(P[:, 4, :], ident[:, :], m_g[:, (n - 3) % 4, :],
                                         start=(n == 3), stop=(n == NS + 2)).then_inc(m_y_ready, 1)

        def scan_act(act):
            k, singles, boths, lns = norm_of[0]
            start(act, 0)
            norm_act(act, k, False, True, lns)
            own = Own(act, act_own)
            for c in range(NB):
                act.wait_ge(m_z_ready, c + 1)
                nc.scalar.activation(m_z[:, c, :], P[:, c, :], ACT.Identity, bias=col("b_delta"))
                own.link(nc.scalar.activation(m_t[:, c, :], P[:, c, :], ACT.Abs, bias=col("b_delta")))
                own.link(nc.scalar.activation(m_t[:, c, :], m_t[:, c, :], ACT.Exp, scale=-1.0))
                nc.scalar.activation(m_t[:, c, :], m_t[:, c, :], ACT.Ln, bias=const(K_ONE))\
                  .then_inc(m_sp_ready, 1)
            act.wait_ge(m_soft_ready, NB)
            nc.scalar.activation(m_t[:, :, :], m_z[:, :, :], ACT.Tanh, scale=1.0 / HALF,
                                 bias=const(K_TANH)).then_inc(m_tanh_ready, 1)
            act.wait_ge(m_delta_ready, 1)
            nc.scalar.preload_act_table_set(EXP_LN)
            own.link(nc.scalar.activation(m_z[:, :, :], delta, ACT.Ln))
            nc.scalar.activation(m_z[:, :, :], m_z[:, :, :], ACT.Exp, scale=0.5).then_inc(m_root_ready, 1)
            own.link(nc.scalar.activation(m_half, cols[:, 0:NS], ACT.Exp))
            own.link(nc.scalar.activation(m_half, m_half, ACT.Copy, scale=0.5))
            with act.Fori(0, NB) as b:
                for n in range(0, NS, 2):
                    base = b * NS + n
                    for q in range(2):
                        nc.scalar.activation(m_l[:, q, :], delta[:, bass.ds(b, 1), :], ACT.Ln,
                                             scale=m_half[:, n + q:n + q + 1], bias=const(K_ONE))\
                          .then_inc(m_sp_ready, 1)
                    for q in range(2):
                        if n >= 4:
                            act.wait_ge(m_bx_ready, base + q - 3)
                        act.wait_ge(m_sp_ready, NB + base + q + 1)
                        nc.scalar.activation(m_r[:, (n + q) % 4, :], m_l[:, q, :], ACT.Exp,
                                             scale=-1.0).then_inc(m_r_ready, 1)
                    for q in range(2):
                        if n >= 4:
                            act.wait_ge(m_h_ready, base + q - 3)
                        act.wait_ge(m_r_ready, base + q + 1)
                        nc.scalar.activation(m_a[:, (n + q) % 4, :], m_r[:, (n + q) % 4, :], ACT.Copy,
                                             scale=2.0, bias=-1.0).then_inc(m_a_ready, 1)
                act.wait_ge(m_h_ready, b * NS + NS)

        def scan_pool(pool):
            with pool.Fori(0, NB) as b:
                for n in range(NS):
                    pool.wait_ge(m_r_ready, b * NS + n + 1)
                    pool.wait_ge(m_u_ready, b * NS + n + 2)
                    if n >= 2:
                        pool.wait_ge(m_h_ready, b * NS + n - 1)
                    nc.gpsimd.tensor_tensor(m_bx[:, n % 2, :], m_u[:, n % 2, :], m_r[:, n % 4, :],
                                            ALU.mult).then_inc(m_bx_ready, 1)

        def scan_dve(dve, own):
            k = norm_of[0][0]
            start(dve, 0)
            for c in range(NB):
                dve.wait_ge(rstd2_ready, c + 1)
                nc.vector.scalar_tensor_tensor(out=y[:, c, :], in0=P[:, c, :], scalar=col("norm_w"),
                                               in1=rstd2[:, c, :], op0=ALU.mult, op1=ALU.mult)\
                  .then_inc(y_ready, 1)
            for c in range(NB):
                dve.wait_ge(m_sp_ready, c + 1)
                nc.vector.scalar_tensor_tensor(out=m_z[:, c, :], in0=m_z[:, c, :], scalar=0.0,
                                               in1=m_t[:, c, :], op0=ALU.max, op1=ALU.add)\
                  .then_inc(m_soft_ready, 1)
            dve.wait_ge(m_tanh_ready, 1)
            nc.vector.tensor_scalar(delta, m_t, HALF, CENTER, ALU.mult, ALU.add)\
              .then_inc(m_delta_ready, 1)
            dve.wait_ge(m_root_ready, 1)
            dve.wait_ge(y_ready, NB)
            nc.vector.tensor_tensor(wsq, m_z, y[:, :, :], ALU.mult).then_inc(m_u_ready, 1)
            dve.wait_ge(m_u_ready, 1)
            with dve.Fori(0, NB) as b:
                for n in range(NS + 2):
                    if n < NS:
                        dve.wait_ge(m_bc_ready, b * NS + n + 1)
                        if n >= 2:
                            dve.wait_ge(m_bx_ready, b * NS + n - 1)
                        nc.vector.tensor_tensor(m_u[:, n % 2, :], wsq[:, bass.ds(b, 1), :].rearrange("p o s -> p (o s)"),
                                                P[:, n % 2, :], ALU.mult).then_inc(m_u_ready, 1)
                    if 1 <= n <= NS:
                        m = n - 1
                        dve.wait_ge(m_bx_ready, b * NS + m + 1)
                        dve.wait_ge(m_a_ready, b * NS + m + 1)
                        if m >= 2:
                            dve.wait_ge(m_g_ready, b * NS + m - 1)
                        nc.vector.tensor_tensor_scan(out=m_h[:, m % 2, :], data0=m_a[:, m % 4, :],
                                                     data1=m_bx[:, m % 2, :], initial=0.0,
                                                     op0=ALU.mult, op1=ALU.add).then_inc(m_h_ready, 1)
                    if n >= 2:
                        m = n - 2
                        dve.wait_ge(m_h_ready, b * NS + m + 1)
                        if m >= 4:
                            dve.wait_ge(m_y_ready, b * NS + m - 3)
                        nc.vector.tensor_tensor(m_g[:, m % 4, :], m_h[:, m % 2, :], P[:, C_BANKS[m % 4], :],
                                                ALU.mult).then_inc(m_g_ready, 1)
                own.loop(b, 1)
                dve.wait_ge(m_y_ready, b * NS + NS)
                own.link(nc.vector.scalar_tensor_tensor(
                    out=m_h[:, 0, :], in0=y[:, bass.ds(b, 1), :].rearrange("p o s -> p (o s)"),
                    scalar=col("D_skip"), in1=P[:, 4, :], op0=ALU.mult, op1=ALU.add))
                xb = x[:, bass.ds(b, 1), :].rearrange("p o s -> p (o s)")
                nc.vector.tensor_tensor(xb, xb, m_h[:, 0, :], ALU.add).then_inc(x_done, 1)
                own.end(NB)

        raw_split = sem("raw_split")
        e_yh_ready = sem("e_yh_ready")
        e_yl_ready = sem("e_yl_ready")
        e_logits_ready = sem("e_logits_ready")
        e_gap_ready = sem("e_gap_ready")
        e_exp_ready = sem("e_exp_ready")
        e_w_ready = sem("e_w_ready")
        e_wt_psum = sem("e_wt_psum")
        e_wth_ready = sem("e_wth_ready")
        e_wtl_ready = sem("e_wtl_ready")
        e_wb_ready = sem("e_wb_ready")
        e_yw_ready = sem("e_yw_ready")
        e_ywh_ready = sem("e_ywh_ready")
        e_ywl_ready = sem("e_ywl_ready")
        e_up_ready = sem("e_up_ready")
        e_gate_ready = sem("e_gate_ready")
        e_act_done = sem("e_act_done")
        e_h_ready = sem("e_h_ready")
        e_hh_ready = sem("e_hh_ready")
        e_hl_ready = sem("e_hl_ready")
        e_down_done = sem("e_down_done")
        e_out_ready = sem("e_out_ready")

        layers = [p for p in phases if p in (1, 3, 5, 7)]
        swiglu = [p for p in layers if p < 5]
        relu = [p for p in layers if p >= 5]

        e_yw = WK[:, 0:1024].rearrange("p (c s) -> p c s", c=2)
        e_act = WK[:, 1024:2048].rearrange("p (c s) -> p c s", c=2)
        e_hid = WK[:, 2048:3584].rearrange("p (c s) -> p c s", c=3)

        def halves(at, n, c):
            return WK[:, at:at + n * S // 2].bitcast(F16).rearrange("p (c s) -> p c s", c=c)

        e_ywh, e_ywl = halves(3584, 2, 2), halves(4096, 2, 2)
        e_hh, e_hl = halves(4608, 3, 3), halves(5376, 3, 3)
        w_th, w_tl = halves(6144, 4, 4)[0:E], halves(7168, 4, 4)[0:E]

        up_w = [w[:, 0:E * DE].rearrange("p (e n) -> p e n", e=E) for w in (w_h, w_l)]
        gate_w = [w[:, E * DE:2 * E * DE].rearrange("p (e n) -> p e n", e=E) for w in (w_h, w_l)]
        down_w = [w[:, 2 * E * DE:F0_COLS].rearrange("p (e j d) -> p e j d", e=E, j=DEC) for w in (w_h, w_l)]
        up1_w = [w[:, 0:E * FE].rearrange("p (e n) -> p e n", e=E) for w in (w_h, w_l)]
        down1_w = [w[:, E * FE:F1_COLS].rearrange("p (e j d) -> p e j d", e=E, j=FC) for w in (w_h, w_l)]
        HIGH, LOW = 0, 1
        TERMS = ((HIGH, HIGH), (HIGH, LOW), (LOW, HIGH))

        def product(out, weights, moving, first=True, last=True):
            for t, (a, b) in enumerate(TERMS):
                ins = nc.tensor.matmul(out, weights[a], moving[b], start=first and t == 0,
                                       stop=last and t == 2)
            return ins

        def chunk(buf, c):
            return buf[:, bass.ds(c, 1), :].rearrange("p o s -> p (o s)")

        def split_pool(pool, own, n, cols_n, count):
            own.link(nc.gpsimd.tensor_scalar(raw[:, 0:cols_n], raw[:, 0:cols_n], W_SCALE, 0.0,
                                             ALU.mult, ALU.add))
            own.link(nc.gpsimd.tensor_scalar(w_h[:, 0:cols_n], raw[:, 0:cols_n], 1.0, 0.0, ALU.mult, ALU.add))
            nc.gpsimd.tensor_tensor(w_l[:, 0:cols_n], raw[:, 0:cols_n], w_h[:, 0:cols_n], ALU.subtract)\
              .then_inc(raw_split, 1)

        def route_pe(pe, p, src, router):
            r = layers.index(p)
            for t in range(NT):
                if t % T == 0:
                    pe.wait_ge(y_ready if p < 5 else xn_ready, xns[p][p < 5] * NB + t // T + 1)
                ins = nc.tensor.matmul(P[:, 0, t * E:(t + 1) * E], src[:, t // T, t % T * 128:t % T * 128 + 128],
                                       router[:, :], start=True, stop=True)
            ins.then_inc(e_logits_ready, 1)
            pe.wait_ge(e_w_ready, r + 1)
            for t in range(NT):
                ins = nc.tensor.transpose(P[0:E, 1 + t // T, t % T * 128:t % T * 128 + 128],
                                          w_rt[:, t, :], ident[:, :])
            ins.then_inc(e_wt_psum, 1)
            pe.wait_ge(e_wth_ready, NB * (r + 1))
            pe.wait_ge(e_wtl_ready, NB * (r + 1))

        def route_act(act, p):
            r = layers.index(p)
            n = xns[p][p < 5] * NB
            for c in range(NB):
                act.wait_ge(y_ready if p < 5 else xn_ready, n + c + 1)
                nc.scalar.activation(y_h[:, c, :], (y if p < 5 else xn)[:, c, :], ACT.Copy, scale=Y_SCALE)\
                  .then_inc(e_yh_ready, 1)
            act.wait_ge(e_gap_ready, r + 1)
            nc.scalar.activation(hot[:, 4, :, 1:2], hot[:, 4, :, 0:1], ACT.Exp).then_inc(e_exp_ready, 1)
            act.wait_ge(e_wt_psum, r + 1)
            for c in range(NB):
                nc.scalar.activation(w_th[:, c, :], P[0:E, 1 + c, :], ACT.Copy, scale=Y_SCALE)\
                  .then_inc(e_wth_ready, 1)

        def route_dve(dve, own, p):
            r = layers.index(p)
            n = xns[p][p < 5] * NB
            src = y if p < 5 else xn
            for c in range(NB):
                dve.wait_ge(e_yh_ready, NB * r + c + 1)
                nc.vector.scalar_tensor_tensor(out=y_l[:, c, :], in0=src[:, c, :], scalar=Y_SCALE,
                                               in1=y_h[:, c, :], op0=ALU.mult, op1=ALU.subtract)\
                  .then_inc(e_yl_ready, 1)
            dve.wait_ge(e_logits_ready, r + 1)
            lg, first, second, key = (hot[:, i, :, :] for i in range(4))
            m1, m2, km = (hot[:, 5, :, i:i + 1] for i in range(3))
            gap, ex, den, w2 = (hot[:, 4, :, i:i + 1] for i in range(4))
            logits = P[:, 0, 0:NT * E].rearrange("p (t e) -> p t e", e=E)
            wide = [128, NT, E]
            if p < 5:
                own.link(nc.vector.tensor_copy(lg, logits))
            else:
                own.link(nc.vector.tensor_tensor(lg, logits, f1_rb[:, :].unsqueeze(1).broadcast_to(wide), ALU.add))
            for best, hit in ((m1, first), (m2, second)):
                own.link(nc.vector.tensor_reduce(out=best, in_=lg, op=ALU.max, axis=AX.X))
                own.link(nc.vector.tensor_tensor(key, lg, best.broadcast_to(wide), ALU.is_equal))
                own.link(nc.vector.tensor_tensor(key, key, rev[:, :, :], ALU.mult))
                own.link(nc.vector.tensor_reduce(out=km, in_=key, op=ALU.max, axis=AX.X))
                own.link(nc.vector.tensor_tensor(hit, key, km.broadcast_to(wide), ALU.is_equal))
                if hit is first:
                    own.link(nc.vector.scalar_tensor_tensor(out=lg, in0=hit, scalar=-3e38, in1=lg,
                                                            op0=ALU.mult, op1=ALU.add))
            nc.vector.tensor_tensor(gap, m2, m1, ALU.subtract).then_inc(e_gap_ready, 1)
            dve.wait_ge(e_exp_ready, r + 1)
            own.link(nc.vector.tensor_scalar_add(den, ex, 1.0))
            own.link(nc.vector.reciprocal(den, den))
            own.link(nc.vector.tensor_tensor(w2, ex, den, ALU.mult))
            own.link(nc.vector.tensor_tensor(first, first, den.broadcast_to(wide), ALU.mult))
            own.link(nc.vector.tensor_tensor(second, second, w2.broadcast_to(wide), ALU.mult))
            nc.vector.tensor_tensor(w_rt[:, :, :], first, second, ALU.add).then_inc(e_w_ready, 1)
            for c in range(NB):
                dve.wait_ge(e_wth_ready, NB * r + c + 1)
                nc.vector.scalar_tensor_tensor(out=w_tl[:, c, :], in0=P[0:E, 1 + c, :], scalar=Y_SCALE,
                                               in1=w_th[:, c, :], op0=ALU.mult, op1=ALU.subtract)\
                  .then_inc(e_wtl_ready, 1)

        def spread_weight(e, bank, c):
            pick = ident_h[0:E, e:e + 1].broadcast_to([E, 128])
            nc.tensor.matmul(P[:, bank, :], pick, w_th[:, bass.ds(c, 1), :], start=True, stop=False)
            nc.tensor.matmul(P[:, bank, :], pick, w_tl[:, bass.ds(c, 1), :], start=False, stop=True)\
              .then_inc(e_wb_ready, 1)

        def bases(p):
            sw, rl = [q for q in swiglu if q < p], [q for q in relu if q < p]
            n = NB * (len(sw) * E * DEC + len(rl) * E * FC)
            return n, NB * E * (len(sw) + len(rl)), NB * E * len(sw), NB * (len(sw) + len(rl))

        def part(j):
            return min(128, DE - 128 * j)

        def swiglu_pe(pe, p):
            steps0, wb0, yw0, out0 = bases(p)
            xd = at[p]
            start(pe, p)
            norm_pe(pe, norm_of[p][0], x)
            route_pe(pe, p, y, f0_router)
            pe.wait_ge(e_yl_ready, NB * (layers.index(p) + 1))
            pe.wait_ge(raw_split, 1)
            with pe.Fori(0, NB) as c:
                n0, e0 = c * (E * DEC) + steps0, c * E
                moving = [y_h[:, bass.ds(c, 1), :], y_l[:, bass.ds(c, 1), :]]

                def down(i):
                    m = part(i % DEC)
                    pe.wait_ge(e_hl_ready, n0 + i + 1)
                    if i == 0:
                        pe.wait_ge(x_done, c + xd)
                    ins = product(P[:, 6, :], [w[0:m, i // DEC, i % DEC, :] for w in down_w],
                                  [e_hh[0:m, i % 3, :], e_hl[0:m, i % 3, :]],
                                  first=i == 0, last=i == E * DEC - 1)
                    ins.then_inc(e_down_done, 1)

                spread_weight(0, 4, c)
                for e in range(E):
                    for j in range(DEC):
                        i, m = DEC * e + j, part(j)
                        if i >= 2:
                            pe.wait_ge(e_act_done, n0 + i - 1)
                        if j == 0 and 1 <= e < E - 1:
                            pe.wait_ge(e_yw_ready, e0 + yw0 + e)
                        product(P[0:m, i % 2, :], [w[:, e, 128 * j:128 * j + m] for w in up_w], moving)\
                            .then_inc(e_up_ready, 1)
                        if j == 0 and e + 1 < E:
                            spread_weight(e + 1, 4 + (e + 1) % 2, c)
                        if j == 0:
                            pe.wait_ge(e_ywl_ready, e0 + yw0 + e + 1)
                        if i >= 2:
                            pe.wait_ge(e_h_ready, n0 + i - 1)
                        product(P[0:m, 2 + i % 2, :], [w[:, e, 128 * j:128 * j + m] for w in gate_w],
                                [e_ywh[:, e % 2, :], e_ywl[:, e % 2, :]]).then_inc(e_gate_ready, 1)
                        if i >= 2:
                            down(i - 2)
                down(E * DEC - 2)
                down(E * DEC - 1)

        def swiglu_act(act, p):
            steps0, wb0, yw0, out0 = bases(p)
            k, singles, boths, lns = norm_of[p]
            start(act, p)
            norm_act(act, k, True, True, lns)
            route_act(act, p)
            with act.Fori(0, NB) as c:
                n0, e0 = c * (E * DEC) + steps0, c * E + yw0

                def high_yw(e):
                    act.wait_ge(e_yw_ready, e0 + e + 1)
                    if e >= 2:
                        act.wait_ge(e_gate_ready, n0 + DEC * (e - 1))
                    nc.scalar.activation(e_ywh[:, e % 2, :], e_yw[:, e % 2, :], ACT.Copy)\
                      .then_inc(e_ywh_ready, 1)

                def high_h(i):
                    m = part(i % DEC)
                    act.wait_ge(e_h_ready, n0 + i + 1)
                    if i >= 3:
                        act.wait_ge(e_down_done, n0 + i - 2)
                    nc.scalar.activation(e_hh[0:m, i % 3, :], e_hid[0:m, i % 3, :], ACT.Copy)\
                      .then_inc(e_hh_ready, 1)

                high_yw(0)
                for i in range(E * DEC + 1):
                    if i < E * DEC:
                        m = part(i % DEC)
                        act.wait_ge(e_up_ready, n0 + i + 1)
                        if i >= 2:
                            act.wait_ge(e_h_ready, n0 + i - 1)
                        nc.scalar.activation(e_act[0:m, i % 2, :], P[0:m, i % 2, :], ACT.Silu, scale=UP_BACK)\
                          .then_inc(e_act_done, 1)
                        if i % DEC == 0 and i // DEC + 1 < E:
                            high_yw(i // DEC + 1)
                    if i >= 1:
                        high_h(i - 1)

        def swiglu_dve(dve, own, p):
            steps0, wb0, yw0, out0 = bases(p)
            k, singles, boths, lns = norm_of[p]
            nxn, nyy, nrr = (NB * v for v in xns[p])
            start(dve, p)
            for c in range(NB):
                dve.wait_ge(rstd_ready, NB * singles + c + 1)
                nc.vector.tensor_tensor(xn[:, c, :], P[:, c, :], rstd[:, c, :], ALU.mult).then_inc(xn_ready, 1)
                dve.wait_ge(rstd2_ready, NB * boths + c + 1)
                nc.vector.scalar_tensor_tensor(out=y[:, c, :], in0=P[:, c, :], scalar=col("rms_w"),
                                               in1=rstd2[:, c, :], op0=ALU.mult, op1=ALU.mult)\
                  .then_inc(y_ready, 1)
            route_dve(dve, own, p)
            xd = at[p]
            with dve.Fori(0, NB) as c:
                n0, e0 = c * (E * DEC) + steps0, c * E
                yc = chunk(y, c)

                def weigh(e):
                    dve.wait_ge(e_wb_ready, e0 + wb0 + e + 1)
                    if e >= 2:
                        dve.wait_ge(e_ywl_ready, e0 + yw0 + e - 1)
                    nc.vector.tensor_tensor(e_yw[:, e % 2, :], yc, P[:, 4 + e % 2, :], ALU.mult)\
                      .then_inc(e_yw_ready, 1)

                def low_yw(e):
                    dve.wait_ge(e_ywh_ready, e0 + yw0 + e + 1)
                    if e >= 2:
                        dve.wait_ge(e_gate_ready, n0 + DEC * (e - 1))
                    nc.vector.tensor_tensor(e_ywl[:, e % 2, :], e_yw[:, e % 2, :], e_ywh[:, e % 2, :],
                                            ALU.subtract).then_inc(e_ywl_ready, 1)

                def low_h(i):
                    m = part(i % DEC)
                    dve.wait_ge(e_hh_ready, n0 + i + 1)
                    nc.vector.tensor_tensor(e_hl[0:m, i % 3, :], e_hid[0:m, i % 3, :], e_hh[0:m, i % 3, :],
                                            ALU.subtract).then_inc(e_hl_ready, 1)

                weigh(0)
                low_yw(0)
                for i in range(E * DEC + 1):
                    if i < E * DEC:
                        m, e = part(i % DEC), i // DEC
                        if i % DEC == 0 and e + 1 < E:
                            weigh(e + 1)
                        dve.wait_ge(e_gate_ready, n0 + i + 1)
                        dve.wait_ge(e_act_done, n0 + i + 1)
                        if i >= 3:
                            dve.wait_ge(e_hl_ready, n0 + i - 2)
                        nc.vector.scalar_tensor_tensor(out=e_hid[0:m, i % 3, :], in0=P[0:m, 2 + i % 2, :],
                                                       scalar=UP_BACK * H_SCALE, in1=e_act[0:m, i % 2, :],
                                                       op0=ALU.mult, op1=ALU.mult).then_inc(e_h_ready, 1)
                        if i % DEC == 1 and e + 1 < E:
                            low_yw(e + 1)
                    if i >= 1:
                        low_h(i - 1)
                dve.wait_ge(e_down_done, n0 + E * DEC)
                dve.wait_ge(resid_ready, NB * nrr // NB + NB)
                xb = chunk(x, c)
                nc.vector.scalar_tensor_tensor(out=xb, in0=P[:, 6, :], scalar=DOWN_BACK, in1=xb,
                                               op0=ALU.mult, op1=ALU.add).then_inc(x_done, 1)

        def swiglu_pool(pool, p):
            k = norm_of[p][0]
            for c in range(NB):
                pool.wait_ge(xn_ready, NB * xns[p][0] + c + 1)
                pool.wait_ge(xc_ready, NB * k + c + 1)
                nc.gpsimd.tensor_tensor(x[:, c, :], x[:, c, :], xn[:, c, :], ALU.add).then_inc(resid_ready, 1)

        def relu_pe(pe, p):
            steps0, wb0, yw0, out0 = bases(p)
            xd = at[p]
            start(pe, p)
            norm_pe(pe, norm_of[p][0], x)
            route_pe(pe, p, xn, f1_router)
            pe.wait_ge(e_yl_ready, NB * (layers.index(p) + 1))
            pe.wait_ge(raw_split, 1 + bool(swiglu))
            n_steps = E * FC
            with pe.Fori(0, NB) as c:
                n0, e0 = c * n_steps + steps0, c * E + wb0
                moving = [y_h[:, bass.ds(c, 1), :], y_l[:, bass.ds(c, 1), :]]

                def down(i):
                    pe.wait_ge(e_hl_ready, n0 + i + 1)
                    product(P[:, 6, :], [w[:, i // FC, i % FC, :] for w in down1_w],
                            [e_hh[:, i % 3, :], e_hl[:, i % 3, :]], first=False, last=i == n_steps - 1)\
                        .then_inc(e_down_done, 1)

                spread_weight(0, 3, c)
                for e in range(E):
                    for j in range(FC):
                        i = FC * e + j
                        if i >= 3:
                            pe.wait_ge(e_act_done, n0 + i - 2)
                        if j == 0 and 2 <= e < E - 1:
                            pe.wait_ge(e_h_ready, n0 + FC * (e - 1))
                        if i == 1:
                            pe.wait_ge(x_done, c + xd)
                        product(P[:, i % 3, :], [w[:, e, 128 * j:128 * j + 128] for w in up1_w], moving)\
                            .then_inc(e_up_ready, 1)
                        if j == 0 and e + 1 < E:
                            spread_weight(e + 1, 3 + (e + 1) % 3, c)
                        if i == 1:
                            for t, wt in enumerate((w_th, w_tl)):
                                for u in range(2):
                                    nc.tensor.matmul(P[:, 6, :], b2_parts[:, u, :], wt[:, bass.ds(c, 1), :],
                                                     start=t + u == 0, stop=False)
                        if i >= 2:
                            down(i - 2)
                down(n_steps - 2)
                down(n_steps - 1)

        b2_parts = sb("b2_parts", [E, 2, D], F16)

        def relu_act(act, p):
            steps0, wb0, yw0, out0 = bases(p)
            k, singles, boths, lns = norm_of[p]
            start(act, p)
            norm_act(act, k, True, False, lns)
            route_act(act, p)
            n_steps = E * FC
            with act.Fori(0, NB) as c:
                n0 = c * n_steps + steps0
                for i in range(n_steps + 1):
                    if i < n_steps:
                        act.wait_ge(e_up_ready, n0 + i + 1)
                        if i >= 2:
                            act.wait_ge(e_h_ready, n0 + i - 1)
                        nc.scalar.activation(e_act[:, i % 2, :], P[:, i % 3, :], ACT.Relu, scale=UP_BACK,
                                             bias=col("b1", i)).then_inc(e_act_done, 1)
                    if i >= 1:
                        act.wait_ge(e_h_ready, n0 + i)
                        if i >= 4:
                            act.wait_ge(e_down_done, n0 + i - 3)
                        nc.scalar.activation(e_hh[:, (i - 1) % 3, :], e_hid[:, (i - 1) % 3, :], ACT.Copy)\
                          .then_inc(e_hh_ready, 1)

        def relu_dve(dve, own, p):
            steps0, wb0, yw0, out0 = bases(p)
            k, singles, boths, lns = norm_of[p]
            start(dve, p)
            for c in range(NB):
                dve.wait_ge(rstd_ready, NB * singles + c + 1)
                nc.vector.tensor_tensor(xn[:, c, :], P[:, c, :], rstd[:, c, :], ALU.mult).then_inc(xn_ready, 1)
            route_dve(dve, own, p)
            n_steps = E * FC
            with dve.Fori(0, NB) as c:
                n0, e0 = c * n_steps + steps0, c * E + wb0
                for i in range(n_steps + 1):
                    if i < n_steps:
                        e = i // FC
                        if i % FC == 0:
                            dve.wait_ge(e_wb_ready, e0 + e + 1)
                        dve.wait_ge(e_act_done, n0 + i + 1)
                        if i >= 3:
                            dve.wait_ge(e_hl_ready, n0 + i - 2)
                        nc.vector.tensor_tensor(e_hid[:, i % 3, :], e_act[:, i % 2, :], P[:, 3 + e % 3, :],
                                                ALU.mult).then_inc(e_h_ready, 1)
                    if i >= 1:
                        dve.wait_ge(e_hh_ready, n0 + i)
                        nc.vector.tensor_tensor(e_hl[:, (i - 1) % 3, :], e_hid[:, (i - 1) % 3, :],
                                                e_hh[:, (i - 1) % 3, :], ALU.subtract).then_inc(e_hl_ready, 1)
                dve.wait_ge(e_down_done, n0 + n_steps)
                xb = chunk(x, c)
                nc.vector.scalar_tensor_tensor(out=xb, in0=P[:, 6, :], scalar=DOWN_BACK, in1=xb,
                                               op0=ALU.mult, op1=ALU.add).then_inc(x_done, 1)

        a_setup = sem("a_setup")
        a_xb_ready = sem("a_xb_ready")
        a_proj_ready = sem("a_proj_ready")
        a_evac_done = sem("a_evac_done")
        a_high_done = sem("a_high_done")
        a_low_done = sem("a_low_done")
        a_v_ready = sem("a_v_ready")
        a_bias_ready = sem("a_bias_ready")
        a_v_done = sem("a_v_done")
        a_s_ready = sem("a_s_ready")
        a_max_done = sem("a_max_done")
        a_row_ready = sem("a_row_ready")
        a_row_done = sem("a_row_done")
        a_st_ready = sem("a_st_ready")
        a_exp_done = sem("a_exp_done")
        a_pv_done = sem("a_pv_done")
        a_den_done = sem("a_den_done")
        a_rec_done = sem("a_rec_done")
        a_at_done = sem("a_at_done")
        a_out_done = sem("a_out_done")
        a_z_done = sem("a_z_done")
        a_zn_ready = sem("a_zn_ready")
        KV, MISC, ST = (4, 5), 7, (2, 3, 6)
        OUTB = 0
        QBUF = 3
        a_q1, a_q2, a_k1, a_k2 = (WK[:, 1536 * i:1536 * i + 1536].bitcast(F16)
                                  .rearrange("p (b o s) -> p b o s", b=QBUF, o=2) for i in range(4))
        a_f32 = WK[:, 6144:7168].rearrange("p (c s) -> p c s", c=2)
        a_v = WK[:, 7168:13312].rearrange("p (t a n) -> p t a n", t=T, a=PAIRS)
        a_pt = WK[:, 13312:15360].rearrange("p (c s) -> p c s", c=4)
        a_at = raw[:, 4096:8192].rearrange("p (c s) -> p c s", c=PAIRS)
        a_xb = WK[:, 16384:16896]
        a_rec = WK[:, 16896:17408]
        a_nm = WK[:, 17408:17416].bitcast(F16).rearrange("p (u t) -> p u t", u=4)
        a_qs = WK[:, 17424:17424 + PAIRS]
        a_bo = WK[:, 17450:17451]
        a_bqs = WK[:, 17440:17440 + PAIRS]
        qkv_w, wo_w = raw[:, 0:3072], raw[:, 3072:4096]
        HALVES = ((0, 64), (64, 128))

        def heads_pe(pe, p):
            start(pe, p)
            norm_pe(pe, norm_of[p][0], x)
            pe.wait_ge(xn_ready, NB * xns[p][0] + NB)
            for a in range(PAIRS):
                ins = nc.tensor.matmul(P[:, MISC, 0:1], wo_w[:, 128 * a:128 * a + 128], col("bv", a),
                                       start=a == 0, stop=a == PAIRS - 1)
            ins.then_inc(a_bias_ready, 1)
            pe.wait_ge(a_setup, 2)
            with pe.Fori(0, NB) as b:
                xb_dyn = xn[:, bass.ds(b, 1), :]

                def project(q, bank):
                    w0 = (q % 2) * H0 * HD0 + (q // 2) * 128
                    nc.tensor.matmul(P[:, bank, :], qkv_w[:, w0:w0 + 128], xb_dyn, start=True, stop=True)\
                      .then_inc(a_proj_ready, 1)

                def maxima(u, t):
                    lo, hi = HALVES[u % 2]
                    buf = u // 2 % QBUF
                    if 4 * u + t >= 2:
                        pe.wait_ge(a_max_done, b * 64 + 4 * u + t - 1)
                    nc.tensor.matmul(P[:, (4 * u + t) % 2, :], a_q1[lo:hi, buf, u % 2, 128 * t:128 * t + 128],
                                     a_k1[lo:hi, buf, u % 2, :], start=True, stop=True).then_inc(a_s_ready, 1)

                def max_row(u):
                    r = 64 if u % 2 == 0 else 0
                    pe.wait_ge(a_max_done, b * 64 + 4 * u + 4)
                    for t in range(T):
                        ins = nc.tensor.matmul(P[r:r + 1, MISC, 128 * t:128 * t + 128], a_nm[:, u % 4, t:t + 1],
                                               ident_h[:, :], start=True, stop=True)
                    ins.then_inc(a_row_ready, 1)

                def values(i):
                    u, t = i // T, i % T
                    pe.wait_ge(a_exp_done, b * 64 + i + 1)
                    if t == 0 and u >= 2:
                        pe.wait_ge(a_at_done, b * 16 + u - 1)
                    v0 = 64 * (u % 2)
                    nc.tensor.matmul(P[:, KV[u % 2], :], a_v[:, t, u // 2, v0:v0 + 128], a_pt[:, i % 4, :],
                                     start=t == 0, stop=t == T - 1).then_inc(a_pv_done, 1)

                def project_out(a):
                    pe.wait_ge(a_at_done, b * 16 + 2 * a + 2)
                    nc.tensor.matmul(P[:, OUTB, :], wo_w[:, 128 * a:128 * a + 128], a_at[:, a, :],
                                     start=a == 0, stop=a == PAIRS - 1).then_inc(a_out_done, 1)

                for q in range(4):
                    project(q, 4 + q)
                pe.wait_ge(a_xb_ready, b + 1)
                for v in range(2 * T):
                    if v >= 4:
                        pe.wait_ge(a_v_done, b * 8 + v - 3)
                    w0 = 2 * H0 * HD0 + 512 * (v % 2)
                    nc.tensor.matmul(P[:, v % 4, :], a_xb[:, 128 * (v // 2):128 * (v // 2) + 128],
                                     qkv_w[:, w0:w0 + 512], start=True, stop=True).then_inc(a_v_ready, 1)
                pe.wait_ge(a_v_done, b * 8 + 8)
                for u in range(2):
                    if u == 0:
                        pe.wait_ge(a_high_done, b * 16 + 2)
                    for t in range(T):
                        maxima(u, t)
                pe.wait_ge(a_evac_done, b * 16 + 4)
                max_row(0)
                for u in range(H0):
                    lo, hi = HALVES[u % 2]
                    buf, o = u // 2 % QBUF, u % 2
                    for t in range(T):
                        i = T * u + t
                        if t == 0 and u + 4 < 2 * PAIRS:
                            pe.wait_ge(a_row_done, b * 16 + u + 1)
                            project(u + 4, MISC)
                        if t == 2 and u + 1 < H0:
                            pe.wait_ge(a_evac_done, b * 16 + min(u + 5, 16))
                            pe.wait_ge(a_row_done, b * 16 + u + 1)
                            max_row(u + 1)
                        if t == 0:
                            pe.wait_ge(a_row_done, b * 16 + u + 1)
                            pe.wait_ge(a_low_done, b * 16 + 2 * (u // 2) + 2)
                        if i >= 3:
                            pe.wait_ge(a_exp_done, b * 64 + i - 2)
                        last_row = 65 if o == 0 else 128
                        nc.tensor.matmul(P[:, ST[i % 3], :], a_k1[:, buf, o, 128 * t:128 * t + 128],
                                         a_q1[:, buf, o, :], start=True, stop=False)
                        nc.tensor.matmul(P[:, ST[i % 3], :], a_k2[0:last_row, buf, o, 128 * t:128 * t + 128],
                                         a_q2[0:last_row, buf, o, :], start=False, stop=True)\
                          .then_inc(a_st_ready, 1)
                        if i >= 2:
                            values(i - 2)
                        if u + 2 < H0:
                            if t == 0:
                                pe.wait_ge(a_high_done, b * 16 + 2 * ((u + 2) // 2) + 2)
                            maxima(u + 2, t)
                values(T * H0 - 2)
                values(T * H0 - 1)
                for a in range(PAIRS):
                    project_out(a)
            pe.wait_ge(a_z_done, NB)
            norm_pe(pe, norm_of["post"][0], xn)

        def heads_act(act, p):
            k, singles, boths, lns = norm_of[p]
            start(act, p)
            norm_act(act, k, True, False, lns)
            act.wait_ge(a_setup, 2)
            with act.Fori(0, NB) as b:
                def evacuate(q, bank):
                    act.wait_ge(a_proj_ready, b * 16 + q + 1)
                    if q >= 2:
                        act.wait_ge(a_high_done, b * 16 + q - 1)
                        act.wait_ge(a_low_done, b * 16 + q - 1)
                    a = q // 2
                    if q % 2 == 0:
                        nc.scalar.activation(a_f32[:, 0, :], P[:, bank, :], ACT.Identity,
                                             scale=a_qs[:, a:a + 1], bias=a_bqs[:, a:a + 1]).then_inc(a_evac_done, 1)
                    else:
                        nc.scalar.activation(a_f32[:, 1, :], P[:, bank, :], ACT.Identity,
                                             bias=col("bk", a)).then_inc(a_evac_done, 1)

                def row(u):
                    r = 64 if u % 2 == 0 else 0
                    act.wait_ge(a_row_ready, b * 16 + u + 1)
                    nc.scalar.activation(a_q2[r:r + 1, u // 2 % QBUF, u % 2, :], P[r:r + 1, MISC, :], ACT.Copy)\
                      .then_inc(a_row_done, 1)

                def reciprocal(u):
                    (lo, hi), (dlo, dhi) = HALVES[u % 2], HALVES[1 - u % 2]
                    act.wait_ge(a_pv_done, b * 64 + 4 * u + 4)
                    if u >= 2:
                        act.wait_ge(a_at_done, b * 16 + u - 1)
                    nc.scalar.activation(a_rec[lo:hi, :], P[dlo:dhi, KV[u % 2], :], ACT.Ln).then_inc(a_den_done, 1)
                    act.wait_ge(a_den_done, b * 16 + u + 1)
                    nc.scalar.activation(a_rec[lo:hi, :], a_rec[lo:hi, :], ACT.Exp, scale=-1.0).then_inc(a_rec_done, 1)

                for q in range(2):
                    evacuate(q, 4 + q)
                for v in range(2 * T):
                    act.wait_ge(a_v_ready, b * 8 + v + 1)
                    dst = a_v[:, v // 2, 4 * (v % 2):4 * (v % 2) + 4, :].rearrange("p a (k n) -> p a k n", k=3)[:, :, 0::2, :]
                    nc.scalar.activation(dst, P[:, v % 4, :].rearrange("p (a k n) -> p a k n", a=4, k=2), ACT.Copy)\
                      .then_inc(a_v_done, 1)
                for q in range(2, 4):
                    evacuate(q, 4 + q)
                row(0)
                for u in range(H0):
                    for t in range(T):
                        i = T * u + t
                        if t == 3 and u + 1 < H0:
                            row(u + 1)
                        if t == 1 and u + 4 < 2 * PAIRS:
                            evacuate(u + 4, MISC)
                        if t == 2 and u >= 1:
                            reciprocal(u - 1)
                        act.wait_ge(a_st_ready, b * 64 + i + 1)
                        if i >= 4:
                            act.wait_ge(a_pv_done, b * 64 + i - 3)
                        nc.scalar.activation(a_pt[:, i % 4, :], P[:, ST[i % 3], :], ACT.Exp).then_inc(a_exp_done, 1)
                reciprocal(H0 - 1)
            k, singles, boths, lns = norm_of["post"]
            norm_act(act, k, True, False, lns)

        def heads_pool(pool, own, p):
            pool.wait_ge(x_done, at[p])
            nc.gpsimd.memset(a_v[:, :, :, 64:128], 1.0)
            nc.gpsimd.memset(a_q2[0:64, :, 1, :], 0.0)
            own.link(nc.gpsimd.memset(a_k2[0:64, :, 1, :], 0.0))
            nc.gpsimd.memset(a_k2[0:1, :, 1, :], 1.0)
            nc.gpsimd.memset(a_k2[64:65, :, 0, :], 1.0).then_inc(a_setup, 1)
            with pool.Fori(0, NB) as b:
                for q in range(2 * PAIRS):
                    buf = q // 2 % QBUF
                    pool.wait_ge(a_evac_done, b * 16 + q + 1)
                    first = True
                    for o, (lo, hi) in enumerate(HALVES):
                        src = a_f32[lo:hi, q % 2, :]
                        if q % 2 == 0:
                            outs = (a_q1[lo:hi, buf, o, :], a_q2[lo:hi, buf, o, :])
                        else:
                            outs = (a_k1[0:64, buf, o, :], a_k1[64:128, buf, o, :])
                        for dst in outs:
                            if first:
                                ins = nc.gpsimd.tensor_tensor(dst, src, ones[lo:hi, 0:1].broadcast_to([64, S]), ALU.mult)
                            else:
                                ins = nc.gpsimd.tensor_scalar(dst, src, 1.0, 0.0, ALU.mult, ALU.add)
                            first = False
                    ins.then_inc(a_high_done, 1)

        def heads_dve(dve, own, p):
            k, singles, boths, lns = norm_of[p]
            start(dve, p)
            dve.wait_ge(w_loaded[2], 32)
            for c in range(NB):
                dve.wait_ge(rstd_ready, NB * singles + c + 1)
                nc.vector.tensor_tensor(xn[:, c, :], P[:, c, :], rstd[:, c, :], ALU.mult).then_inc(xn_ready, 1)
            adaptive = cols[:, COLS["adaptive"][0]:COLS["adaptive"][0] + PAIRS]
            own.link(nc.vector.tensor_scalar(a_qs, adaptive, float(HD0) ** -0.5, None, ALU.mult))
            dve.wait_ge(xn_ready, NB * xns[p][0] + NB)
            dve.wait_ge(a_bias_ready, 1)
            nc.vector.tensor_tensor(a_bo, P[:, MISC, 0:1], col("bo"), ALU.add)
            nc.vector.tensor_tensor(a_bqs, cols[:, COLS["bq"][0]:COLS["bq"][0] + PAIRS], a_qs, ALU.mult)\
              .then_inc(a_setup, 1)
            with dve.Fori(0, NB) as b:
                def low(q):
                    buf = q // 2 % QBUF
                    dve.wait_ge(a_high_done, b * 16 + q + 1)
                    for o, (lo, hi) in enumerate(HALVES):
                        high = (a_q1, a_k1)[q % 2][lo:hi, buf, o, :]
                        if q % 2 == 0:
                            dst = a_q1[64 - lo:128 - lo, buf, o, :]
                        else:
                            dst = a_k2[lo:hi, buf, o, :]
                        ins = nc.vector.tensor_tensor(dst, a_f32[lo:hi, q % 2, :], high, ALU.subtract)
                    ins.then_inc(a_low_done, 1)

                def maxima(u, t):
                    dve.wait_ge(a_s_ready, b * 64 + 4 * u + t + 1)
                    nc.vector.tensor_reduce(out=a_nm[:, u % 4, t:t + 1], in_=P[:, (4 * u + t) % 2, :], op=ALU.max,
                                            axis=AX.X, negate=True).then_inc(a_max_done, 1)

                def normalise(u):
                    lo, hi = HALVES[u % 2]
                    dve.wait_ge(a_rec_done, b * 16 + u + 1)
                    nc.vector.tensor_tensor(a_at[lo:hi, u // 2, :], P[lo:hi, KV[u % 2], :], a_rec[lo:hi, :],
                                            ALU.mult).then_inc(a_at_done, 1)

                nc.vector.tensor_copy(a_xb, chunk(xn, b)).then_inc(a_xb_ready, 1)
                for q in range(2):
                    low(q)
                for u in range(2):
                    for t in range(T):
                        maxima(u, t)
                for q in range(2, 4):
                    low(q)
                for u in range(H0):
                    for t in range(T):
                        if u + 2 < H0:
                            maxima(u + 2, t)
                        if t == 3 and u >= 1:
                            normalise(u - 1)
                        if t == 3 and u + 4 < 2 * PAIRS:
                            low(u + 4)
                normalise(H0 - 1)
                dve.wait_ge(a_out_done, b * 8 + 8)
                xb = chunk(xn, b)
                nc.vector.scalar_tensor_tensor(out=xb, in0=P[:, OUTB, :], scalar=a_bo, in1=xb,
                                               op0=ALU.add, op1=ALU.add).then_inc(a_z_done, 1)
            k, singles, boths, lns = norm_of["post"]
            for c in range(NB):
                dve.wait_ge(rstd_ready, NB * singles + c + 1)
                own.link(nc.vector.scalar_tensor_tensor(out=xn[:, c, :], in0=P[:, c, :], scalar=col("gamma"),
                                                        in1=rstd[:, c, :], op0=ALU.mult, op1=ALU.mult))
                nc.vector.scalar_tensor_tensor(out=x[:, c, :], in0=xn[:, c, :], scalar=col("beta"),
                                               in1=x[:, c, :], op0=ALU.add, op1=ALU.add).then_inc(x_done, 1)

        h_setup = sem("h_setup")
        h_proj_ready = sem("h_proj_ready")
        h_v_ready = sem("h_v_ready")
        h_theta_ready = sem("h_theta_ready")
        h_v_done = sem("h_v_done")
        h_red_ready = sem("h_red_ready")
        h_abs_ready = sem("h_abs_ready")
        h_sin_ready = sem("h_sin_ready")
        h_cos_ready = sem("h_cos_ready")
        h_st_ready = sem("h_st_ready")
        h_exp_done = sem("h_exp_done")
        h_pv_done = sem("h_pv_done")
        h_sum_ready = sem("h_sum_ready")
        h_den_ready = sem("h_den_ready")
        h_den_done = sem("h_den_done")
        h_rec_done = sem("h_rec_done")
        h_sin, h_cos = (WK[:, 4096 * i:4096 * i + 4096].rearrange("p (c k s) -> p c k s", c=NB, k=2)
                        for i in range(2))
        h_v = WK[:, 8192:10240].rearrange("p (c s) -> p c s", c=NB)
        h_th, h_n = (WK[:, 10240 + 2048 * i:12288 + 2048 * i].rearrange("p (c k s) -> p c k s", c=2, k=2)
                     for i in range(2))
        h_pt = WK[:, 14336:16384].rearrange("p (t s) -> p t s", t=T)
        h_rec, h_o, h_sum = (WK[:, 16384 + 512 * i:16896 + 512 * i] for i in range(3))
        h_bias = WK[:, 17920:17922]
        phase_w = [small_w[:, 128 * i:128 * i + 128] for i in range(3)]
        V_BANK, PV_BANK, DEN = 6, 4, 5

        def phase_pe(pe, p):
            start(pe, p)
            norm_pe(pe, norm_of[p][0], x)
            for c in range(NB):
                pe.wait_ge(xn_ready, NB * xns[p][0] + (NB if c == 0 else c + 1))
                for k in range(2):
                    if c >= 2:
                        pe.wait_ge(h_theta_ready, 2 * (c - 2) + k + 1)
                    nc.tensor.matmul(P[:, 2 * (c % 2) + k, :], phase_w[k], xn[:, c, :], start=True, stop=True)\
                      .then_inc(h_proj_ready, 1)
                if c >= 2:
                    pe.wait_ge(h_v_done, c - 1)
                for t in range(T):
                    ins = nc.tensor.matmul(P[:, V_BANK + c % 2, 128 * t:128 * t + 128],
                                           xn[:, c, 128 * t:128 * t + 128], phase_w[2], start=True, stop=True)
                ins.then_inc(h_v_ready, 1)
            pe.wait_ge(h_theta_ready, 2 * NB)
            for b in range(NB):
                def values(t):
                    pe.wait_ge(h_exp_done, b * T + t + 1)
                    if t == 0:
                        pe.wait_ge(h_v_done, NB)
                        pe.wait_ge(x_done, b + at[p])
                    nc.tensor.matmul(P[:, PV_BANK, :], h_v[:, b, 128 * t:128 * t + 128], h_pt[:, t, :],
                                     start=t == 0, stop=t == T - 1).then_inc(h_pv_done, 1)

                pe.wait_ge(h_cos_ready, b + 1)
                for t in range(T):
                    for f in (h_cos, h_sin):
                        ins = nc.tensor.matmul(P[:, t, :], f[:, b, 1, 128 * t:128 * t + 128],
                                               f[:, b, 0, :], start=f is h_cos, stop=f is h_sin)
                    ins.then_inc(h_st_ready, 1)
                    if t >= 2:
                        values(t - 2)
                values(T - 2)
                values(T - 1)
                pe.wait_ge(h_sum_ready, b + 1)
                nc.tensor.matmul(P[:, DEN, :], ones[:, :], h_sum, start=True, stop=True).then_inc(h_den_ready, 1)

        def phase_act(act, p):
            k, singles, boths, lns = norm_of[p]
            start(act, p)
            norm_act(act, k, True, False, lns)
            act.wait_ge(h_setup, 1)

            def sines(c):
                act.wait_ge(h_red_ready, c + 1)
                nc.scalar.activation(h_n[:, c % 2, :, :], h_th[:, c % 2, :, :], ACT.Abs).then_inc(h_abs_ready, 1)
                nc.scalar.activation(h_sin[:, c, :, :], h_th[:, c % 2, :, :], ACT.Sin).then_inc(h_sin_ready, 1)
                act.wait_ge(h_abs_ready, c + 1)
                nc.scalar.activation(h_cos[:, c, :, :], h_n[:, c % 2, :, :], ACT.Sin, scale=-1.0,
                                     bias=const(K_HALFPI)).then_inc(h_cos_ready, 1)

            for c in range(NB):
                for q in range(2):
                    act.wait_ge(h_proj_ready, 2 * c + q + 1)
                    if c >= 2:
                        act.wait_ge(h_sin_ready, c - 1)
                    nc.scalar.activation(h_th[:, c % 2, q, :], P[:, 2 * (c % 2) + q, :], ACT.Identity,
                                         scale=col("inv_wl"), bias=h_bias[:, q:q + 1]).then_inc(h_theta_ready, 1)
                act.wait_ge(h_v_ready, c + 1)
                nc.scalar.activation(h_v[:, c, :], P[:, V_BANK + c % 2, :], ACT.Copy).then_inc(h_v_done, 1)
                if c >= 1:
                    sines(c - 1)
            sines(NB - 1)
            nc.scalar.preload_act_table_set(EXP_LN)
            with act.Fori(0, NB) as b:
                for t in range(T):
                    act.wait_ge(h_st_ready, b * T + t + 1)
                    nc.scalar.activation(h_pt[:, t, :], P[:, t, :], ACT.Exp, scale=float(D) ** -0.5)\
                      .then_inc(h_exp_done, 1)
                act.wait_ge(h_den_ready, b + 1)
                nc.scalar.activation(h_rec, P[:, DEN, :], ACT.Ln).then_inc(h_den_done, 1)
                act.wait_ge(h_den_done, b + 1)
                nc.scalar.activation(h_rec, h_rec, ACT.Exp, scale=-1.0).then_inc(h_rec_done, 1)

        def phase_dve(dve, own, p):
            k, singles, boths, lns = norm_of[p]
            start(dve, p)
            for q, name in enumerate(("pq", "pk")):
                ins = nc.vector.tensor_scalar(h_bias[:, q:q + 1], col(name), col("inv_wl"), col("phase"),
                                              ALU.mult, ALU.add)
            ins.then_inc(h_setup, 1)
            for c in range(NB):
                dve.wait_ge(rstd_ready, NB * singles + c + 1)
                nc.vector.tensor_tensor(xn[:, c, :], P[:, c, :], rstd[:, c, :], ALU.mult).then_inc(xn_ready, 1)
            for c in range(NB):
                th, n = h_th[:, c % 2, :, :], h_n[:, c % 2, :, :]
                dve.wait_ge(h_theta_ready, 2 * c + 2)
                if c >= 2:
                    dve.wait_ge(h_cos_ready, c - 1)
                own.link(nc.vector.tensor_scalar(n, th, 1.0 / (2.0 * math.pi), MAGIC, ALU.mult, ALU.add))
                own.link(nc.vector.tensor_scalar(n, n, MAGIC, None, ALU.subtract))
                for part_2pi in (TWO_PI_HI, TWO_PI_LO):
                    own.link(nc.vector.scalar_tensor_tensor(out=th, in0=n, scalar=-part_2pi, in1=th,
                                                            op0=ALU.mult, op1=ALU.add))
                nc.vector.tensor_scalar(th, th, PI_F, -PI_F, ALU.min, ALU.max).then_inc(h_red_ready, 1)
            with dve.Fori(0, NB) as b:
                own.loop(b, 3)
                dve.wait_ge(h_exp_done, b * T + 2)
                own.link(nc.vector.tensor_tensor(h_sum, h_pt[:, 0, :], h_pt[:, 1, :], ALU.add))
                dve.wait_ge(h_exp_done, b * T + 3)
                own.link(nc.vector.tensor_tensor(h_sum, h_sum, h_pt[:, 2, :], ALU.add))
                dve.wait_ge(h_exp_done, b * T + 4)
                nc.vector.tensor_tensor(h_sum, h_sum, h_pt[:, 3, :], ALU.add).then_inc(h_sum_ready, 1)
                dve.wait_ge(h_rec_done, b + 1)
                dve.wait_ge(h_pv_done, b * T + T)
                own.link(nc.vector.tensor_tensor(h_o, P[:, PV_BANK, :], h_rec, ALU.mult))
                xb = chunk(x, b)
                nc.vector.scalar_tensor_tensor(out=xb, in0=h_o, scalar=col("pv"), in1=xb,
                                               op0=ALU.add, op1=ALU.add).then_inc(x_done, 1)
                own.end(NB)

        c_setup = sem("c_setup")
        c_xb_ready = sem("c_xb_ready")
        c_proj_ready = sem("c_proj_ready")
        c_high_done = sem("c_high_done")
        c_parts_done = sem("c_parts_done")
        c_v_ready = sem("c_v_ready")
        c_v_done = sem("c_v_done")
        c_s_ready = sem("c_s_ready")
        c_max_done = sem("c_max_done")
        c_rows_ready = sem("c_rows_ready")
        c_q_done = sem("c_q_done")
        c_st_ready = sem("c_st_ready")
        c_exp_done = sem("c_exp_done")
        c_ph_done = sem("c_ph_done")
        c_pl_dve = sem("c_pl_dve")
        c_pl_pool = sem("c_pl_pool")
        c_pv_done = sem("c_pv_done")
        c_u_done = sem("c_u_done")
        c_den_ready = sem("c_den_ready")
        c_ln_done = sem("c_ln_done")
        c_rec_done = sem("c_rec_done")
        c_at_done = sem("c_at_done")
        c_out_done = sem("c_out_done")
        STEPS = 4 * T
        CN = GROUPS * STEPS
        RING, LAG = 6, 4
        LEAD = STEPS + 3
        ROWS_AT = STEPS - 2
        O_BANK, DEN_BANK, OUT_BANK, ROW_BANK, ST_BANKS = 4, 5, 6, 5, (2, 3, 7)
        c_xb = WK[:, 0:512]
        c_h = WK[:, 1536:2048].bitcast(F16).rearrange("p (c s) -> p c s", c=2)
        c_q = WK[:, 2048:3072].bitcast(F16).rearrange("p (c s) -> p c s", c=GROUPS)
        c_k = WK[:, 3072:4096].bitcast(F16).rearrange("p (c s) -> p c s", c=GROUPS)
        c_qm = WK[:, 4096:4608].bitcast(F16).rearrange("p (c s) -> p c s", c=2)
        c_va = WK[:, 4608:5632].bitcast(F16).rearrange("p (t h n) -> p t h n", t=T, h=H1)
        c_ph = WK[:, 6656:8192].bitcast(F16).rearrange("p (c s) -> p c s", c=RING)
        c_pl = WK[:, 10240:11776].bitcast(F16).rearrange("p (c s) -> p c s", c=RING)
        c_pt = WK[:, 16064:19136].rearrange("p (c s) -> p c s", c=RING)
        c_u, c_rec = WK[:, 8704:9216], WK[:, 9216:9728]
        c_at = WK[:, 11968:16064].rearrange("p (c j s) -> p c j s", c=2, j=4)
        c_nm = WK[:, 9728:10240].bitcast(F16).rearrange("p (c t n) -> p c t n", c=2, t=T)
        mask_h = WK[:, 11776:11904].bitcast(BF16).rearrange("p (c s) -> p c s", c=2)
        ident_b = WK[:, 11904:11968].bitcast(BF16)
        LOW_Q, LOW_K = col("low_q"), col("low_k")
        cq_w, ck_w, cv_w, co_w = (small_w[:, a:b] for a, b in ((384, 896), (896, 1408), (1408, 1536), (1536, CAUSAL_END)))

        def causal_pe(pe, p):
            start(pe, p)
            norm_pe(pe, norm_of[p][0], x)
            pe.wait_ge(c_setup, 2)
            pe.wait_ge(xn_ready, NB * xns[p][0] + NB)
            with pe.Fori(0, NB) as b:
                def maxima(n):
                    g, i = n // STEPS, n % STEPS
                    j, t = i // T, i % T
                    w = 128 * (t + 1)
                    if n >= 2:
                        pe.wait_ge(c_max_done, b * CN + n - 1)
                    lo = 32 * j
                    nc.tensor.matmul(P[:, n % 2, 0:w], c_q[lo:lo + 32, g, 128 * t:w], c_k[lo:lo + 32, g, 0:w],
                                     start=True, stop=False)
                    nc.tensor.matmul(P[:, n % 2, w - 128:w], ident_b, mask_h[:, 0, :], start=False, stop=True)\
                      .then_inc(c_s_ready, 1)

                def rows(g):
                    pe.wait_ge(c_max_done, b * 64 + (g + 1) * STEPS)
                    if g >= 2:
                        pe.wait_ge(c_ln_done, b * GROUPS + g - 1)
                    for t in range(T):
                        ins = nc.tensor.matmul(P[:, ROW_BANK, 128 * t:128 * t + 128], c_nm[:, g % 2, t, :],
                                               ident_h[:, :], start=True, stop=True)
                    ins.then_inc(c_rows_ready, 1)

                def values(n):
                    g, i = n // STEPS, n % STEPS
                    j, t = i // T, i % T
                    out_rows = P[32 * j:32 * j + 32, O_BANK, 128 * t:S]
                    pe.wait_ge(c_ph_done, b * 64 + n + 1)
                    if i == 0 and g >= 1:
                        pe.wait_ge(c_u_done, b * GROUPS + g)
                    nc.tensor.matmul(out_rows, c_va[:, t, 4 * g + j, :], c_ph[:, n % RING, 0:S - 128 * t],
                                     start=t == 0, stop=False)
                    if t == 0:
                        pe.wait_ge(c_pl_dve, b * 16 + n // T + 1)
                    else:
                        pe.wait_ge(c_pl_pool, b * 48 + n // T * 3 + t)
                    nc.tensor.matmul(out_rows, c_va[:, t, 4 * g + j, :], c_pl[:, n % RING, 0:S - 128 * t],
                                     start=False, stop=t == T - 1).then_inc(c_pv_done, 1)

                def denominators(g):
                    pe.wait_ge(c_u_done, b * GROUPS + g + 1)
                    if g >= 1:
                        pe.wait_ge(c_ln_done, b * GROUPS + g)
                    nc.tensor.matmul(P[:, DEN_BANK, :], masks[:, 2, :], c_u, start=True, stop=True)\
                      .then_inc(c_den_ready, 1)

                def project_out(g):
                    pe.wait_ge(c_at_done, 4 * (b * GROUPS + g + 1))
                    for r in range(16):
                        ins = nc.tensor.matmul(P[:, OUT_BANK, 128 * g:128 * g + 128],
                                               co_w[:, 128 * r:128 * r + 128], c_at[:, g % 2, :, r::16],
                                               start=r == 0, stop=r == 15)
                    ins.then_inc(c_out_done, 1)

                xb_dyn = xn[:, bass.ds(b, 1), :]

                def project(q):
                    w = (cq_w, ck_w)[q % 2][:, 128 * (q // 2):128 * (q // 2) + 128]
                    nc.tensor.matmul(P[:, q, :], w, xb_dyn, start=True, stop=True).then_inc(c_proj_ready, 1)

                for q in range(6):
                    project(q)
                pe.wait_ge(c_xb_ready, b + 1)
                for t in range(T):
                    ins = nc.tensor.matmul(P[:, 7, 128 * t:128 * t + 128], c_xb[:, 128 * t:128 * t + 128], cv_w,
                                           start=True, stop=True)
                ins.then_inc(c_v_ready, 1)
                project(6)
                pe.wait_ge(c_v_done, 2 * b + 2)
                project(7)
                for n in range(LEAD):
                    if n % STEPS == 0:
                        pe.wait_ge(c_parts_done, b * 8 + 2 * (n // STEPS) + 2)
                    maxima(n)
                rows(0)
                for g in range(GROUPS):
                    for i in range(STEPS):
                        n = g * STEPS + i
                        j, t = i // T, i % T
                        if i == 0:
                            pe.wait_ge(c_q_done, b * GROUPS + g + 1)
                        if n >= 3:
                            pe.wait_ge(c_exp_done, b * 64 + n - 2)
                        lo, w, bank = 32 * j, S - 128 * t, ST_BANKS[n % 3]
                        nc.tensor.matmul(P[:, bank, 0:w], c_k[lo:lo + 32, g, 128 * t:128 * t + 128],
                                         c_qm[lo:lo + 32, g % 2, 128 * t:S], start=True, stop=False)
                        nc.tensor.matmul(P[:, bank, 0:128], ident_b, mask_h[:, 1, :], start=False, stop=True)\
                          .then_inc(c_st_ready, 1)
                        if n >= LAG:
                            values(n - LAG)
                        if n + LEAD < CN:
                            if (n + LEAD) % STEPS == 0:
                                pe.wait_ge(c_parts_done, b * 8 + 2 * ((n + LEAD) // STEPS) + 2)
                            maxima(n + LEAD)
                        if i == ROWS_AT and g + 1 < GROUPS:
                            rows(g + 1)
                        if g >= 1 and i == 6:
                            denominators(g - 1)
                        if g >= 1 and i == 14:
                            project_out(g - 1)
                for n in range(CN - LAG, CN):
                    values(n)
                denominators(GROUPS - 1)
                project_out(GROUPS - 1)

        def causal_act(act, p):
            k, singles, boths, lns = norm_of[p]
            start(act, p)
            norm_act(act, k, True, False, lns)
            with act.Fori(0, NB) as b:
                def unnormalised(g):
                    act.wait_ge(c_pv_done, b * 64 + (g + 1) * STEPS)
                    if g >= 1:
                        act.wait_ge(c_at_done, 4 * (b * GROUPS + g))
                        act.wait_ge(c_den_ready, b * GROUPS + g)
                    nc.scalar.activation(c_u, P[:, O_BANK, :], ACT.Copy).then_inc(c_u_done, 1)

                def reciprocal(g):
                    act.wait_ge(c_den_ready, b * GROUPS + g + 1)
                    nc.scalar.activation(c_rec, P[:, DEN_BANK, :], ACT.Ln).then_inc(c_ln_done, 1)
                    act.wait_ge(c_ln_done, b * GROUPS + g + 1)
                    nc.scalar.activation(c_rec, c_rec, ACT.Exp, scale=-1.0).then_inc(c_rec_done, 1)

                for q in range(2 * GROUPS):
                    act.wait_ge(c_proj_ready, b * 8 + q + 1)
                    if q >= 2:
                        act.wait_ge(c_parts_done, b * 8 + q - 1)
                    if q % 2 == 0:
                        ins = nc.scalar.activation(c_h[:, 0, :], P[:, q, :], ACT.Copy)
                    else:
                        ins = nc.scalar.activation(c_h[:, 1, :], P[:, q, :], ACT.Identity, bias=col("one_row"))
                    ins.then_inc(c_high_done, 1)
                for g in range(GROUPS):
                    for i in range(STEPS):
                        n, w = g * STEPS + i, S - 128 * (i % T)
                        act.wait_ge(c_st_ready, b * 64 + n + 1)
                        if n >= RING:
                            act.wait_ge(c_pv_done, b * CN + n - RING + 1)
                        for dst, done in ((c_ph, c_ph_done), (c_pt, c_exp_done)):
                            nc.scalar.activation(dst[:, n % RING, 0:w], P[:, ST_BANKS[n % 3], 0:w], ACT.Exp,
                                                 scale=float(HD1) ** -0.5).then_inc(done, 1)
                        if g >= 1 and i == LAG - 1:
                            unnormalised(g - 1)
                        if g >= 1 and i == 7:
                            reciprocal(g - 1)
                unnormalised(GROUPS - 1)
                reciprocal(GROUPS - 1)

        def causal_pool(pool, own, p):
            pool.wait_ge(x_done, at[p])
            nc.gpsimd.memset(c_nm[:, :, :, :], 0.0)
            nc.gpsimd.memset(c_at[:, :, :, :], 0.0)
            own.link(nc.gpsimd.memset(c_va[:, :, :, :], 0.0))
            nc.gpsimd.memset(c_va[:, :, :, HD1:HD1 + 1], 1.0).then_inc(c_setup, 1)
            with pool.Fori(0, NB) as b:
                for n in range(GROUPS * STEPS):
                    t = n % T
                    if t == 0:
                        continue
                    w = S - 128 * t
                    pool.wait_ge(c_exp_done, b * 64 + n + 1)
                    if n >= RING:
                        pool.wait_ge(c_pv_done, b * CN + n - RING + 1)
                    nc.gpsimd.tensor_tensor(c_pl[:, n % RING, 0:w], c_pt[:, n % RING, 0:w], c_ph[:, n % RING, 0:w],
                                            ALU.subtract).then_inc(c_pl_pool, 1)

        def causal_dve(dve, own, p):
            k, singles, boths, lns = norm_of[p]
            start(dve, p)
            nc.vector.tensor_copy(ident_b, ident[:, :])
            nc.vector.tensor_copy(mask_h[:, :, :], masks[:, 0:2, :]).then_inc(c_setup, 1)
            for c in range(NB):
                dve.wait_ge(rstd_ready, NB * singles + c + 1)
                nc.vector.tensor_tensor(xn[:, c, :], P[:, c, :], rstd[:, c, :], ALU.mult).then_inc(xn_ready, 1)
            dve.wait_ge(xn_ready, NB * xns[p][0] + NB)
            dve.wait_ge(c_setup, 2)
            with dve.Fori(0, NB) as b:
                def maxima(n):
                    g, i = n // STEPS, n % STEPS
                    j, t = i // T, i % T
                    if g >= 2 and i == 0:
                        dve.wait_ge(c_rows_ready, b * GROUPS + g - 1)
                    dve.wait_ge(c_s_ready, b * 64 + n + 1)
                    nc.vector.tensor_reduce(out=c_nm[:, g % 2, t, 32 * j + 24:32 * j + 25],
                                            in_=P[:, n % 2, 0:128 * (t + 1)], op=ALU.max, axis=AX.X, negate=True)\
                      .then_inc(c_max_done, 1)

                def low_part(n):
                    dve.wait_ge(c_exp_done, b * 64 + n + 1)
                    if n >= RING:
                        dve.wait_ge(c_pv_done, b * CN + n - RING + 1)
                    nc.vector.tensor_tensor(c_pl[:, n % RING, :], c_pt[:, n % RING, :], c_ph[:, n % RING, :],
                                            ALU.subtract).then_inc(c_pl_dve, 1)

                def add_rows(g):
                    dve.wait_ge(c_rows_ready, b * GROUPS + g + 1)
                    nc.vector.tensor_tensor(c_qm[:, g % 2, :], c_q[:, g, :], P[:, ROW_BANK, :], ALU.add)\
                      .then_inc(c_q_done, 1)

                def normalise(g, j):
                    if j == 0:
                        dve.wait_ge(c_rec_done, b * GROUPS + g + 1)
                        if g >= 2:
                            dve.wait_ge(c_out_done, b * GROUPS + g - 1)
                    lo = 32 * j
                    nc.vector.tensor_tensor(c_at[lo:lo + 32, g % 2, j, :], c_u[lo:lo + 32], c_rec[lo:lo + 32],
                                            ALU.mult).then_inc(c_at_done, 1)

                def parts(q):
                    dve.wait_ge(c_high_done, b * 8 + q + 1)
                    nc.vector.scalar_tensor_tensor(out=(c_q, c_k)[q % 2][:, q // 2, :], in0=c_h[:, q % 2, :],
                                                   scalar=(LOW_Q, LOW_K)[q % 2], in1=P[:, q, :],
                                                   op0=ALU.mult, op1=ALU.add).then_inc(c_parts_done, 1)

                nc.vector.tensor_copy(c_xb, chunk(xn, b)).then_inc(c_xb_ready, 1)
                for q in range(6):
                    parts(q)
                dve.wait_ge(c_v_ready, b + 1)
                v_psum = P[:, 7, :].rearrange("p (t h n) -> p t h n", t=T, h=H1)
                nc.vector.tensor_copy(c_va[:, :, :, 0:HD1], v_psum).then_inc(c_v_done, 1)
                dve.wait_ge(c_v_done, 2 * b + 1)
                nc.vector.tensor_tensor(c_va[:, :, :, 16:16 + HD1], v_psum, c_va[:, :, :, 0:HD1], ALU.subtract)\
                  .then_inc(c_v_done, 1)
                for q in range(6, 8):
                    parts(q)
                for n in range(LEAD):
                    maxima(n)
                add_rows(0)
                for g in range(GROUPS):
                    for i in range(STEPS):
                        if g * STEPS + i + LEAD < CN:
                            maxima(g * STEPS + i + LEAD)
                        if i == ROWS_AT and g + 1 < GROUPS:
                            add_rows(g + 1)
                        if i % T == 1:
                            low_part(g * STEPS + i - 1)
                        if g >= 1 and 9 <= i < 13:
                            normalise(g - 1, i - 9)
                for j in range(4):
                    normalise(GROUPS - 1, j)
                dve.wait_ge(c_out_done, b * GROUPS + GROUPS)
                xb = chunk(x, b)
                nc.vector.scalar_tensor_tensor(out=xb, in0=P[:, OUT_BANK, :], scalar=col("co"), in1=xb,
                                               op0=ALU.add, op1=ALU.add).then_inc(x_done, 1)

        block = ctx.enter_context(nc.Block())

        @block.sync
        def _(sp):
            for dst, src in ((x[:, :, :], x_t), (cols[:, :], cols_d), (ident[:, :], ident_d),
                             (masks[:, :, :], mask_d)):
                sp.dma_start(dst, src).then_inc(x_loaded, 16)
            sp.dma_start(wm[:, :], wm_d).then_inc(w_loaded[0], 16)
            if swiglu:
                for dst, src in ((raw[:, 0:E * DE], f0_up_d.rearrange("p e n -> p (e n)")),
                                 (raw[:, E * DE:2 * E * DE], f0_gate_d.rearrange("p e n -> p (e n)")),
                                 (raw[:, 2 * E * DE:F0_COLS], f0_down_d.rearrange("p e j d -> p (e j d)")),
                                 (f0_router[:, :], f0_router_d)):
                    sp.dma_start(dst, src).then_inc(w_loaded[1], 16)
            sp.dma_start(small_w[:, 0:384], phase_w_d).then_inc(w_loaded[4], 16)
            sp.dma_start(small_w[:, 384:CAUSAL_END], causal_w_d).then_inc(w_loaded[6], 16)
            if 2 in phases:
                if swiglu:
                    sp.wait_ge(raw_split, 1)
                for dst, src in ((qkv_w, qkv_d), (wo_w, wo_d.rearrange("p a d -> p (a d)"))):
                    sp.dma_start(dst, src).then_inc(w_loaded[2], 16)
            if relu:
                if swiglu:
                    sp.wait_ge(raw_split, 1)
                if 2 in phases:
                    sp.wait_ge(x_done, at[2] + NB)
                for dst, src in ((raw[:, 0:E * FE], f1_up_d.rearrange("p e n -> p (e n)")),
                                 (raw[:, E * FE:F1_COLS], f1_down_d.rearrange("p e j d -> p (e j d)")),
                                 (f1_router[:, :], f1_router_d), (f1_b2[:, :], f1_b2_d),
                                 (f1_rb[:, :], f1_rb_d[0, :].partition_broadcast(128))):
                    sp.dma_start(dst, src).then_inc(w_loaded[5], 16)
            sp.wait_ge(x_done, NB * len(phases) + 1)
            sp.dma_start(out, x[:, :, :]).then_inc(stored, 16)
            sp.wait_ge(stored, 16)

        @block.tensor
        def _(pe):
            for p in phases:
                if p == 0:
                    pe.wait_ge(w_loaded[0], 16)
                    scan_pe(pe)
                if p in (1, 3):
                    pe.wait_ge(w_loaded[1], 64)
                    swiglu_pe(pe, p)
                if p == 2:
                    pe.wait_ge(w_loaded[2], 32)
                    heads_pe(pe, p)
                if p == 4:
                    pe.wait_ge(w_loaded[4], 16)
                    phase_pe(pe, p)
                if p == 6:
                    pe.wait_ge(w_loaded[6], 16)
                    causal_pe(pe, p)
                if p in (5, 7):
                    pe.wait_ge(w_loaded[5], 80)
                    relu_pe(pe, p)

        @block.scalar
        def _(act):
            nc.scalar.preload_act_table_set(EXP_LN)
            for p in phases:
                if p:
                    nc.scalar.preload_act_table_set(EXP_LN)
                if p == 0:
                    scan_act(act)
                if p in (1, 3):
                    swiglu_act(act, p)
                if p == 2:
                    heads_act(act, p)
                if p == 4:
                    phase_act(act, p)
                if p == 6:
                    causal_act(act, p)
                if p in (5, 7):
                    relu_act(act, p)

        @block.gpsimd
        def _(pool):
            own = Own(pool, pool_own)
            nc.gpsimd.memset(ones[:, :], 1.0)
            for e in range(E):
                ins = nc.gpsimd.memset(rev[:, :, e:e + 1], float(E - e))
            ins.then_inc(x_done, 1)
            if swiglu:
                pool.wait_ge(w_loaded[1], 64)
                split_pool(pool, own, 0, F0_COLS, 1)
            for p in phases:
                if p == 0:
                    scan_pool(pool)
                if p in (1, 3):
                    swiglu_pool(pool, p)
                if p == 2:
                    heads_pool(pool, own, p)
                if p == 6:
                    causal_pool(pool, own, p)
                if p == (4 if 4 in phases and relu else relu[0] if relu else None):
                    pool.wait_ge(x_done, at[p])
                    pool.wait_ge(w_loaded[5], 80)
                    split_pool(pool, own, 0, F1_COLS, 1)
        @block.vector
        def _(dve):
            nc.vector.memset(mean_w[:, :], 1.0 / D)
            for k, v in ((K_LN, LN_EPS), (K_BOTH, BOTH_EPS), (K_ONE, 1.0), (K_TANH, -CENTER / HALF),
                         (K_HALFPI, math.pi / 2)):
                last = nc.vector.memset(kc[:, k:k + 1], v)
            last.then_inc(consts_set, 1)
            dve.wait_ge(x_loaded, 64)
            dve.wait_ge(consts_set, 1)
            nc.vector.tensor_tensor(center_w[:, :], ident[:, :], mean_w[:, :], ALU.subtract)
            nc.vector.tensor_copy(ident_h[:, :], ident[:, :]).then_inc(consts_set, 1)
            own = Own(dve, dve_own)
            for p in phases:
                if p == 0:
                    scan_dve(dve, own)
                if p in (1, 3):
                    swiglu_dve(dve, own, p)
                if p == 2:
                    heads_dve(dve, own, p)
                if p == 4:
                    phase_dve(dve, own, p)
                if p == 6:
                    causal_dve(dve, own, p)
                if p in (5, 7):
                    if p == relu[0]:
                        dve.wait_ge(w_loaded[5], 80)
                        own.link(nc.vector.tensor_scalar(b2_s[:, :], f1_b2[:, :], W_SCALE, None, ALU.mult))
                        own.link(nc.vector.tensor_copy(b2_parts[:, 0, :], b2_s[:, :]))
                        own.link(nc.vector.tensor_tensor(b2_parts[:, 1, :], b2_s[:, :], b2_parts[:, 0, :], ALU.subtract))
                    relu_dve(dve, own, p)


def layout(x, v):
    f32 = np.float32

    def pair_cols(a):
        return np.repeat(a.reshape(PAIRS, 2), HD0, axis=1).T

    def rows_at(lo, hi):
        return ((np.arange(128) % 32 >= lo) & (np.arange(128) % 32 < hi)).astype(f32)

    parts = {
        "A_log": v["L0_attn_a_A_log"], "b_delta": v["L0_attn_a_b_delta"],
        "D_skip": v["L0_attn_a_D_skip"], "norm_w": v["L0_attn_a_norm_weight"],
        "rms_w": v["L0_ffn_rms_w"], "adaptive": pair_cols(v["L0_attn_b_adaptive_scale"]),
        "bq": v["L0_attn_b_bq"].reshape(PAIRS, 128).T, "bk": v["L0_attn_b_bk"].reshape(PAIRS, 128).T,
        "bv": v["L0_attn_b_bv"].reshape(PAIRS, 128).T,
        "bo": v["L0_attn_b_bo"], "gamma": v["L0_attn_b_gamma"], "beta": v["L0_attn_b_beta"],
        "pq": v["L1_attn_a_bq"], "pk": v["L1_attn_a_bk"], "pv": v["L1_attn_a_bv"],
        "phase": v["L1_attn_a_phase_bias"], "inv_wl": inverse_wavelengths(),
        "co": v["L1_attn_b_bo"], "one_row": rows_at(24, 25),
        "low_q": -rows_at(8, 16), "low_k": rows_at(24, 25) - rows_at(16, 24),
        "b1": v["L1_ffn_b1"].reshape(E * FC, 128).T,
    }
    cols = np.concatenate([parts[n].reshape(128, -1) for n in COLS], axis=1)

    masks = np.zeros((128, 3, 128), f32)
    later = np.triu(np.ones((128, 128), bool), 1)
    masks[:, 0][later] = -1e30
    masks[:, 1][later.T] = -1e30
    rows = np.arange(128)
    masks[:, 2] = rows[:, None] == 32 * (rows[None, :] // 32) + HD1

    down0 = np.zeros((E, DEC * 128, D), f32)
    down0[:, :DE] = v["L0_ffn_W3"].transpose(0, 2, 1)

    def spread(w):
        out = np.zeros((128, GROUPS, 4, 32), f32)
        for n in range(3):
            out[..., n * HD1:n * HD1 + HD1] = w.reshape(128, GROUPS, 4, HD1)
        return out.reshape(128, GROUPS * 128)

    co = np.zeros((4, 32, 16, D), f32)
    for lo in (0, 16):
        co[:, lo:lo + HD1] = v["L1_attn_b_Wo"].reshape(16, HD1, D).transpose(1, 0, 2)
    return {
        "x_t": x.reshape(NB * S, D).T.reshape(D, NB, S),
        "cols": cols, "ident": np.eye(128, dtype=f32), "masks": masks,
        "wm": np.concatenate([v["L0_attn_a_W_delta"], v["L0_attn_a_W_B"], v["L0_attn_a_W_C"]], axis=1),
        "f0_up": v["L0_ffn_W1"].transpose(2, 0, 1), "f0_gate": v["L0_ffn_W2"].transpose(2, 0, 1),
        "f0_down": down0.reshape(E, DEC, 128, D).transpose(2, 0, 1, 3),
        "f0_router": v["L0_ffn_gate_w"].T,
        "qkv": np.concatenate([v["L0_attn_b_Wq"].T, v["L0_attn_b_Wk"].T, v["L0_attn_b_Wv"].T], axis=1),
        "wo": v["L0_attn_b_Wo"].T.reshape(PAIRS, 128, D).transpose(1, 0, 2),
        "phase_w": np.concatenate([v["L1_attn_a_Wq"].T, v["L1_attn_a_Wk"].T, v["L1_attn_a_Wv"].T], axis=1),
        "causal_w": np.concatenate([spread(v["L1_attn_b_Wq"]), spread(v["L1_attn_b_Wk"]),
                                    v["L1_attn_b_Wv"],
                                    co.reshape(128, 16 * D)], axis=1),
        "f1_up": v["L1_ffn_w1"].transpose(1, 0, 2),
        "f1_down": v["L1_ffn_w2"].reshape(E, FC, 128, D).transpose(2, 0, 1, 3),
        "f1_router": v["L1_ffn_gate_w"], "f1_rb": v["L1_ffn_gate_b"].reshape(1, E),
        "f1_b2": v["L1_ffn_b2"],
    }


def inverse_wavelengths():
    lengths = np.arange(1, D + 1, dtype=np.float32) * np.float32(2.0 * math.pi / D)
    return np.float32(1.0) / (lengths + np.float32(1e-8))


def kernel(**inputs):
    import concourse.bacc as bacc
    from concourse.bass_utils import run_bass_kernel_spmd

    v = {name: np.asarray(a) for name, a in inputs.items()}
    arrays = {f"in_{n}": np.ascontiguousarray(a) for n, a in layout(v["L0_attn_a_x"], v).items()}
    nc = bacc.Bacc("TRN2", target_bir_lowering=False, num_devices=1)
    args = [nc.dram_tensor(n, a.shape, mybir.dt.from_np(a.dtype), kind="ExternalInput").ap()
            for n, a in arrays.items()]
    out = nc.dram_tensor("x_out", (D, NB, S), F32, kind="ExternalOutput").ap()
    hybrid(nc, *args, out)
    r = run_bass_kernel_spmd(nc, [arrays], core_ids=[0])
    got = r.results[0]["x_out"]
    return np.ascontiguousarray(got.reshape(D, NB * S).T.reshape(NB, S, D))
```

```python
import math

import numpy as np

import concourse.bass as bass
from concourse import mybir

F32 = mybir.dt.float32
BF16 = mybir.dt.bfloat16
F16 = mybir.dt.float16
ACT = mybir.ActivationFunctionType
ALU = mybir.AluOpType
AX = mybir.AxisListType

D = 128
S = 512
NB = 4
T = S // 128
NT = NB * T
E = 8
NS = 16
DE = 352
DEC = 3
FE = 512
FC = FE // 128
H0, HD0 = 16, 64
PAIRS = H0 // 2
H1, HD1 = 16, 8
GROUPS = H1 // 4
CAUSAL_END = 3 * D + 2 * GROUPS * 128 + D + 16 * D
EXP_LN = "natural_log_exp_and_others"
LN_EPS, RMS_EPS = 1e-5, 1e-6
BOTH_SCALE, BOTH_EPS = 1.0 + RMS_EPS, LN_EPS * RMS_EPS
DT_MIN, DT_MAX = 1e-4, 10.0
CENTER, HALF = (DT_MAX + DT_MIN) / 2.0, (DT_MAX - DT_MIN) / 2.0
MAGIC = 1.5 * 2.0 ** 23
TWO_PI_HI = 6.28125
TWO_PI_LO = 2.0 * math.pi - TWO_PI_HI
PI_F = float(np.nextafter(np.float32(math.pi), np.float32(0)))

W_SCALE, Y_SCALE, H_SCALE = 2.0 ** 10, 2.0 ** 6, 2.0 ** 6
UP_BACK, DOWN_BACK = 1.0 / (W_SCALE * Y_SCALE), 1.0 / (W_SCALE * H_SCALE)
F0_COLS = 2 * E * DE + E * DEC * D
F1_COLS = E * FE + E * FC * D

COLS = {}
for _name, _n in (("A_log", NS), ("b_delta", 1), ("D_skip", 1), ("norm_w", 1), ("rms_w", 1),
                  ("adaptive", PAIRS), ("bq", PAIRS), ("bk", PAIRS), ("bv", PAIRS), ("bo", 1), ("gamma", 1),
                  ("beta", 1), ("pq", 1), ("pk", 1), ("pv", 1), ("phase", 1), ("inv_wl", 1),
                  ("co", 1), ("one_row", 1), ("low_q", 1), ("low_k", 1), ("b1", E * FC)):
    COLS[_name] = (sum(n for _, n in COLS.values()), _n)
NCOLS = sum(n for _, n in COLS.values())


def hybrid(nc, x_t, cols_d, ident_d, mask_d, wm_d, f0_up_d, f0_gate_d, f0_down_d, f0_router_d,
           qkv_d, wo_d, phase_w_d, causal_w_d, f1_up_d, f1_down_d, f1_router_d, f1_rb_d,
           f1_b2_d, out, phases=range(8)):
    from contextlib import ExitStack
    ctx = ExitStack()
    with ctx:
        def sb(name, shape, dt=F32):
            return ctx.enter_context(nc.sbuf_tensor(name, shape, dt))

        def sem(name):
            return ctx.enter_context(nc.semaphore(name))

        x = sb("x", [D, NB, S])
        sq = sb("sq", [D, NB, S])
        xn = sb("xn", [D, NB, S])
        y = sb("y", [D, NB, S])
        rstd, rstd2 = xn, y
        cols = sb("cols", [D, NCOLS])
        ident = sb("ident_sb", [128, 128])
        masks = sb("masks", [128, 3, 128])
        mean_w = sb("mean_w", [128, 128])
        center_w = sb("center_w", [128, 128])
        ones = sb("ones", [128, 128])
        kc = sb("kc", [128, 8])
        wm = sb("wm", [D, D + 2 * NS])
        f0_router = sb("f0_router", [D, E])
        f1_router = sb("f1_router", [D, E])
        f1_rb = sb("f1_rb", [128, E])
        f1_b2 = sb("f1_b2", [2 * E, D])
        hot = sb("hot", [128, 6, NT, E])
        w_rt = sb("w_rt", [128, NT, E])
        w16 = sb("w16", [128, NT, 2 * E], F16)
        pick_both = sb("pick_both", [2 * E, E], F16)
        pick_row = sb("pick_row", [128, 2 * NS], F16)
        rev = sb("rev", [128, NT, E])
        ident_h = sb("ident_h", [128, 128], F16)
        b2_s = sb("b2_s", [2 * E, D])
        raw = sb("raw", [128, F0_COLS])
        w_h = sb("w_h", [128, F0_COLS], F16)
        w_l = sb("w_l", [128, F0_COLS], F16)
        small_w = sb("small_w", [128, CAUSAL_END])
        WK = sb("WK", [128, 19480])
        y_h = sq[:, :, :].bitcast(F16)[:, :, 0:S]
        y_l = sq[:, :, :].bitcast(F16)[:, :, S:2 * S]
        P = ctx.enter_context(nc.psum_tensor("P", [128, 8, S], F32))

        def col(name, i=0, lo=0, hi=128):
            return cols[lo:hi, COLS[name][0] + i:COLS[name][0] + i + 1]

        K_LN, K_BOTH, K_ONE, K_TANH, K_HALFPI = range(5)

        def const(k, lo=0, hi=128):
            return kc[lo:hi, k:k + 1]

        x_loaded = sem("x_loaded")
        w_loaded = [sem(f"w_loaded{p}") for p in range(8)]
        consts_set = sem("consts_set")
        x_done = sem("x_done")
        stored = sem("stored")
        dve_own = sem("dve_own")
        act_own = sem("act_own")
        pool_own = sem("pool_own")
        xc_ready = sem("xc_ready")
        sq_ready = sem("sq_ready")
        var_ready = sem("var_ready")
        ln_ready = sem("ln_ready")
        rstd_ready = sem("rstd_ready")
        rstd2_ready = sem("rstd2_ready")
        xn_ready = sem("xn_ready")
        y_ready = sem("y_ready")
        resid_ready = sem("resid_ready")

        class Own:

            def __init__(self, eng, s):
                self.eng, self.sem, self.n, self.base = eng, s, 0, 0

            def link(self, ins):
                self.n += 1
                ins.then_inc(self.sem, 1)
                self.eng.wait_ge(self.sem, self.base + self.n)

            def loop(self, i, per):
                self.saved, self.per = self.n, per
                self.base, self.n = self.n + i * per, 0

            def end(self, times):
                assert self.n == self.per, (self.n, self.per)
                self.base, self.n = 0, self.saved + times * self.per

        def norm_pe(pe, k, src, p=None):
            for c in range(NB):
                if p is not None and p != phases[0]:
                    pe.wait_ge(x_done, at[p] - NB + c + 1)
                nc.tensor.matmul(P[:, c, :], center_w[:, :], src[:, c, :], start=True, stop=True)\
                  .then_inc(xc_ready, 1)
            for c in range(NB):
                pe.wait_ge(sq_ready, NB * k + c + 1)
                nc.tensor.matmul(P[:, 4 + c, :], mean_w[:, :], sq[:, c, :], start=True, stop=True)\
                  .then_inc(var_ready, 1)

        def norm_act(act, k, single, both, k2):
            for c in range(NB):
                act.wait_ge(xc_ready, NB * k + c + 1)
                nc.scalar.activation(sq[:, c, :], P[:, c, :], ACT.Square).then_inc(sq_ready, 1)
            jobs = [(c,) + kind for want, kind in ((both, (rstd2, rstd2_ready, BOTH_SCALE, K_BOTH)),
                                                   (single, (rstd, rstd_ready, 1.0, K_LN))) if want
                    for c in range(NB)]
            for n, (c, dst, done, scale, eps) in enumerate(jobs + [jobs[-1]]):
                if n < len(jobs):
                    act.wait_ge(var_ready, NB * k + c + 1)
                    nc.scalar.activation(dst[:, c, :], P[:, 4 + c, :], ACT.Ln, scale=scale,
                                         bias=const(eps)).then_inc(ln_ready, 1)
                if n >= 1:
                    act.wait_ge(ln_ready, NB * k2 + n)
                    c, dst, done = jobs[n - 1][:3]
                    nc.scalar.activation(dst[:, c, :], dst[:, c, :], ACT.Exp, scale=-0.5).then_inc(done, 1)

        NORMS = []
        for p in phases:
            NORMS.append((p, p != 0, p in (0, 1, 3)))
            if p == 2:
                NORMS.append(("post", True, False))
        norm_of = {}
        singles = boths = lns = 0
        for k, (p, s1, b2) in enumerate(NORMS):
            norm_of[p] = (k, singles, boths, lns)
            singles += s1
            boths += b2
            lns += s1 + b2
        xns = {}
        nx = ny = nr = 0
        for p in phases:
            xns[p] = (nx, ny, nr)
            nx += p not in (0,)
            ny += p in (0, 1, 3)
            nr += p in (1, 3)
        at = {p: NB * i + 1 for i, p in enumerate(phases)}

        def start(eng, p, by_chunk=False):
            if not by_chunk or p == phases[0]:
                eng.wait_ge(x_done, at[p])
            if p == phases[0]:
                eng.wait_ge(x_loaded, 16 * 4)
                eng.wait_ge(consts_set, 2)

        m_z_ready = sem("m_z_ready")
        m_abs_ready = sem("m_abs_ready")
        m_exp_ready = sem("m_exp_ready")
        m_pos_ready = sem("m_pos_ready")
        m_log_ready = sem("m_log_ready")
        m_sp_ready = sem("m_sp_ready")
        m_soft_ready = sem("m_soft_ready")
        m_tanh_ready = sem("m_tanh_ready")
        m_delta_ready = sem("m_delta_ready")
        m_root_ready = sem("m_root_ready")
        m_bc_ready = sem("m_bc_ready")
        m_rows_ready = sem("m_rows_ready")
        m_high_done = sem("m_high_done")
        m_low_done = sem("m_low_done")
        m_u_ready = sem("m_u_ready")
        m_r_ready = sem("m_r_ready")
        m_a_ready = sem("m_a_ready")
        m_bx_ready = sem("m_bx_ready")
        m_h_ready = sem("m_h_ready")
        m_g_ready = sem("m_g_ready")
        m_y_ready = sem("m_y_ready")

        C_BANKS = (2, 3, 5, 6)
        delta = WK[:, 0:2048].rearrange("p (c s) -> p c s", c=NB)
        wsq = WK[:, 2048:4096].rearrange("p (c s) -> p c s", c=NB)
        m_z = WK[:, 4096:6144].rearrange("p (c s) -> p c s", c=NB)
        m_t = WK[:, 6144:8192].rearrange("p (c s) -> p c s", c=NB)
        m_half = WK[:, 8192:8208]
        mb = 8208
        m_r = WK[:, mb:mb + 2048].rearrange("p (c s) -> p c s", c=4)
        m_a = WK[:, mb + 2048:mb + 4096].rearrange("p (c s) -> p c s", c=4)
        m_u = WK[:, mb + 4096:mb + 5120].rearrange("p (c s) -> p c s", c=2)
        m_bx = WK[:, mb + 5120:mb + 6144].rearrange("p (c s) -> p c s", c=2)
        m_h = WK[:, mb + 6144:mb + 7168].rearrange("p (c s) -> p c s", c=2)
        m_g = WK[:, mb + 7168:mb + 9216].rearrange("p (c s) -> p c s", c=4)
        m_l = WK[:, mb + 9216:mb + 10240].rearrange("p (c s) -> p c s", c=2)
        m_bc = WK[:, mb + 10240:mb + 11264].bitcast(F16).rearrange("p (c s) -> p c s", c=NB)

        def scan_pe(pe):
            start(pe, 0)
            norm_pe(pe, norm_of[0][0], x)
            for c in range(NB):
                pe.wait_ge(y_ready, c + 1)
                nc.tensor.matmul(P[:, c, :], wm[:, 0:D], y[:, c, :], start=True, stop=True)\
                  .then_inc(m_z_ready, 1)
            for c in range(NB):
                nc.tensor.matmul(P[0:2 * NS, 4 + c, :], wm[:, D:D + 2 * NS], y[:, c, :], start=True, stop=True)\
                  .then_inc(m_rows_ready, 1)
            pe.wait_ge(m_low_done, NB)
            pe.wait_ge(m_u_ready, 1)
            with pe.Fori(0, NB) as b:
                for n in range(NS + 3):
                    if n < NS:
                        if n >= 2:
                            pe.wait_ge(m_u_ready, b * NS + n)
                        rows = m_bc[:, bass.ds(b, 1), :]
                        nc.tensor.matmul(P[:, n % 2, :], pick_row[:, n:n + 1].broadcast_to([128, 128]), rows,
                                         start=True, stop=True)
                        if n >= 4:
                            pe.wait_ge(m_g_ready, b * NS + n - 3)
                        nc.tensor.matmul(P[:, C_BANKS[n % 4], :], pick_row[:, NS + n:NS + n + 1].broadcast_to([128, 128]),
                                         rows, start=True, stop=True).then_inc(m_bc_ready, 1)
                    if n >= 3:
                        pe.wait_ge(m_g_ready, b * NS + n - 2)
                        if n == 3:
                            pe.wait_ge(x_done, b + 1)
                        nc.tensor.matmul(P[:, 4, :], ident[:, :], m_g[:, (n - 3) % 4, :],
                                         start=(n == 3), stop=(n == NS + 2)).then_inc(m_y_ready, 1)

        def scan_act(act):
            k, singles, boths, lns = norm_of[0]
            start(act, 0)
            own = Own(act, act_own)
            own.link(nc.scalar.activation(m_half, cols[:, 0:NS], ACT.Exp))
            own.link(nc.scalar.activation(m_half, m_half, ACT.Copy, scale=0.5))
            norm_act(act, k, False, True, lns)
            for c in range(NB):
                act.wait_ge(m_z_ready, c + 1)
                nc.scalar.activation(m_t[:, c, :], P[:, c, :], ACT.Abs, bias=col("b_delta")).then_inc(m_abs_ready, 1)
            for c in range(NB):
                act.wait_ge(m_abs_ready, c + 1)
                nc.scalar.activation(m_t[:, c, :], m_t[:, c, :], ACT.Exp, scale=-1.0).then_inc(m_exp_ready, 1)
            for c in range(NB):
                act.wait_ge(m_exp_ready, c + 1)
                nc.scalar.activation(m_t[:, c, :], m_t[:, c, :], ACT.Ln, bias=const(K_ONE)).then_inc(m_sp_ready, 1)
            for c in range(NB):
                act.wait_ge(m_soft_ready, c + 1)
                nc.scalar.activation(m_t[:, c, :], m_z[:, c, :], ACT.Tanh, scale=1.0 / HALF, bias=const(K_TANH))\
                  .then_inc(m_tanh_ready, 1)
            nc.scalar.preload_act_table_set(EXP_LN)
            for c in range(NB + 1):
                if c < NB:
                    act.wait_ge(m_delta_ready, c + 1)
                    nc.scalar.activation(m_z[:, c, :], delta[:, c, :], ACT.Ln).then_inc(m_log_ready, 1)
                if c >= 1:
                    act.wait_ge(m_log_ready, c)
                    nc.scalar.activation(m_z[:, c - 1, :], m_z[:, c - 1, :], ACT.Exp, scale=0.5).then_inc(m_root_ready, 1)
            with act.Fori(0, NB) as b:
                for n in range(0, NS, 2):
                    base = b * NS + n
                    for q in range(2):
                        nc.scalar.activation(m_l[:, q, :], delta[:, bass.ds(b, 1), :], ACT.Ln,
                                             scale=m_half[:, n + q:n + q + 1], bias=const(K_ONE))\
                          .then_inc(m_sp_ready, 1)
                    for q in range(2):
                        if n >= 4:
                            act.wait_ge(m_bx_ready, base + q - 3)
                        act.wait_ge(m_sp_ready, NB + base + q + 1)
                        nc.scalar.activation(m_r[:, (n + q) % 4, :], m_l[:, q, :], ACT.Exp,
                                             scale=-1.0).then_inc(m_r_ready, 1)
                    for q in range(2):
                        if n >= 4:
                            act.wait_ge(m_h_ready, base + q - 3)
                        act.wait_ge(m_r_ready, base + q + 1)
                        nc.scalar.activation(m_a[:, (n + q) % 4, :], m_r[:, (n + q) % 4, :], ACT.Copy,
                                             scale=2.0, bias=-1.0).then_inc(m_a_ready, 1)
                act.wait_ge(m_h_ready, b * NS + NS)

        def scan_pool(pool):
            with pool.Fori(0, NB) as b:
                for n in range(NS):
                    pool.wait_ge(m_r_ready, b * NS + n + 1)
                    pool.wait_ge(m_u_ready, b * NS + n + 2)
                    if n >= 2:
                        pool.wait_ge(m_h_ready, b * NS + n - 1)
                    nc.gpsimd.tensor_tensor(m_bx[:, n % 2, :], m_u[:, n % 2, :], m_r[:, n % 4, :],
                                            ALU.mult).then_inc(m_bx_ready, 1)

        def scan_dve(dve, own):
            k = norm_of[0][0]
            start(dve, 0)
            for c in range(NB):
                dve.wait_ge(rstd2_ready, c + 1)
                nc.vector.scalar_tensor_tensor(out=y[:, c, :], in0=P[:, c, :], scalar=col("norm_w"),
                                               in1=rstd2[:, c, :], op0=ALU.mult, op1=ALU.mult)\
                  .then_inc(y_ready, 1)
            for c in range(NB):
                dve.wait_ge(m_abs_ready, c + 1)
                nc.vector.tensor_scalar(m_z[:, c, :], P[:, c, :], col("b_delta"), 0.0, ALU.add, ALU.max)\
                  .then_inc(m_pos_ready, 1)
            for c in range(NB):
                dve.wait_ge(m_rows_ready, c + 1)
                nc.vector.tensor_copy(m_bc[0:2 * NS, c, :], P[0:2 * NS, 4 + c, :]).then_inc(m_high_done, 1)
            for c in range(NB):
                dve.wait_ge(m_high_done, c + 1)
                nc.vector.tensor_tensor(m_bc[2 * NS:4 * NS, c, :], P[0:2 * NS, 4 + c, :], m_bc[0:2 * NS, c, :],
                                        ALU.subtract).then_inc(m_low_done, 1)
            for c in range(NB):
                dve.wait_ge(m_pos_ready, c + 1)
                dve.wait_ge(m_sp_ready, c + 1)
                nc.vector.tensor_tensor(m_z[:, c, :], m_z[:, c, :], m_t[:, c, :], ALU.add).then_inc(m_soft_ready, 1)
            for c in range(NB):
                dve.wait_ge(m_tanh_ready, c + 1)
                nc.vector.tensor_scalar(delta[:, c, :], m_t[:, c, :], HALF, CENTER, ALU.mult, ALU.add)\
                  .then_inc(m_delta_ready, 1)
            dve.wait_ge(y_ready, NB)
            for c in range(NB):
                dve.wait_ge(m_root_ready, c + 1)
                ins = nc.vector.tensor_tensor(wsq[:, c, :], m_z[:, c, :], y[:, c, :], ALU.mult)
            ins.then_inc(m_u_ready, 1)
            dve.wait_ge(m_u_ready, 1)
            with dve.Fori(0, NB) as b:
                for n in range(NS + 2):
                    if n < NS:
                        dve.wait_ge(m_bc_ready, b * NS + n + 1)
                        if n >= 2:
                            dve.wait_ge(m_bx_ready, b * NS + n - 1)
                        nc.vector.tensor_tensor(m_u[:, n % 2, :], wsq[:, bass.ds(b, 1), :].rearrange("p o s -> p (o s)"),
                                                P[:, n % 2, :], ALU.mult).then_inc(m_u_ready, 1)
                    if 1 <= n <= NS:
                        m = n - 1
                        dve.wait_ge(m_bx_ready, b * NS + m + 1)
                        dve.wait_ge(m_a_ready, b * NS + m + 1)
                        if m >= 2:
                            dve.wait_ge(m_g_ready, b * NS + m - 1)
                        nc.vector.tensor_tensor_scan(out=m_h[:, m % 2, :], data0=m_a[:, m % 4, :],
                                                     data1=m_bx[:, m % 2, :], initial=0.0,
                                                     op0=ALU.mult, op1=ALU.add).then_inc(m_h_ready, 1)
                    if n >= 2:
                        m = n - 2
                        dve.wait_ge(m_h_ready, b * NS + m + 1)
                        if m >= 4:
                            dve.wait_ge(m_y_ready, b * NS + m - 3)
                        nc.vector.tensor_tensor(m_g[:, m % 4, :], m_h[:, m % 2, :], P[:, C_BANKS[m % 4], :],
                                                ALU.mult).then_inc(m_g_ready, 1)
                own.loop(b, 1)
                dve.wait_ge(m_y_ready, b * NS + NS)
                own.link(nc.vector.scalar_tensor_tensor(
                    out=m_h[:, 0, :], in0=y[:, bass.ds(b, 1), :].rearrange("p o s -> p (o s)"),
                    scalar=col("D_skip"), in1=P[:, 4, :], op0=ALU.mult, op1=ALU.add))
                xb = x[:, bass.ds(b, 1), :].rearrange("p o s -> p (o s)")
                nc.vector.tensor_tensor(xb, xb, m_h[:, 0, :], ALU.add).then_inc(x_done, 1)
                own.end(NB)

        raw_split = sem("raw_split")
        e_yh_ready = sem("e_yh_ready")
        e_yl_ready = sem("e_yl_ready")
        e_logits_ready = sem("e_logits_ready")
        e_gap_ready = sem("e_gap_ready")
        e_exp_ready = sem("e_exp_ready")
        e_w_ready = sem("e_w_ready")
        e_wt_psum = sem("e_wt_psum")
        e_wth_ready = sem("e_wth_ready")
        e_wb_ready = sem("e_wb_ready")
        e_yw_ready = sem("e_yw_ready")
        e_ywh_ready = sem("e_ywh_ready")
        e_ywl_ready = sem("e_ywl_ready")
        e_up_ready = sem("e_up_ready")
        e_gate_ready = sem("e_gate_ready")
        e_act_done = sem("e_act_done")
        e_h_ready = sem("e_h_ready")
        e_hh_ready = sem("e_hh_ready")
        e_hl_ready = sem("e_hl_ready")
        e_down_done = sem("e_down_done")

        layers = [p for p in phases if p in (1, 3, 5, 7)]
        splits = [p for p in phases if p in (1, 2, 3, 5, 7)]
        swiglu = [p for p in layers if p < 5]
        relu = [p for p in layers if p >= 5]


        def halves(at, n, c):
            return WK[:, at:at + n * S // 2].bitcast(F16).rearrange("p (c s) -> p c s", c=c)

        HRING, AHEAD, E_LAG, R_LAG = 6, 4, 5, 5
        R_SPREAD, E_UP = (4, 5, 7), (0, 1, 7)
        e_act = WK[:, 0:2048].rearrange("p (c s) -> p c s", c=AHEAD)
        e_hid = WK[:, 2048:5120].rearrange("p (c s) -> p c s", c=HRING)
        e_yw = WK[:, 5120:6144].rearrange("p (c s) -> p c s", c=2)
        e_ywh, e_ywl = halves(7168, 2, 2), halves(7680, 2, 2)
        e_hh, e_hl = halves(8192, HRING, HRING), halves(9728, HRING, HRING)
        w_t = halves(6144, 4, 4)[0:2 * E]

        up_w = [w[:, 0:E * DE].rearrange("p (e n) -> p e n", e=E) for w in (w_h, w_l)]
        gate_w = [w[:, E * DE:2 * E * DE].rearrange("p (e n) -> p e n", e=E) for w in (w_h, w_l)]
        down_w = [w[:, 2 * E * DE:F0_COLS].rearrange("p (e j d) -> p e j d", e=E, j=DEC) for w in (w_h, w_l)]
        up1_w = [w[:, 0:E * FE].rearrange("p (e n) -> p e n", e=E) for w in (w_h, w_l)]
        down1_w = [w[:, E * FE:F1_COLS].rearrange("p (e j d) -> p e j d", e=E, j=FC) for w in (w_h, w_l)]
        HIGH, LOW = 0, 1
        TERMS = ((HIGH, HIGH), (HIGH, LOW), (LOW, HIGH))

        def product(out, weights, moving, first=True, last=True):
            for t, (a, b) in enumerate(TERMS):
                ins = nc.tensor.matmul(out, weights[a], moving[b], start=first and t == 0,
                                       stop=last and t == 2)
            return ins

        def chunk(buf, c):
            return buf[:, bass.ds(c, 1), :].rearrange("p o s -> p (o s)")

        def high_pool(own, src, high):
            own.link(nc.gpsimd.tensor_scalar(src, src, W_SCALE, 0.0, ALU.mult, ALU.add))
            own.link(nc.gpsimd.tensor_scalar(high, src, 1.0, 0.0, ALU.mult, ALU.add))

        def split_pool(own, src, high, low):
            high_pool(own, src, high)
            return nc.gpsimd.tensor_tensor(low, src, high, ALU.subtract)

        def split_input_act(act, r, n, src, ready):
            for c in range(NB):
                act.wait_ge(ready, n + c + 1)
                nc.scalar.activation(y_h[:, c, :], src[:, c, :], ACT.Copy, scale=Y_SCALE).then_inc(e_yh_ready, 1)

        def split_input_dve(dve, r, src):
            for c in range(NB):
                dve.wait_ge(e_yh_ready, NB * r + c + 1)
                nc.vector.scalar_tensor_tensor(out=y_l[:, c, :], in0=src[:, c, :], scalar=Y_SCALE,
                                               in1=y_h[:, c, :], op0=ALU.mult, op1=ALU.subtract)\
                  .then_inc(e_yl_ready, 1)

        def route_pe(pe, p, src, router):
            r = layers.index(p)
            k, singles, boths, lns = norm_of[p]
            for t in range(NT):
                if t % T == 0:
                    pe.wait_ge(y_ready if p < 5 else xn_ready, xns[p][p < 5] * NB + t // T + 1)
                if t == 0 and p < 5:
                    pe.wait_ge(ln_ready, NB * (lns + 1) + 1)
                ins = nc.tensor.matmul(P[:, 4, t * E:(t + 1) * E], src[:, t // T, t % T * 128:t % T * 128 + 128],
                                       router[:, :], start=True, stop=True)
            ins.then_inc(e_logits_ready, 1)
            pe.wait_ge(e_w_ready, r + 1)
            if p < 5:
                pe.wait_ge(ln_ready, NB * (lns + 2))
            for t in range(NT):
                ins = nc.tensor.matmul(P[0:2 * E, 4 + t // T, t % T * 128:t % T * 128 + 128],
                                       w16[:, t, :], ident_h[:, :], start=True, stop=True)
            ins.then_inc(e_wt_psum, 1)
            pe.wait_ge(e_wth_ready, NB * (r + 1))

        def route_act(act, p):
            r = layers.index(p)
            n = xns[p][p < 5] * NB
            split_input_act(act, splits.index(p), n, y if p < 5 else xn, y_ready if p < 5 else xn_ready)
            act.wait_ge(e_gap_ready, r + 1)
            nc.scalar.activation(hot[:, 4, :, 1:2], hot[:, 4, :, 0:1], ACT.Exp).then_inc(e_exp_ready, 1)
            act.wait_ge(e_wt_psum, r + 1)
            for c in range(NB):
                nc.scalar.activation(w_t[:, c, :], P[0:2 * E, 4 + c, :], ACT.Copy)\
                  .then_inc(e_wth_ready, 1)

        def route_dve(dve, own, p):
            r = layers.index(p)
            n = xns[p][p < 5] * NB
            src = y if p < 5 else xn
            dve.wait_ge(e_logits_ready, r + 1)
            lg, first, second, key = (hot[:, i, :, :] for i in range(4))
            m1, m2, km = (hot[:, 5, :, i:i + 1] for i in range(3))
            gap, ex, den, w2 = (hot[:, 4, :, i:i + 1] for i in range(4))
            logits = P[:, 4, 0:NT * E].rearrange("p (t e) -> p t e", e=E)
            wide = [128, NT, E]
            if p < 5:
                own.link(nc.vector.tensor_copy(lg, logits))
            else:
                own.link(nc.vector.tensor_tensor(lg, logits, f1_rb[:, :].unsqueeze(1).broadcast_to(wide), ALU.add))
            for best, hit in ((m1, first), (m2, second)):
                own.link(nc.vector.tensor_reduce(out=best, in_=lg, op=ALU.max, axis=AX.X))
                own.link(nc.vector.tensor_tensor(key, lg, best.broadcast_to(wide), ALU.is_equal))
                own.link(nc.vector.tensor_tensor(key, key, rev[:, :, :], ALU.mult))
                own.link(nc.vector.tensor_reduce(out=km, in_=key, op=ALU.max, axis=AX.X))
                own.link(nc.vector.tensor_tensor(hit, key, km.broadcast_to(wide), ALU.is_equal))
                if hit is first:
                    own.link(nc.vector.scalar_tensor_tensor(out=lg, in0=hit, scalar=-3e38, in1=lg,
                                                            op0=ALU.mult, op1=ALU.add))
            nc.vector.tensor_tensor(gap, m2, m1, ALU.subtract).then_inc(e_gap_ready, 1)
            dve.wait_ge(e_exp_ready, r + 1)
            own.link(nc.vector.tensor_scalar(den, ex, 1.0, 1.0 / Y_SCALE, ALU.add, ALU.mult))
            own.link(nc.vector.reciprocal(den, den))
            own.link(nc.vector.tensor_tensor(w2, ex, den, ALU.mult))
            nc.vector.tensor_tensor(first, first, den.broadcast_to(wide), ALU.mult)
            own.link(nc.vector.tensor_tensor(second, second, w2.broadcast_to(wide), ALU.mult))
            own.link(nc.vector.tensor_tensor(w_rt[:, :, :], first, second, ALU.add))
            own.link(nc.vector.tensor_copy(w16[:, :, 0:E], w_rt[:, :, :]))
            nc.vector.tensor_tensor(w16[:, :, E:2 * E], w_rt[:, :, :], w16[:, :, 0:E], ALU.subtract)\
              .then_inc(e_w_ready, 1)
            split_input_dve(dve, splits.index(p), src)

        def spread_weight(e, bank, c):
            nc.tensor.matmul(P[:, bank, :], pick_both[:, e:e + 1].broadcast_to([2 * E, 128]),
                             w_t[:, bass.ds(c, 1), :], start=True, stop=True).then_inc(e_wb_ready, 1)

        def bases(p):
            sw, rl = [q for q in swiglu if q < p], [q for q in relu if q < p]
            n = NB * (len(sw) * E * DEC + len(rl) * E * FC)
            return n, NB * E * (len(sw) + len(rl)), NB * E * len(sw), NB * (len(sw) + len(rl))

        def part(j):
            return min(128, DE - 128 * j)

        def swiglu_pe(pe, p):
            steps0, wb0, yw0, out0 = bases(p)
            xd = at[p]
            start(pe, p, by_chunk=True)
            norm_pe(pe, norm_of[p][0], x, p)
            route_pe(pe, p, y, f0_router)
            pe.wait_ge(xn_ready, NB * xns[p][0] + NB)
            pe.wait_ge(e_yl_ready, NB * (splits.index(p) + 1))
            pe.wait_ge(raw_split, 1)
            with pe.Fori(0, NB) as c:
                n0, e0 = c * (E * DEC) + steps0, c * E
                moving = [y_h[:, bass.ds(c, 1), :], y_l[:, bass.ds(c, 1), :]]

                def down(i):
                    m = part(i % DEC)
                    pe.wait_ge(e_hl_ready, n0 + i + 1)
                    if i == 0:
                        pe.wait_ge(x_done, c + xd)
                    ins = product(P[:, 6, :], [w[0:m, i // DEC, i % DEC, :] for w in down_w],
                                  [e_hh[0:m, i % HRING, :], e_hl[0:m, i % HRING, :]],
                                  first=i == 0, last=i == E * DEC - 1)
                    ins.then_inc(e_down_done, 1)

                def gate(i):
                    e, j, m = i // DEC, i % DEC, part(i % DEC)
                    if j == 0:
                        pe.wait_ge(e_ywl_ready, e0 + yw0 + e + 1)
                    if i >= 2:
                        pe.wait_ge(e_h_ready, n0 + i - 1)
                    product(P[0:m, 2 + i % 2, :], [w[:, e, 128 * j:128 * j + m] for w in gate_w],
                            [e_ywh[:, e % 2, :], e_ywl[:, e % 2, :]]).then_inc(e_gate_ready, 1)

                spread_weight(0, 4, c)
                for i in range(E * DEC):
                    e, j, m = i // DEC, i % DEC, part(i % DEC)
                    if i >= 3:
                        pe.wait_ge(e_act_done, n0 + i - 2)
                    if j == 0 and 1 <= e < E - 1:
                        pe.wait_ge(e_yw_ready, e0 + yw0 + e)
                    product(P[0:m, E_UP[i % 3], :], [w[:, e, 128 * j:128 * j + m] for w in up_w], moving)\
                        .then_inc(e_up_ready, 1)
                    if j == 0 and e + 1 < E:
                        spread_weight(e + 1, 4 + (e + 1) % 2, c)
                    if i >= 1:
                        gate(i - 1)
                    if i >= E_LAG:
                        down(i - E_LAG)
                gate(E * DEC - 1)
                for i in range(E * DEC - E_LAG, E * DEC):
                    down(i)

        def swiglu_act(act, p):
            steps0, wb0, yw0, out0 = bases(p)
            k, singles, boths, lns = norm_of[p]
            start(act, p, by_chunk=True)
            norm_act(act, k, True, True, lns)
            route_act(act, p)
            nc.scalar.preload_act_table_set("silu_and_others")
            with act.Fori(0, NB) as c:
                n0, e0 = c * (E * DEC) + steps0, c * E + yw0

                def high_yw(e):
                    act.wait_ge(e_yw_ready, e0 + e + 1)
                    if e >= 2:
                        act.wait_ge(e_gate_ready, n0 + DEC * (e - 1))
                    nc.scalar.activation(e_ywh[:, e % 2, :], e_yw[:, e % 2, :], ACT.Copy)\
                      .then_inc(e_ywh_ready, 1)

                def high_h(i):
                    m = part(i % DEC)
                    act.wait_ge(e_h_ready, n0 + i + 1)
                    if i >= HRING:
                        act.wait_ge(e_down_done, n0 + i - HRING + 1)
                    nc.scalar.activation(e_hh[0:m, i % HRING, :], e_hid[0:m, i % HRING, :], ACT.Copy)\
                      .then_inc(e_hh_ready, 1)

                high_yw(0)
                for i in range(E * DEC + 1):
                    if i < E * DEC:
                        m = part(i % DEC)
                        act.wait_ge(e_up_ready, n0 + i + 1)
                        if i >= AHEAD:
                            act.wait_ge(e_h_ready, n0 + i - AHEAD + 1)
                        nc.scalar.activation(e_act[0:m, i % AHEAD, :], P[0:m, E_UP[i % 3], :], ACT.Silu, scale=UP_BACK)\
                          .then_inc(e_act_done, 1)
                        if i % DEC == 0 and i // DEC + 1 < E:
                            high_yw(i // DEC + 1)
                    if i >= 1:
                        high_h(i - 1)

        def swiglu_dve(dve, own, p):
            steps0, wb0, yw0, out0 = bases(p)
            k, singles, boths, lns = norm_of[p]
            nxn, nyy, nrr = (NB * v for v in xns[p])
            start(dve, p)
            for c in range(NB):
                dve.wait_ge(rstd2_ready, NB * boths + c + 1)
                nc.vector.scalar_tensor_tensor(out=y[:, c, :], in0=P[:, c, :], scalar=col("rms_w"),
                                               in1=rstd2[:, c, :], op0=ALU.mult, op1=ALU.mult)\
                  .then_inc(y_ready, 1)
            route_dve(dve, own, p)
            for c in range(NB):
                dve.wait_ge(rstd_ready, NB * singles + c + 1)
                nc.vector.tensor_tensor(xn[:, c, :], P[:, c, :], rstd[:, c, :], ALU.mult).then_inc(xn_ready, 1)
            xd = at[p]
            with dve.Fori(0, NB) as c:
                n0, e0 = c * (E * DEC) + steps0, c * E
                yc = chunk(y, c)

                def weigh(e):
                    dve.wait_ge(e_wb_ready, e0 + wb0 + e + 1)
                    if e >= 2:
                        dve.wait_ge(e_ywl_ready, e0 + yw0 + e - 1)
                    nc.vector.tensor_tensor(e_yw[:, e % 2, :], yc, P[:, 4 + e % 2, :], ALU.mult)\
                      .then_inc(e_yw_ready, 1)

                def low_yw(e):
                    dve.wait_ge(e_ywh_ready, e0 + yw0 + e + 1)
                    if e >= 2:
                        dve.wait_ge(e_gate_ready, n0 + DEC * (e - 1))
                    nc.vector.tensor_tensor(e_ywl[:, e % 2, :], e_yw[:, e % 2, :], e_ywh[:, e % 2, :],
                                            ALU.subtract).then_inc(e_ywl_ready, 1)

                def low_h(i):
                    m = part(i % DEC)
                    dve.wait_ge(e_hh_ready, n0 + i + 1)
                    nc.vector.tensor_tensor(e_hl[0:m, i % HRING, :], e_hid[0:m, i % HRING, :], e_hh[0:m, i % HRING, :],
                                            ALU.subtract).then_inc(e_hl_ready, 1)

                weigh(0)
                low_yw(0)
                for i in range(E * DEC + 1):
                    if i < E * DEC:
                        m, e = part(i % DEC), i // DEC
                        if i % DEC == 0 and e + 1 < E:
                            weigh(e + 1)
                        dve.wait_ge(e_gate_ready, n0 + i + 1)
                        dve.wait_ge(e_act_done, n0 + i + 1)
                        if i >= HRING:
                            dve.wait_ge(e_hl_ready, n0 + i - HRING + 1)
                        nc.vector.scalar_tensor_tensor(out=e_hid[0:m, i % HRING, :], in0=P[0:m, 2 + i % 2, :],
                                                       scalar=UP_BACK * H_SCALE, in1=e_act[0:m, i % AHEAD, :],
                                                       op0=ALU.mult, op1=ALU.mult).then_inc(e_h_ready, 1)
                        if i % DEC == 1 and e + 1 < E:
                            low_yw(e + 1)
                    if i >= 1:
                        low_h(i - 1)
                dve.wait_ge(e_down_done, n0 + E * DEC)
                dve.wait_ge(resid_ready, NB * nrr // NB + NB)
                xb = chunk(x, c)
                nc.vector.scalar_tensor_tensor(out=xb, in0=P[:, 6, :], scalar=DOWN_BACK, in1=xb,
                                               op0=ALU.mult, op1=ALU.add).then_inc(x_done, 1)

        def swiglu_pool(pool, p):
            k = norm_of[p][0]
            for c in range(NB):
                pool.wait_ge(xn_ready, NB * xns[p][0] + c + 1)
                pool.wait_ge(xc_ready, NB * k + c + 1)
                nc.gpsimd.tensor_tensor(x[:, c, :], x[:, c, :], xn[:, c, :], ALU.add).then_inc(resid_ready, 1)

        def relu_pe(pe, p):
            steps0, wb0, yw0, out0 = bases(p)
            xd = at[p]
            start(pe, p, by_chunk=True)
            norm_pe(pe, norm_of[p][0], x, p)
            route_pe(pe, p, xn, f1_router)
            pe.wait_ge(e_yl_ready, NB * (splits.index(p) + 1))
            pe.wait_ge(raw_split, 1 + bool(swiglu))
            n_steps = E * FC
            with pe.Fori(0, NB) as c:
                n0, e0 = c * n_steps + steps0, c * E + wb0
                moving = [y_h[:, bass.ds(c, 1), :], y_l[:, bass.ds(c, 1), :]]

                def down(i):
                    pe.wait_ge(e_hl_ready, n0 + i + 1)
                    product(P[:, 6, :], [w[:, i // FC, i % FC, :] for w in down1_w],
                            [e_hh[:, i % HRING, :], e_hl[:, i % HRING, :]], first=False, last=i == n_steps - 1)\
                        .then_inc(e_down_done, 1)

                spread_weight(0, R_SPREAD[0], c)
                for e in range(E):
                    for j in range(FC):
                        i = FC * e + j
                        if i >= 4:
                            pe.wait_ge(e_act_done, n0 + i - 3)
                        if j == 0 and 2 <= e < E - 1:
                            pe.wait_ge(e_h_ready, n0 + FC * (e - 1))
                        if i == 1:
                            pe.wait_ge(x_done, c + xd)
                        product(P[:, i % 4, :], [w[:, e, 128 * j:128 * j + 128] for w in up1_w], moving)\
                            .then_inc(e_up_ready, 1)
                        if j == 0 and e + 1 < E:
                            spread_weight(e + 1, R_SPREAD[(e + 1) % 3], c)
                        if i == 1:
                            for u in range(2):
                                nc.tensor.matmul(P[:, 6, :], b2_parts[:, u, :], w_t[:, bass.ds(c, 1), :],
                                                 start=u == 0, stop=False)
                        if i >= R_LAG:
                            down(i - R_LAG)
                for i in range(n_steps - R_LAG, n_steps):
                    down(i)

        b2_parts = sb("b2_parts", [2 * E, 2, D], F16)

        def relu_act(act, p):
            steps0, wb0, yw0, out0 = bases(p)
            k, singles, boths, lns = norm_of[p]
            start(act, p, by_chunk=True)
            norm_act(act, k, True, False, lns)
            route_act(act, p)
            n_steps = E * FC
            with act.Fori(0, NB) as c:
                n0 = c * n_steps + steps0
                for i in range(n_steps + 1):
                    if i < n_steps:
                        act.wait_ge(e_up_ready, n0 + i + 1)
                        if i >= 4:
                            act.wait_ge(e_h_ready, n0 + i - 3)
                        nc.scalar.activation(e_act[:, i % 4, :], P[:, i % 4, :], ACT.Relu, scale=UP_BACK,
                                             bias=col("b1", i)).then_inc(e_act_done, 1)
                    if i >= 1:
                        act.wait_ge(e_h_ready, n0 + i)
                        if i > HRING:
                            act.wait_ge(e_down_done, n0 + i - HRING)
                        nc.scalar.activation(e_hh[:, (i - 1) % HRING, :], e_hid[:, (i - 1) % HRING, :], ACT.Copy)\
                          .then_inc(e_hh_ready, 1)

        def relu_dve(dve, own, p):
            steps0, wb0, yw0, out0 = bases(p)
            k, singles, boths, lns = norm_of[p]
            start(dve, p)
            for c in range(NB):
                dve.wait_ge(rstd_ready, NB * singles + c + 1)
                nc.vector.tensor_tensor(xn[:, c, :], P[:, c, :], rstd[:, c, :], ALU.mult).then_inc(xn_ready, 1)
            route_dve(dve, own, p)
            n_steps = E * FC
            with dve.Fori(0, NB) as c:
                n0, e0 = c * n_steps + steps0, c * E + wb0
                for i in range(n_steps + 1):
                    if i < n_steps:
                        e = i // FC
                        if i % FC == 0:
                            dve.wait_ge(e_wb_ready, e0 + e + 1)
                        dve.wait_ge(e_act_done, n0 + i + 1)
                        if i >= HRING:
                            dve.wait_ge(e_hl_ready, n0 + i - HRING + 1)
                        nc.vector.tensor_tensor(e_hid[:, i % HRING, :], e_act[:, i % 4, :], P[:, R_SPREAD[e % 3], :],
                                                ALU.mult).then_inc(e_h_ready, 1)
                    if i >= 1:
                        dve.wait_ge(e_hh_ready, n0 + i)
                        nc.vector.tensor_tensor(e_hl[:, (i - 1) % HRING, :], e_hid[:, (i - 1) % HRING, :],
                                                e_hh[:, (i - 1) % HRING, :], ALU.subtract).then_inc(e_hl_ready, 1)
                dve.wait_ge(e_down_done, n0 + n_steps)
                xb = chunk(x, c)
                nc.vector.scalar_tensor_tensor(out=xb, in0=P[:, 6, :], scalar=DOWN_BACK, in1=xb,
                                               op0=ALU.mult, op1=ALU.add).then_inc(x_done, 1)

        a_setup = sem("a_setup")
        a_split = sem("a_split")
        a_proj_ready = sem("a_proj_ready")
        a_evac_done = sem("a_evac_done")
        a_high_done = sem("a_high_done")
        a_low_done = sem("a_low_done")
        a_v_ready = sem("a_v_ready")
        a_bias_ready = sem("a_bias_ready")
        a_v_done = sem("a_v_done")
        a_s_ready = sem("a_s_ready")
        a_max_done = sem("a_max_done")
        a_row_ready = sem("a_row_ready")
        a_row_done = sem("a_row_done")
        a_st_ready = sem("a_st_ready")
        a_exp_done = sem("a_exp_done")
        a_pv_done = sem("a_pv_done")
        a_den_done = sem("a_den_done")
        a_rec_done = sem("a_rec_done")
        a_at_done = sem("a_at_done")
        a_out_done = sem("a_out_done")
        a_z_done = sem("a_z_done")
        KV, MISC, ST = (4, 5), 7, (2, 3, 6)
        OUTB = 0
        QBUF = 3
        a_q1, a_q2, a_k1, a_k2 = (WK[:, 1536 * i:1536 * i + 1536].bitcast(F16)
                                  .rearrange("p (b o s) -> p b o s", b=QBUF, o=2) for i in range(4))
        a_f32 = WK[:, 6144:7168].rearrange("p (c s) -> p c s", c=2)
        a_v = WK[:, 7168:13312].rearrange("p (t a n) -> p t a n", t=T, a=PAIRS)
        a_pt = WK[:, 13312:15360].rearrange("p (c s) -> p c s", c=4)
        a_at = raw[:, 4096:8192].rearrange("p (c s) -> p c s", c=PAIRS)
        a_rec = WK[:, 16896:17408]
        a_nm = WK[:, 17408:17416].bitcast(F16).rearrange("p (u t) -> p u t", u=4)
        a_qs = WK[:, 17424:17424 + PAIRS]
        a_bo = WK[:, 17450:17451]
        a_bqs = WK[:, 17440:17440 + PAIRS]
        wo_w = raw[:, 3072:4096]
        qkv_f32 = raw[:, 4096:7168]
        qkv_parts = [raw[:, 1536 * i:1536 * i + 1536].bitcast(F16) for i in range(2)]
        HALVES = ((0, 64), (64, 128))

        def heads_pe(pe, p):
            start(pe, p, by_chunk=True)
            norm_pe(pe, norm_of[p][0], x, p)
            pe.wait_ge(xn_ready, NB * xns[p][0] + NB)
            for a in range(PAIRS):
                ins = nc.tensor.matmul(P[:, MISC, 0:1], wo_w[:, 128 * a:128 * a + 128], col("bv", a),
                                       start=a == 0, stop=a == PAIRS - 1)
            ins.then_inc(a_bias_ready, 1)
            pe.wait_ge(a_setup, 2)
            pe.wait_ge(a_split, 1)
            pe.wait_ge(e_yl_ready, NB * (splits.index(p) + 1))
            with pe.Fori(0, NB) as b:
                xb_parts = [w[:, bass.ds(b, 1), :] for w in (y_h, y_l)]

                def project(q, bank):
                    w0 = (q % 2) * H0 * HD0 + (q // 2) * 128
                    product(P[:, bank, :], [w[:, w0:w0 + 128] for w in qkv_parts], xb_parts)\
                      .then_inc(a_proj_ready, 1)

                def maxima(u, t):
                    lo, hi = HALVES[u % 2]
                    buf = u // 2 % QBUF
                    if 4 * u + t >= 2:
                        pe.wait_ge(a_max_done, b * 64 + 4 * u + t - 1)
                    nc.tensor.matmul(P[:, (4 * u + t) % 2, :], a_q1[lo:hi, buf, u % 2, 128 * t:128 * t + 128],
                                     a_k1[lo:hi, buf, u % 2, :], start=True, stop=True).then_inc(a_s_ready, 1)

                def max_row(u):
                    r = 64 if u % 2 == 0 else 0
                    pe.wait_ge(a_max_done, b * 64 + 4 * u + 4)
                    for t in range(T):
                        ins = nc.tensor.matmul(P[r:r + 1, MISC, 128 * t:128 * t + 128], a_nm[:, u % 4, t:t + 1],
                                               ident_h[:, :], start=True, stop=True)
                    ins.then_inc(a_row_ready, 1)

                def values(i):
                    u, t = i // T, i % T
                    pe.wait_ge(a_exp_done, b * 64 + i + 1)
                    if t == 0 and u >= 2:
                        pe.wait_ge(a_at_done, b * 16 + u - 1)
                    v0 = 64 * (u % 2)
                    nc.tensor.matmul(P[:, KV[u % 2], :], a_v[:, t, u // 2, v0:v0 + 128], a_pt[:, i % 4, :],
                                     start=t == 0, stop=t == T - 1).then_inc(a_pv_done, 1)

                def project_out(a):
                    pe.wait_ge(a_at_done, b * 16 + 2 * a + 2)
                    nc.tensor.matmul(P[:, OUTB, :], wo_w[:, 128 * a:128 * a + 128], a_at[:, a, :],
                                     start=a == 0, stop=a == PAIRS - 1).then_inc(a_out_done, 1)

                for q in range(4):
                    project(q, 4 + q)
                pe.wait_ge(a_z_done, b + 1)
                for v in range(2 * T):
                    if v >= 4:
                        pe.wait_ge(a_v_done, b * 8 + v - 3)
                    w0 = 2 * H0 * HD0 + 512 * (v % 2)
                    tokens = slice(128 * (v // 2), 128 * (v // 2) + 128)
                    product(P[:, v % 4, :], [w[:, bass.ds(b, 1), tokens].rearrange("p o s -> p (o s)") for w in (y_h, y_l)],
                            [w[:, w0:w0 + 512] for w in qkv_parts]).then_inc(a_v_ready, 1)
                pe.wait_ge(a_v_done, b * 8 + 8)
                for u in range(2):
                    if u == 0:
                        pe.wait_ge(a_high_done, b * 16 + 2)
                    for t in range(T):
                        maxima(u, t)
                pe.wait_ge(a_evac_done, b * 16 + 4)
                max_row(0)
                for u in range(H0):
                    lo, hi = HALVES[u % 2]
                    buf, o = u // 2 % QBUF, u % 2
                    for t in range(T):
                        i = T * u + t
                        if t == 0 and u + 4 < 2 * PAIRS:
                            pe.wait_ge(a_row_done, b * 16 + u + 1)
                            project(u + 4, MISC)
                        if t == 2 and u + 1 < H0:
                            pe.wait_ge(a_evac_done, b * 16 + min(u + 5, 16))
                            pe.wait_ge(a_row_done, b * 16 + u + 1)
                            max_row(u + 1)
                        if t == 0:
                            pe.wait_ge(a_row_done, b * 16 + u + 1)
                            pe.wait_ge(a_low_done, b * 16 + 2 * (u // 2) + 2)
                        if i >= 3:
                            pe.wait_ge(a_exp_done, b * 64 + i - 2)
                        last_row = 65 if o == 0 else 128
                        nc.tensor.matmul(P[:, ST[i % 3], :], a_k1[:, buf, o, 128 * t:128 * t + 128],
                                         a_q1[:, buf, o, :], start=True, stop=False)
                        nc.tensor.matmul(P[:, ST[i % 3], :], a_k2[0:last_row, buf, o, 128 * t:128 * t + 128],
                                         a_q2[0:last_row, buf, o, :], start=False, stop=True)\
                          .then_inc(a_st_ready, 1)
                        if i >= 2:
                            values(i - 2)
                        if u + 2 < H0:
                            if t == 0:
                                pe.wait_ge(a_high_done, b * 16 + 2 * ((u + 2) // 2) + 2)
                            maxima(u + 2, t)
                values(T * H0 - 2)
                values(T * H0 - 1)
                for a in range(PAIRS):
                    project_out(a)
            pe.wait_ge(a_z_done, NB + 1)
            norm_pe(pe, norm_of["post"][0], xn)

        def heads_act(act, p):
            k, singles, boths, lns = norm_of[p]
            start(act, p, by_chunk=True)
            norm_act(act, k, True, False, lns)
            split_input_act(act, splits.index(p), NB * xns[p][0], xn, xn_ready)
            act.wait_ge(a_setup, 2)
            with act.Fori(0, NB) as b:
                def evacuate(q, bank):
                    act.wait_ge(a_proj_ready, b * 16 + q + 1)
                    if q >= 2:
                        act.wait_ge(a_high_done, b * 16 + q - 1)
                        act.wait_ge(a_low_done, b * 16 + q - 1)
                    a = q // 2
                    if q % 2 == 0:
                        nc.scalar.activation(a_f32[:, 0, :], P[:, bank, :], ACT.Identity,
                                             scale=a_qs[:, a:a + 1], bias=a_bqs[:, a:a + 1]).then_inc(a_evac_done, 1)
                    else:
                        nc.scalar.activation(a_f32[:, 1, :], P[:, bank, :], ACT.Identity, scale=UP_BACK,
                                             bias=col("bk", a)).then_inc(a_evac_done, 1)

                def row(u):
                    r = 64 if u % 2 == 0 else 0
                    act.wait_ge(a_row_ready, b * 16 + u + 1)
                    nc.scalar.activation(a_q2[r:r + 1, u // 2 % QBUF, u % 2, :], P[r:r + 1, MISC, :], ACT.Copy)\
                      .then_inc(a_row_done, 1)

                def reciprocal(u):
                    (lo, hi), (dlo, dhi) = HALVES[u % 2], HALVES[1 - u % 2]
                    act.wait_ge(a_pv_done, b * 64 + 4 * u + 4)
                    if u >= 2:
                        act.wait_ge(a_at_done, b * 16 + u - 1)
                    nc.scalar.activation(a_rec[lo:hi, :], P[dlo:dhi, KV[u % 2], :], ACT.Ln).then_inc(a_den_done, 1)
                    act.wait_ge(a_den_done, b * 16 + u + 1)
                    nc.scalar.activation(a_rec[lo:hi, :], a_rec[lo:hi, :], ACT.Exp, scale=-1.0).then_inc(a_rec_done, 1)

                for q in range(2):
                    evacuate(q, 4 + q)
                for v in range(2 * T):
                    act.wait_ge(a_v_ready, b * 8 + v + 1)
                    dst = a_v[:, v // 2, 4 * (v % 2):4 * (v % 2) + 4, :].rearrange("p a (k n) -> p a k n", k=3)[:, :, 0::2, :]
                    nc.scalar.activation(dst, P[:, v % 4, :].rearrange("p (a k n) -> p a k n", a=4, k=2), ACT.Copy,
                                         scale=UP_BACK).then_inc(a_v_done, 1)
                for q in range(2, 4):
                    evacuate(q, 4 + q)
                row(0)
                for u in range(H0):
                    for t in range(T):
                        i = T * u + t
                        if t == 3 and u + 1 < H0:
                            row(u + 1)
                        if t == 1 and u + 4 < 2 * PAIRS:
                            evacuate(u + 4, MISC)
                        if t == 2 and u >= 1:
                            reciprocal(u - 1)
                        act.wait_ge(a_st_ready, b * 64 + i + 1)
                        if i >= 4:
                            act.wait_ge(a_pv_done, b * 64 + i - 3)
                        nc.scalar.activation(a_pt[:, i % 4, :], P[:, ST[i % 3], :], ACT.Exp).then_inc(a_exp_done, 1)
                reciprocal(H0 - 1)
            k, singles, boths, lns = norm_of["post"]
            norm_act(act, k, True, False, lns)

        def heads_pool(pool, own, p):
            pool.wait_ge(x_done, at[p])
            nc.gpsimd.memset(a_v[:, :, :, 64:128], 1.0)
            nc.gpsimd.memset(a_q2[0:64, :, 1, :], 0.0)
            own.link(nc.gpsimd.memset(a_k2[0:64, :, 1, :], 0.0))
            nc.gpsimd.memset(a_k2[0:1, :, 1, :], 1.0)
            nc.gpsimd.memset(a_k2[64:65, :, 0, :], 1.0).then_inc(a_setup, 1)
            with pool.Fori(0, NB) as b:
                for q in range(2 * PAIRS):
                    buf = q // 2 % QBUF
                    pool.wait_ge(a_evac_done, b * 16 + q + 1)
                    first = True
                    for o, (lo, hi) in enumerate(HALVES):
                        src = a_f32[lo:hi, q % 2, :]
                        if q % 2 == 0:
                            outs = (a_q1[lo:hi, buf, o, :], a_q2[lo:hi, buf, o, :])
                        else:
                            outs = (a_k1[0:64, buf, o, :], a_k1[64:128, buf, o, :])
                        for dst in outs:
                            if first:
                                ins = nc.gpsimd.tensor_tensor(dst, src, ones[lo:hi, 0:1].broadcast_to([64, S]), ALU.mult)
                            else:
                                ins = nc.gpsimd.tensor_scalar(dst, src, 1.0, 0.0, ALU.mult, ALU.add)
                            first = False
                    ins.then_inc(a_high_done, 1)

        def heads_dve(dve, own, p):
            k, singles, boths, lns = norm_of[p]
            start(dve, p)
            dve.wait_ge(w_loaded[2], 32)
            for c in range(NB):
                dve.wait_ge(rstd_ready, NB * singles + c + 1)
                nc.vector.tensor_tensor(xn[:, c, :], P[:, c, :], rstd[:, c, :], ALU.mult).then_inc(xn_ready, 1)
            adaptive = cols[:, COLS["adaptive"][0]:COLS["adaptive"][0] + PAIRS]
            own.link(nc.vector.tensor_scalar(a_qs, adaptive, float(HD0) ** -0.5, None, ALU.mult))
            dve.wait_ge(xn_ready, NB * xns[p][0] + NB)
            dve.wait_ge(a_bias_ready, 1)
            nc.vector.tensor_tensor(a_bo, P[:, MISC, 0:1], col("bo"), ALU.add).then_inc(a_z_done, 1)
            own.link(nc.vector.tensor_tensor(a_bqs, cols[:, COLS["bq"][0]:COLS["bq"][0] + PAIRS], a_qs, ALU.mult))
            nc.vector.tensor_scalar(a_qs, a_qs, UP_BACK, None, ALU.mult).then_inc(a_setup, 1)
            split_input_dve(dve, splits.index(p), xn)
            with dve.Fori(0, NB) as b:
                def low(q):
                    buf = q // 2 % QBUF
                    dve.wait_ge(a_high_done, b * 16 + q + 1)
                    for o, (lo, hi) in enumerate(HALVES):
                        high = (a_q1, a_k1)[q % 2][lo:hi, buf, o, :]
                        if q % 2 == 0:
                            dst = a_q1[64 - lo:128 - lo, buf, o, :]
                        else:
                            dst = a_k2[lo:hi, buf, o, :]
                        ins = nc.vector.tensor_tensor(dst, a_f32[lo:hi, q % 2, :], high, ALU.subtract)
                    ins.then_inc(a_low_done, 1)

                def maxima(u, t):
                    dve.wait_ge(a_s_ready, b * 64 + 4 * u + t + 1)
                    nc.vector.tensor_reduce(out=a_nm[:, u % 4, t:t + 1], in_=P[:, (4 * u + t) % 2, :], op=ALU.max,
                                            axis=AX.X, negate=True).then_inc(a_max_done, 1)

                def normalise(u):
                    lo, hi = HALVES[u % 2]
                    dve.wait_ge(a_rec_done, b * 16 + u + 1)
                    nc.vector.tensor_tensor(a_at[lo:hi, u // 2, :], P[lo:hi, KV[u % 2], :], a_rec[lo:hi, :],
                                            ALU.mult).then_inc(a_at_done, 1)

                for q in range(2):
                    low(q)
                for u in range(2):
                    for t in range(T):
                        maxima(u, t)
                for q in range(2, 4):
                    low(q)
                for u in range(H0):
                    for t in range(T):
                        if u + 2 < H0:
                            maxima(u + 2, t)
                        if t == 3 and u >= 1:
                            normalise(u - 1)
                        if t == 3 and u + 4 < 2 * PAIRS:
                            low(u + 4)
                normalise(H0 - 1)
                dve.wait_ge(a_out_done, b * 8 + 8)
                xb = chunk(xn, b)
                nc.vector.scalar_tensor_tensor(out=xb, in0=P[:, OUTB, :], scalar=a_bo, in1=xb,
                                               op0=ALU.add, op1=ALU.add).then_inc(a_z_done, 1)
            k, singles, boths, lns = norm_of["post"]
            for c in range(NB):
                dve.wait_ge(rstd_ready, NB * singles + c + 1)
                own.link(nc.vector.scalar_tensor_tensor(out=xn[:, c, :], in0=P[:, c, :], scalar=col("gamma"),
                                                        in1=rstd[:, c, :], op0=ALU.mult, op1=ALU.mult))
                nc.vector.scalar_tensor_tensor(out=x[:, c, :], in0=xn[:, c, :], scalar=col("beta"),
                                               in1=x[:, c, :], op0=ALU.add, op1=ALU.add).then_inc(x_done, 1)

        h_setup = sem("h_setup")
        h_proj_ready = sem("h_proj_ready")
        h_v_ready = sem("h_v_ready")
        h_theta_ready = sem("h_theta_ready")
        h_v_done = sem("h_v_done")
        h_red_ready = sem("h_red_ready")
        h_abs_ready = sem("h_abs_ready")
        h_sin_ready = sem("h_sin_ready")
        h_cos_ready = sem("h_cos_ready")
        h_st_ready = sem("h_st_ready")
        h_exp_done = sem("h_exp_done")
        h_pv_done = sem("h_pv_done")
        h_sum_ready = sem("h_sum_ready")
        h_den_ready = sem("h_den_ready")
        h_den_done = sem("h_den_done")
        h_rec_done = sem("h_rec_done")
        h_sin, h_cos = (WK[:, 4096 * i:4096 * i + 4096].rearrange("p (c k s) -> p c k s", c=NB, k=2)
                        for i in range(2))
        h_v = WK[:, 8192:10240].rearrange("p (c s) -> p c s", c=NB)
        h_th, h_n = (WK[:, 10240 + 2048 * i:12288 + 2048 * i].rearrange("p (c k s) -> p c k s", c=2, k=2)
                     for i in range(2))
        h_pt = WK[:, 14336:16384].rearrange("p (t s) -> p t s", t=T)
        h_rec, h_o, h_sum = (WK[:, 16384 + 512 * i:16896 + 512 * i] for i in range(3))
        h_bias = WK[:, 17920:17922]
        phase_w = [small_w[:, 128 * i:128 * i + 128] for i in range(3)]
        V_BANK, PV_BANK, DEN = 6, 4, 5

        def phase_pe(pe, p):
            start(pe, p, by_chunk=True)
            norm_pe(pe, norm_of[p][0], x, p)
            for c in range(NB):
                pe.wait_ge(xn_ready, NB * xns[p][0] + (NB if c == 0 else c + 1))
                for k in range(2):
                    if c >= 2:
                        pe.wait_ge(h_theta_ready, 2 * (c - 2) + k + 1)
                    nc.tensor.matmul(P[:, 2 * (c % 2) + k, :], phase_w[k], xn[:, c, :], start=True, stop=True)\
                      .then_inc(h_proj_ready, 1)
                if c >= 2:
                    pe.wait_ge(h_v_done, c - 1)
                for t in range(T):
                    ins = nc.tensor.matmul(P[:, V_BANK + c % 2, 128 * t:128 * t + 128],
                                           xn[:, c, 128 * t:128 * t + 128], phase_w[2], start=True, stop=True)
                ins.then_inc(h_v_ready, 1)
            pe.wait_ge(h_theta_ready, 2 * NB)
            for b in range(NB):
                def values(t):
                    pe.wait_ge(h_exp_done, b * T + t + 1)
                    if t == 0:
                        pe.wait_ge(h_v_done, NB)
                        pe.wait_ge(x_done, b + at[p])
                    nc.tensor.matmul(P[:, PV_BANK, :], h_v[:, b, 128 * t:128 * t + 128], h_pt[:, t, :],
                                     start=t == 0, stop=t == T - 1).then_inc(h_pv_done, 1)

                pe.wait_ge(h_cos_ready, b + 1)
                for t in range(T):
                    for f in (h_cos, h_sin):
                        ins = nc.tensor.matmul(P[:, t, :], f[:, b, 1, 128 * t:128 * t + 128],
                                               f[:, b, 0, :], start=f is h_cos, stop=f is h_sin)
                    ins.then_inc(h_st_ready, 1)
                    if t >= 2:
                        values(t - 2)
                values(T - 2)
                values(T - 1)
                pe.wait_ge(h_sum_ready, b + 1)
                nc.tensor.matmul(P[:, DEN, :], ones[:, :], h_sum, start=True, stop=True).then_inc(h_den_ready, 1)

        def phase_act(act, p):
            k, singles, boths, lns = norm_of[p]
            start(act, p, by_chunk=True)
            norm_act(act, k, True, False, lns)
            act.wait_ge(h_setup, 1)

            def sines(c):
                act.wait_ge(h_red_ready, c + 1)
                nc.scalar.activation(h_n[:, c % 2, :, :], h_th[:, c % 2, :, :], ACT.Abs).then_inc(h_abs_ready, 1)
                nc.scalar.activation(h_sin[:, c, :, :], h_th[:, c % 2, :, :], ACT.Sin).then_inc(h_sin_ready, 1)
                act.wait_ge(h_abs_ready, c + 1)
                nc.scalar.activation(h_cos[:, c, :, :], h_n[:, c % 2, :, :], ACT.Sin, scale=-1.0,
                                     bias=const(K_HALFPI)).then_inc(h_cos_ready, 1)

            for c in range(NB):
                for q in range(2):
                    act.wait_ge(h_proj_ready, 2 * c + q + 1)
                    if c >= 2:
                        act.wait_ge(h_sin_ready, c - 1)
                    nc.scalar.activation(h_th[:, c % 2, q, :], P[:, 2 * (c % 2) + q, :], ACT.Identity,
                                         scale=col("inv_wl"), bias=h_bias[:, q:q + 1]).then_inc(h_theta_ready, 1)
                act.wait_ge(h_v_ready, c + 1)
                nc.scalar.activation(h_v[:, c, :], P[:, V_BANK + c % 2, :], ACT.Copy).then_inc(h_v_done, 1)
                if c >= 1:
                    sines(c - 1)
            sines(NB - 1)
            nc.scalar.preload_act_table_set(EXP_LN)
            with act.Fori(0, NB) as b:
                for t in range(T):
                    act.wait_ge(h_st_ready, b * T + t + 1)
                    nc.scalar.activation(h_pt[:, t, :], P[:, t, :], ACT.Exp, scale=float(D) ** -0.5)\
                      .then_inc(h_exp_done, 1)
                act.wait_ge(h_den_ready, b + 1)
                nc.scalar.activation(h_rec, P[:, DEN, :], ACT.Ln).then_inc(h_den_done, 1)
                act.wait_ge(h_den_done, b + 1)
                nc.scalar.activation(h_rec, h_rec, ACT.Exp, scale=-1.0).then_inc(h_rec_done, 1)

        def phase_dve(dve, own, p):
            k, singles, boths, lns = norm_of[p]
            start(dve, p)
            for q, name in enumerate(("pq", "pk")):
                ins = nc.vector.tensor_scalar(h_bias[:, q:q + 1], col(name), col("inv_wl"), col("phase"),
                                              ALU.mult, ALU.add)
            ins.then_inc(h_setup, 1)
            for c in range(NB):
                dve.wait_ge(rstd_ready, NB * singles + c + 1)
                nc.vector.tensor_tensor(xn[:, c, :], P[:, c, :], rstd[:, c, :], ALU.mult).then_inc(xn_ready, 1)
            for c in range(NB):
                th, n = h_th[:, c % 2, :, :], h_n[:, c % 2, :, :]
                dve.wait_ge(h_theta_ready, 2 * c + 2)
                if c >= 2:
                    dve.wait_ge(h_cos_ready, c - 1)
                own.link(nc.vector.tensor_scalar(n, th, 1.0 / (2.0 * math.pi), MAGIC, ALU.mult, ALU.add))
                own.link(nc.vector.tensor_scalar(n, n, MAGIC, None, ALU.subtract))
                for part_2pi in (TWO_PI_HI, TWO_PI_LO):
                    own.link(nc.vector.scalar_tensor_tensor(out=th, in0=n, scalar=-part_2pi, in1=th,
                                                            op0=ALU.mult, op1=ALU.add))
                nc.vector.tensor_scalar(th, th, PI_F, -PI_F, ALU.min, ALU.max).then_inc(h_red_ready, 1)
            with dve.Fori(0, NB) as b:
                own.loop(b, 3)
                dve.wait_ge(h_exp_done, b * T + 2)
                own.link(nc.vector.tensor_tensor(h_sum, h_pt[:, 0, :], h_pt[:, 1, :], ALU.add))
                dve.wait_ge(h_exp_done, b * T + 3)
                own.link(nc.vector.tensor_tensor(h_sum, h_sum, h_pt[:, 2, :], ALU.add))
                dve.wait_ge(h_exp_done, b * T + 4)
                nc.vector.tensor_tensor(h_sum, h_sum, h_pt[:, 3, :], ALU.add).then_inc(h_sum_ready, 1)
                dve.wait_ge(h_rec_done, b + 1)
                dve.wait_ge(h_pv_done, b * T + T)
                own.link(nc.vector.tensor_tensor(h_o, P[:, PV_BANK, :], h_rec, ALU.mult))
                xb = chunk(x, b)
                nc.vector.scalar_tensor_tensor(out=xb, in0=h_o, scalar=col("pv"), in1=xb,
                                               op0=ALU.add, op1=ALU.add).then_inc(x_done, 1)
                own.end(NB)

        c_setup = sem("c_setup")
        c_xb_ready = sem("c_xb_ready")
        c_proj_ready = sem("c_proj_ready")
        c_high_done = sem("c_high_done")
        c_parts_done = sem("c_parts_done")
        c_v_ready = sem("c_v_ready")
        c_v_done = sem("c_v_done")
        c_s_ready = sem("c_s_ready")
        c_max_done = sem("c_max_done")
        c_rows_ready = sem("c_rows_ready")
        c_q_done = sem("c_q_done")
        c_st_ready = sem("c_st_ready")
        c_exp_done = sem("c_exp_done")
        c_ph_done = sem("c_ph_done")
        c_pl_dve = sem("c_pl_dve")
        c_pl_pool = sem("c_pl_pool")
        c_pv_done = sem("c_pv_done")
        c_u_done = sem("c_u_done")
        c_den_ready = sem("c_den_ready")
        c_ln_done = sem("c_ln_done")
        c_rec_done = sem("c_rec_done")
        c_at_done = sem("c_at_done")
        c_out_done = sem("c_out_done")
        STEPS = 4 * T
        CN = GROUPS * STEPS
        RING, LAG = 6, 4
        LEAD = STEPS + 3
        LATE_PROJECTIONS = (1, 3, 5, 7)
        ROWS_AT = STEPS - 2
        O_BANK, DEN_BANK, OUT_BANK, ROW_BANK, ST_BANKS = 4, 5, 6, 5, (2, 3, 7)
        c_xb = WK[:, 0:512]
        c_h = WK[:, 1536:2048].bitcast(F16).rearrange("p (c s) -> p c s", c=2)
        c_q = WK[:, 2048:3072].bitcast(F16).rearrange("p (c s) -> p c s", c=GROUPS)
        c_k = WK[:, 3072:4096].bitcast(F16).rearrange("p (c s) -> p c s", c=GROUPS)
        c_qm = WK[:, 4096:4608].bitcast(F16).rearrange("p (c s) -> p c s", c=2)
        c_va = WK[:, 4608:5632].bitcast(F16).rearrange("p (t h n) -> p t h n", t=T, h=H1)
        c_ph = WK[:, 6656:8192].bitcast(F16).rearrange("p (c s) -> p c s", c=RING)
        c_pl = WK[:, 10240:11776].bitcast(F16).rearrange("p (c s) -> p c s", c=RING)
        c_pt = WK[:, 16064:19136].rearrange("p (c s) -> p c s", c=RING)
        c_u, c_rec = WK[:, 8704:9216], WK[:, 9216:9728]
        c_at = WK[:, 11968:16064].rearrange("p (c j s) -> p c j s", c=2, j=4)
        c_nm = WK[:, 9728:10240].bitcast(F16).rearrange("p (c t n) -> p c t n", c=2, t=T)
        mask_h = WK[:, 11776:11904].bitcast(BF16).rearrange("p (c s) -> p c s", c=2)
        ident_b = WK[:, 11904:11968].bitcast(BF16)
        LOW_Q, LOW_K = col("low_q"), col("low_k")
        cq_w, ck_w, cv_w, co_w = (small_w[:, a:b] for a, b in ((384, 896), (896, 1408), (1408, 1536), (1536, CAUSAL_END)))

        def causal_pe(pe, p):
            start(pe, p, by_chunk=True)
            norm_pe(pe, norm_of[p][0], x, p)
            pe.wait_ge(c_setup, 2)
            pe.wait_ge(xn_ready, NB * xns[p][0] + NB)
            with pe.Fori(0, NB) as b:
                def maxima(n):
                    g, i = n // STEPS, n % STEPS
                    j, t = i // T, i % T
                    w = 128 * (t + 1)
                    if n >= 2:
                        pe.wait_ge(c_max_done, b * CN + n - 1)
                    lo = 32 * j
                    nc.tensor.matmul(P[:, n % 2, 0:w], c_q[lo:lo + 32, g, 128 * t:w], c_k[lo:lo + 32, g, 0:w],
                                     start=True, stop=False)
                    nc.tensor.matmul(P[:, n % 2, w - 128:w], ident_b, mask_h[:, 0, :], start=False, stop=True)\
                      .then_inc(c_s_ready, 1)

                def rows(g):
                    pe.wait_ge(c_max_done, b * 64 + (g + 1) * STEPS)
                    if g >= 2:
                        pe.wait_ge(c_ln_done, b * GROUPS + g - 1)
                    for t in range(T):
                        ins = nc.tensor.matmul(P[:, ROW_BANK, 128 * t:128 * t + 128], c_nm[:, g % 2, t, :],
                                               ident_h[:, :], start=True, stop=True)
                    ins.then_inc(c_rows_ready, 1)

                def values(n):
                    g, i = n // STEPS, n % STEPS
                    j, t = i // T, i % T
                    out_rows = P[32 * j:32 * j + 32, O_BANK, 128 * t:S]
                    pe.wait_ge(c_ph_done, b * 64 + n + 1)
                    if i == 0 and g >= 1:
                        pe.wait_ge(c_u_done, b * GROUPS + g)
                    nc.tensor.matmul(out_rows, c_va[:, t, 4 * g + j, :], c_ph[:, n % RING, 0:S - 128 * t],
                                     start=t == 0, stop=False)
                    if t == 0:
                        pe.wait_ge(c_pl_dve, b * 16 + n // T + 1)
                    else:
                        pe.wait_ge(c_pl_pool, b * 48 + n // T * 3 + t)
                    nc.tensor.matmul(out_rows, c_va[:, t, 4 * g + j, :], c_pl[:, n % RING, 0:S - 128 * t],
                                     start=False, stop=t == T - 1).then_inc(c_pv_done, 1)

                def denominators(g):
                    pe.wait_ge(c_u_done, b * GROUPS + g + 1)
                    if g >= 1:
                        pe.wait_ge(c_ln_done, b * GROUPS + g)
                    nc.tensor.matmul(P[:, DEN_BANK, :], masks[:, 2, :], c_u, start=True, stop=True)\
                      .then_inc(c_den_ready, 1)

                def project_out(g):
                    pe.wait_ge(c_at_done, 4 * (b * GROUPS + g + 1))
                    for r in range(16):
                        ins = nc.tensor.matmul(P[:, OUT_BANK, 128 * g:128 * g + 128],
                                               co_w[:, 128 * r:128 * r + 128], c_at[:, g % 2, :, r::16],
                                               start=r == 0, stop=r == 15)
                    ins.then_inc(c_out_done, 1)

                xb_dyn = xn[:, bass.ds(b, 1), :]

                def project(q):
                    w = (cq_w, ck_w)[q % 2][:, 128 * (q // 2):128 * (q // 2) + 128]
                    if q >= 4:
                        pe.wait_ge(c_parts_done, b * 8 + q - 3)
                    nc.tensor.matmul(P[:, 2 + q % 4, :], w, xb_dyn, start=True, stop=True).then_inc(c_proj_ready, 1)

                for q in range(4):
                    project(q)
                pe.wait_ge(c_xb_ready, b + 1)
                for t in range(T):
                    ins = nc.tensor.matmul(P[:, 7, 128 * t:128 * t + 128], c_xb[:, 128 * t:128 * t + 128], cv_w,
                                           start=True, stop=True)
                ins.then_inc(c_v_ready, 1)
                for n in range(LEAD):
                    if n % STEPS == 0:
                        pe.wait_ge(c_parts_done, b * 8 + 2 * (n // STEPS) + 2)
                    maxima(n)
                    if n in LATE_PROJECTIONS:
                        project(4 + LATE_PROJECTIONS.index(n))
                pe.wait_ge(c_parts_done, b * 8 + 8)
                pe.wait_ge(c_v_done, 2 * b + 2)
                rows(0)
                for g in range(GROUPS):
                    for i in range(STEPS):
                        n = g * STEPS + i
                        j, t = i // T, i % T
                        if i == 0:
                            pe.wait_ge(c_q_done, b * GROUPS + g + 1)
                        if n >= 3:
                            pe.wait_ge(c_exp_done, b * 64 + n - 2)
                        lo, w, bank = 32 * j, S - 128 * t, ST_BANKS[n % 3]
                        nc.tensor.matmul(P[:, bank, 0:w], c_k[lo:lo + 32, g, 128 * t:128 * t + 128],
                                         c_qm[lo:lo + 32, g % 2, 128 * t:S], start=True, stop=False)
                        nc.tensor.matmul(P[:, bank, 0:128], ident_b, mask_h[:, 1, :], start=False, stop=True)\
                          .then_inc(c_st_ready, 1)
                        if n >= LAG:
                            values(n - LAG)
                        if n + LEAD < CN:
                            if (n + LEAD) % STEPS == 0:
                                pe.wait_ge(c_parts_done, b * 8 + 2 * ((n + LEAD) // STEPS) + 2)
                            maxima(n + LEAD)
                        if i == ROWS_AT and g + 1 < GROUPS:
                            rows(g + 1)
                        if g >= 1 and i == 6:
                            denominators(g - 1)
                        if g >= 1 and i == 14:
                            project_out(g - 1)
                for n in range(CN - LAG, CN):
                    values(n)
                denominators(GROUPS - 1)
                project_out(GROUPS - 1)

        def causal_act(act, p):
            k, singles, boths, lns = norm_of[p]
            start(act, p, by_chunk=True)
            norm_act(act, k, True, False, lns)
            with act.Fori(0, NB) as b:
                def unnormalised(g):
                    act.wait_ge(c_pv_done, b * 64 + (g + 1) * STEPS)
                    if g >= 1:
                        act.wait_ge(c_at_done, 4 * (b * GROUPS + g))
                        act.wait_ge(c_den_ready, b * GROUPS + g)
                    nc.scalar.activation(c_u, P[:, O_BANK, :], ACT.Copy).then_inc(c_u_done, 1)

                def reciprocal(g):
                    act.wait_ge(c_den_ready, b * GROUPS + g + 1)
                    nc.scalar.activation(c_rec, P[:, DEN_BANK, :], ACT.Ln).then_inc(c_ln_done, 1)
                    act.wait_ge(c_ln_done, b * GROUPS + g + 1)
                    nc.scalar.activation(c_rec, c_rec, ACT.Exp, scale=-1.0).then_inc(c_rec_done, 1)

                for q in range(2 * GROUPS):
                    act.wait_ge(c_proj_ready, b * 8 + q + 1)
                    if q >= 2:
                        act.wait_ge(c_parts_done, b * 8 + q - 1)
                    if q % 2 == 0:
                        ins = nc.scalar.activation(c_h[:, 0, :], P[:, 2 + q % 4, :], ACT.Copy)
                    else:
                        ins = nc.scalar.activation(c_h[:, 1, :], P[:, 2 + q % 4, :], ACT.Identity, bias=col("one_row"))
                    ins.then_inc(c_high_done, 1)
                for g in range(GROUPS):
                    for i in range(STEPS):
                        n, w = g * STEPS + i, S - 128 * (i % T)
                        act.wait_ge(c_st_ready, b * 64 + n + 1)
                        if n >= RING:
                            act.wait_ge(c_pv_done, b * CN + n - RING + 1)
                        for dst, done in ((c_ph, c_ph_done), (c_pt, c_exp_done)):
                            nc.scalar.activation(dst[:, n % RING, 0:w], P[:, ST_BANKS[n % 3], 0:w], ACT.Exp,
                                                 scale=float(HD1) ** -0.5).then_inc(done, 1)
                        if g >= 1 and i == LAG - 1:
                            unnormalised(g - 1)
                        if g >= 1 and i == 7:
                            reciprocal(g - 1)
                unnormalised(GROUPS - 1)
                reciprocal(GROUPS - 1)

        def causal_pool(pool, own, p):
            pool.wait_ge(x_done, at[p])
            nc.gpsimd.memset(c_nm[:, :, :, :], 0.0)
            nc.gpsimd.memset(c_at[:, :, :, :], 0.0)
            own.link(nc.gpsimd.memset(c_va[:, :, :, :], 0.0))
            nc.gpsimd.memset(c_va[:, :, :, HD1:HD1 + 1], 1.0).then_inc(c_setup, 1)
            with pool.Fori(0, NB) as b:
                for n in range(GROUPS * STEPS):
                    t = n % T
                    if t == 0:
                        continue
                    w = S - 128 * t
                    pool.wait_ge(c_exp_done, b * 64 + n + 1)
                    if n >= RING:
                        pool.wait_ge(c_pv_done, b * CN + n - RING + 1)
                    nc.gpsimd.tensor_tensor(c_pl[:, n % RING, 0:w], c_pt[:, n % RING, 0:w], c_ph[:, n % RING, 0:w],
                                            ALU.subtract).then_inc(c_pl_pool, 1)

        def causal_dve(dve, own, p):
            k, singles, boths, lns = norm_of[p]
            start(dve, p)
            nc.vector.tensor_copy(ident_b, ident[:, :])
            nc.vector.tensor_copy(mask_h[:, :, :], masks[:, 0:2, :]).then_inc(c_setup, 1)
            for c in range(NB):
                dve.wait_ge(rstd_ready, NB * singles + c + 1)
                nc.vector.tensor_tensor(xn[:, c, :], P[:, c, :], rstd[:, c, :], ALU.mult).then_inc(xn_ready, 1)
            dve.wait_ge(xn_ready, NB * xns[p][0] + NB)
            dve.wait_ge(c_setup, 2)
            with dve.Fori(0, NB) as b:
                def maxima(n):
                    g, i = n // STEPS, n % STEPS
                    j, t = i // T, i % T
                    if g >= 2 and i == 0:
                        dve.wait_ge(c_rows_ready, b * GROUPS + g - 1)
                    dve.wait_ge(c_s_ready, b * 64 + n + 1)
                    nc.vector.tensor_reduce(out=c_nm[:, g % 2, t, 32 * j + 24:32 * j + 25],
                                            in_=P[:, n % 2, 0:128 * (t + 1)], op=ALU.max, axis=AX.X, negate=True)\
                      .then_inc(c_max_done, 1)

                def low_part(n):
                    dve.wait_ge(c_exp_done, b * 64 + n + 1)
                    if n >= RING:
                        dve.wait_ge(c_pv_done, b * CN + n - RING + 1)
                    nc.vector.tensor_tensor(c_pl[:, n % RING, :], c_pt[:, n % RING, :], c_ph[:, n % RING, :],
                                            ALU.subtract).then_inc(c_pl_dve, 1)

                def add_rows(g):
                    dve.wait_ge(c_rows_ready, b * GROUPS + g + 1)
                    nc.vector.tensor_tensor(c_qm[:, g % 2, :], c_q[:, g, :], P[:, ROW_BANK, :], ALU.add)\
                      .then_inc(c_q_done, 1)

                def normalise(g, j):
                    if j == 0:
                        dve.wait_ge(c_rec_done, b * GROUPS + g + 1)
                        if g >= 2:
                            dve.wait_ge(c_out_done, b * GROUPS + g - 1)
                    lo = 32 * j
                    nc.vector.tensor_tensor(c_at[lo:lo + 32, g % 2, j, :], c_u[lo:lo + 32], c_rec[lo:lo + 32],
                                            ALU.mult).then_inc(c_at_done, 1)

                def parts(q):
                    dve.wait_ge(c_high_done, b * 8 + q + 1)
                    nc.vector.scalar_tensor_tensor(out=(c_q, c_k)[q % 2][:, q // 2, :], in0=c_h[:, q % 2, :],
                                                   scalar=(LOW_Q, LOW_K)[q % 2], in1=P[:, 2 + q % 4, :],
                                                   op0=ALU.mult, op1=ALU.add).then_inc(c_parts_done, 1)

                nc.vector.tensor_copy(c_xb, chunk(xn, b)).then_inc(c_xb_ready, 1)
                for q in range(4):
                    parts(q)
                dve.wait_ge(c_v_ready, b + 1)
                v_psum = P[:, 7, :].rearrange("p (t h n) -> p t h n", t=T, h=H1)
                nc.vector.tensor_copy(c_va[:, :, :, 0:HD1], v_psum).then_inc(c_v_done, 1)
                dve.wait_ge(c_v_done, 2 * b + 1)
                nc.vector.tensor_tensor(c_va[:, :, :, 16:16 + HD1], v_psum, c_va[:, :, :, 0:HD1], ALU.subtract)\
                  .then_inc(c_v_done, 1)
                for n in range(LEAD):
                    maxima(n)
                    if n - 2 in LATE_PROJECTIONS:
                        parts(4 + LATE_PROJECTIONS.index(n - 2))
                add_rows(0)
                for g in range(GROUPS):
                    for i in range(STEPS):
                        if g * STEPS + i + LEAD < CN:
                            maxima(g * STEPS + i + LEAD)
                        if i == ROWS_AT and g + 1 < GROUPS:
                            add_rows(g + 1)
                        if i % T == 1:
                            low_part(g * STEPS + i - 1)
                        if g >= 1 and 9 <= i < 13:
                            normalise(g - 1, i - 9)
                for j in range(4):
                    normalise(GROUPS - 1, j)
                dve.wait_ge(c_out_done, b * GROUPS + GROUPS)
                xb = chunk(x, b)
                nc.vector.scalar_tensor_tensor(out=xb, in0=P[:, OUT_BANK, :], scalar=col("co"), in1=xb,
                                               op0=ALU.add, op1=ALU.add).then_inc(x_done, 1)

        block = ctx.enter_context(nc.Block())

        @block.sync
        def _(sp):
            for dst, src in ((x[:, :, :], x_t), (cols[:, :], cols_d), (ident[:, :], ident_d),
                             (masks[:, :, :], mask_d)):
                sp.dma_start(dst, src).then_inc(x_loaded, 16)
            sp.dma_start(wm[:, :], wm_d).then_inc(w_loaded[0], 16)
            if swiglu:
                for dst, src in ((raw[:, 0:E * DE], f0_up_d.rearrange("p e n -> p (e n)")),
                                 (raw[:, E * DE:2 * E * DE], f0_gate_d.rearrange("p e n -> p (e n)")),
                                 (raw[:, 2 * E * DE:F0_COLS], f0_down_d.rearrange("p e j d -> p (e j d)")),
                                 (f0_router[:, :], f0_router_d)):
                    sp.dma_start(dst, src).then_inc(w_loaded[1], 16)
            sp.dma_start(small_w[:, 0:384], phase_w_d).then_inc(w_loaded[4], 16)
            sp.dma_start(small_w[:, 384:CAUSAL_END], causal_w_d).then_inc(w_loaded[6], 16)
            if 2 in phases:
                if swiglu:
                    sp.wait_ge(raw_split, 1)
                for dst, src in ((qkv_f32, qkv_d), (wo_w, wo_d.rearrange("p a d -> p (a d)"))):
                    sp.dma_start(dst, src).then_inc(w_loaded[2], 16)
            if relu:
                if swiglu:
                    sp.wait_ge(raw_split, 1)
                if 2 in phases:
                    sp.wait_ge(x_done, at[2] + NB)
                for dst, src in ((raw[:, 0:E * FE], f1_up_d.rearrange("p e n -> p (e n)")),
                                 (raw[:, E * FE:F1_COLS], f1_down_d.rearrange("p e j d -> p (e j d)")),
                                 (f1_router[:, :], f1_router_d), (f1_b2[0:E, :], f1_b2_d), (f1_b2[E:2 * E, :], f1_b2_d),
                                 (f1_rb[:, :], f1_rb_d[0, :].partition_broadcast(128))):
                    sp.dma_start(dst, src).then_inc(w_loaded[5], 16)
            sp.wait_ge(x_done, NB * len(phases) + 1)
            sp.dma_start(out, x[:, :, :]).then_inc(stored, 16)
            sp.wait_ge(stored, 16)

        @block.tensor
        def _(pe):
            for p in phases:
                if p == 0:
                    pe.wait_ge(w_loaded[0], 16)
                    scan_pe(pe)
                if p in (1, 3):
                    pe.wait_ge(w_loaded[1], 64)
                    swiglu_pe(pe, p)
                if p == 2:
                    pe.wait_ge(w_loaded[2], 32)
                    heads_pe(pe, p)
                if p == 4:
                    pe.wait_ge(w_loaded[4], 16)
                    phase_pe(pe, p)
                if p == 6:
                    pe.wait_ge(w_loaded[6], 16)
                    causal_pe(pe, p)
                if p in (5, 7):
                    pe.wait_ge(w_loaded[5], 96)
                    relu_pe(pe, p)

        @block.scalar
        def _(act):
            nc.scalar.preload_act_table_set(EXP_LN)
            for p in phases:
                if p:
                    nc.scalar.preload_act_table_set(EXP_LN)
                if p == 0:
                    scan_act(act)
                if p in (1, 3):
                    swiglu_act(act, p)
                if p == 2:
                    heads_act(act, p)
                if p == 4:
                    phase_act(act, p)
                if p == 6:
                    causal_act(act, p)
                if p in (5, 7):
                    relu_act(act, p)

        @block.gpsimd
        def _(pool):
            own = Own(pool, pool_own)
            nc.gpsimd.memset(ones[:, :], 1.0)
            nc.gpsimd.memset(m_bc[:, :, :], 0.0)
            for e in range(E):
                ins = nc.gpsimd.memset(rev[:, :, e:e + 1], float(E - e))
            ins.then_inc(x_done, 1)
            if swiglu:
                pool.wait_ge(w_loaded[1], 64)
                high_pool(own, raw[:, :], w_h[:, :])
            if 0 in phases:
                scan_pool(pool)
            if swiglu:
                nc.gpsimd.tensor_tensor(w_l[:, :], raw[:, :], w_h[:, :], ALU.subtract).then_inc(raw_split, 1)
            for p in phases:
                if p in (1, 3):
                    swiglu_pool(pool, p)
                if p == 1 and 2 in phases:
                    pool.wait_ge(w_loaded[2], 32)
                    split_pool(own, qkv_f32, qkv_parts[0], qkv_parts[1]).then_inc(a_split, 1)
                if p == 2:
                    if 1 not in phases:
                        pool.wait_ge(w_loaded[2], 32)
                        split_pool(own, qkv_f32, qkv_parts[0], qkv_parts[1]).then_inc(a_split, 1)
                    heads_pool(pool, own, p)
                if p == 6:
                    causal_pool(pool, own, p)
                if p == (4 if 4 in phases and relu else relu[0] if relu else None):
                    pool.wait_ge(x_done, at[p])
                    pool.wait_ge(w_loaded[5], 96)
                    split_pool(own, raw[:, 0:F1_COLS], w_h[:, 0:F1_COLS], w_l[:, 0:F1_COLS]).then_inc(raw_split, 1)

        @block.vector
        def _(dve):
            nc.vector.memset(mean_w[:, :], 1.0 / D)
            for k, v in ((K_LN, LN_EPS), (K_BOTH, BOTH_EPS), (K_ONE, 1.0), (K_TANH, -CENTER / HALF),
                         (K_HALFPI, math.pi / 2)):
                last = nc.vector.memset(kc[:, k:k + 1], v)
            last.then_inc(consts_set, 1)
            dve.wait_ge(x_loaded, 64)
            dve.wait_ge(consts_set, 1)
            nc.vector.tensor_tensor(center_w[:, :], ident[:, :], mean_w[:, :], ALU.subtract)
            nc.vector.tensor_tensor(pick_row[:, :], ident[:, 0:2 * NS], ident[:, 2 * NS:4 * NS], ALU.add)
            nc.vector.tensor_tensor(pick_both[:, :], ident[0:2 * E, 0:E], ident[0:2 * E, E:2 * E], ALU.add)
            nc.vector.tensor_copy(ident_h[:, :], ident[:, :]).then_inc(consts_set, 1)
            own = Own(dve, dve_own)
            for p in phases:
                if p == 0:
                    scan_dve(dve, own)
                if p in (1, 3):
                    swiglu_dve(dve, own, p)
                if p == 2:
                    heads_dve(dve, own, p)
                if p == 4:
                    phase_dve(dve, own, p)
                if p == 6:
                    causal_dve(dve, own, p)
                if p in (5, 7):
                    if p == relu[0]:
                        dve.wait_ge(w_loaded[5], 96)
                        own.link(nc.vector.tensor_scalar(b2_s[:, :], f1_b2[:, :], W_SCALE, None, ALU.mult))
                        own.link(nc.vector.tensor_copy(b2_parts[:, 0, :], b2_s[:, :]))
                        own.link(nc.vector.tensor_tensor(b2_parts[:, 1, :], b2_s[:, :], b2_parts[:, 0, :], ALU.subtract))
                    relu_dve(dve, own, p)


def layout(x, v):
    f32 = np.float32

    def pair_cols(a):
        return np.repeat(a.reshape(PAIRS, 2), HD0, axis=1).T

    def rows_at(lo, hi):
        return ((np.arange(128) % 32 >= lo) & (np.arange(128) % 32 < hi)).astype(f32)

    parts = {
        "A_log": v["L0_attn_a_A_log"], "b_delta": v["L0_attn_a_b_delta"],
        "D_skip": v["L0_attn_a_D_skip"], "norm_w": v["L0_attn_a_norm_weight"],
        "rms_w": v["L0_ffn_rms_w"], "adaptive": pair_cols(v["L0_attn_b_adaptive_scale"]),
        "bq": v["L0_attn_b_bq"].reshape(PAIRS, 128).T, "bk": v["L0_attn_b_bk"].reshape(PAIRS, 128).T,
        "bv": v["L0_attn_b_bv"].reshape(PAIRS, 128).T,
        "bo": v["L0_attn_b_bo"], "gamma": v["L0_attn_b_gamma"], "beta": v["L0_attn_b_beta"],
        "pq": v["L1_attn_a_bq"], "pk": v["L1_attn_a_bk"], "pv": v["L1_attn_a_bv"],
        "phase": v["L1_attn_a_phase_bias"], "inv_wl": inverse_wavelengths(),
        "co": v["L1_attn_b_bo"], "one_row": rows_at(24, 25),
        "low_q": -rows_at(8, 16), "low_k": rows_at(24, 25) - rows_at(16, 24),
        "b1": v["L1_ffn_b1"].reshape(E * FC, 128).T,
    }
    cols = np.concatenate([parts[n].reshape(128, -1) for n in COLS], axis=1)

    masks = np.zeros((128, 3, 128), f32)
    later = np.triu(np.ones((128, 128), bool), 1)
    masks[:, 0][later] = -1e30
    masks[:, 1][later.T] = -1e30
    rows = np.arange(128)
    masks[:, 2] = rows[:, None] == 32 * (rows[None, :] // 32) + HD1

    down0 = np.zeros((E, DEC * 128, D), f32)
    down0[:, :DE] = v["L0_ffn_W3"].transpose(0, 2, 1)

    def spread(w):
        out = np.zeros((128, GROUPS, 4, 32), f32)
        for n in range(3):
            out[..., n * HD1:n * HD1 + HD1] = w.reshape(128, GROUPS, 4, HD1)
        return out.reshape(128, GROUPS * 128)

    co = np.zeros((4, 32, 16, D), f32)
    for lo in (0, 16):
        co[:, lo:lo + HD1] = v["L1_attn_b_Wo"].reshape(16, HD1, D).transpose(1, 0, 2)
    return {
        "x_t": x.reshape(NB * S, D).T.reshape(D, NB, S),
        "cols": cols, "ident": np.eye(128, dtype=f32), "masks": masks,
        "wm": np.concatenate([v["L0_attn_a_W_delta"], v["L0_attn_a_W_B"], v["L0_attn_a_W_C"]], axis=1),
        "f0_up": v["L0_ffn_W1"].transpose(2, 0, 1), "f0_gate": v["L0_ffn_W2"].transpose(2, 0, 1),
        "f0_down": down0.reshape(E, DEC, 128, D).transpose(2, 0, 1, 3),
        "f0_router": v["L0_ffn_gate_w"].T,
        "qkv": np.concatenate([v["L0_attn_b_Wq"].T, v["L0_attn_b_Wk"].T, v["L0_attn_b_Wv"].T], axis=1),
        "wo": v["L0_attn_b_Wo"].T.reshape(PAIRS, 128, D).transpose(1, 0, 2),
        "phase_w": np.concatenate([v["L1_attn_a_Wq"].T, v["L1_attn_a_Wk"].T, v["L1_attn_a_Wv"].T], axis=1),
        "causal_w": np.concatenate([spread(v["L1_attn_b_Wq"]), spread(v["L1_attn_b_Wk"]),
                                    v["L1_attn_b_Wv"],
                                    co.reshape(128, 16 * D)], axis=1),
        "f1_up": v["L1_ffn_w1"].transpose(1, 0, 2),
        "f1_down": v["L1_ffn_w2"].reshape(E, FC, 128, D).transpose(2, 0, 1, 3),
        "f1_router": v["L1_ffn_gate_w"], "f1_rb": v["L1_ffn_gate_b"].reshape(1, E),
        "f1_b2": v["L1_ffn_b2"],
    }


def inverse_wavelengths():
    lengths = np.arange(1, D + 1, dtype=np.float32) * np.float32(2.0 * math.pi / D)
    return np.float32(1.0) / (lengths + np.float32(1e-8))


def kernel(**inputs):
    import concourse.bacc as bacc
    from concourse.bass_utils import run_bass_kernel_spmd

    v = {name: np.asarray(a) for name, a in inputs.items()}
    arrays = {f"in_{n}": np.ascontiguousarray(a) for n, a in layout(v["L0_attn_a_x"], v).items()}
    nc = bacc.Bacc("TRN2", target_bir_lowering=False, num_devices=1)
    args = [nc.dram_tensor(n, a.shape, mybir.dt.from_np(a.dtype), kind="ExternalInput").ap()
            for n, a in arrays.items()]
    out = nc.dram_tensor("x_out", (D, NB, S), F32, kind="ExternalOutput").ap()
    hybrid(nc, *args, out)
    r = run_bass_kernel_spmd(nc, [arrays], core_ids=[0])
    got = r.results[0]["x_out"]
    return np.ascontiguousarray(got.reshape(D, NB * S).T.reshape(NB, S, D))
```
